# Optimizing a Trainium2 kernel written in Bass

```python
import numpy as np
import jax
import jax.numpy as jnp

def _softmax(x, axis=-1):
    return jax.nn.softmax(x, axis=axis)

def _gelu(x):
    return jax.nn.gelu(x, approximate=True)

def _silu(x):
    return jax.nn.silu(x)

def _sigmoid(x):
    return jax.nn.sigmoid(x)

def _layernorm(x, axis=-1, eps=1e-05):
    m = jnp.mean(x, axis=axis, keepdims=True)
    v = jnp.var(x, axis=axis, keepdims=True)
    return (x - m) / jnp.sqrt(v + eps)

def _scatter_add(tgt, idx, src, axis=0):
    return tgt.at[idx].add(src)

def _segment_sum(src, seg, n):
    return jax.ops.segment_sum(src, seg, n)
kernel_name = 'mk_xattn_ffn_d1_seqx_r4_fd1087'

def setup_inputs(seed: int=0):
    np.random.seed(seed)
    _w = jnp.asarray

    def _rec_inputs():
        import jax
        import jax.numpy as jnp
        _rk = jax.random.key(seed)
        x = -0.0005207 + 1.001 * jax.random.normal(jax.random.fold_in(_rk, 1), (8, 512, 256), jnp.float32)
        _lenS = 512 - jax.random.randint(jax.random.fold_in(_rk, 7), (8,), 0, max(1, 512 // 4) + 1, jnp.int32)
        _lenS2 = 1024 - jax.random.randint(jax.random.fold_in(_rk, 8), (8,), 0, max(1, 1024 // 4) + 1, jnp.int32)
        _ctx_1024P = jax.random.normal(jax.random.fold_in(_rk, 11), (8, 16, 256), jnp.float32)
        _ctx_1024c = jax.random.dirichlet(jax.random.fold_in(_rk, 511), 0.3 * jnp.ones((16,), jnp.float32), (8, 1024))
        _ctx_1024t = jnp.einsum('bsk,bkd->bsd', _ctx_1024c, _ctx_1024P)
        _ctx_1024t = _ctx_1024t * jax.lax.rsqrt(jnp.mean(jnp.square(_ctx_1024t)) + 1e-12) * 0.953939
        ctx_1024 = -1.52775e-05 + 0.999936 * (_ctx_1024t + 0.3 * jax.random.normal(jax.random.fold_in(_rk, 611), (8, 1024, 256), jnp.float32))
        return (x, ctx_1024)
    x, ctx_1024 = _rec_inputs()

    def _L0_xattn_setup():
        import jax, jax.numpy as jnp
        import numpy as np
        DIM = 256
        HEADS = 16
        DHEAD = 64
        INNER = HEADS * DHEAD
        EPS = 1e-05

        def layer_norm(x, g, b):
            mu = jnp.mean(x, axis=-1, keepdims=True)
            var = jnp.mean(jnp.square(x - mu), axis=-1, keepdims=True)
            return (x - mu) * jax.lax.rsqrt(var + EPS) * g + b

        def apply_rope(x, cos, sin):
            d2 = x.shape[-1] // 2
            x1, x2 = (x[..., :d2], x[..., d2:])
            return jnp.concatenate([x1 * cos - x2 * sin, x2 * cos + x1 * sin], axis=-1)
        key = jax.random.key(seed)
        ks = jax.random.split(key, 10)
        B, N, S = (8, 64, 1024)
        latents = jax.random.normal(ks[0], (B, N, DIM), dtype=jnp.float32)
        context = jax.random.normal(ks[1], (B, S, DIM), dtype=jnp.float32)
        cos = jax.random.uniform(ks[2], (S, DHEAD // 2), dtype=jnp.float32)
        sin = jax.random.uniform(ks[3], (S, DHEAD // 2), dtype=jnp.float32)
        init = lambda k, shp, fan_in: jax.random.normal(k, shp, dtype=jnp.float32) / np.sqrt(fan_in)
        return {'latents': latents, 'context': context, 'cos': cos, 'sin': sin, 'ln_lat_g': jnp.ones((DIM,), jnp.float32), 'ln_lat_b': jnp.zeros((DIM,), jnp.float32), 'ln_ctx_g': jnp.ones((DIM,), jnp.float32), 'ln_ctx_b': jnp.zeros((DIM,), jnp.float32), 'Wq': init(ks[4], (DIM, INNER), DIM), 'Wkv': init(ks[5], (DIM, 2 * INNER), DIM), 'Wo': init(ks[6], (INNER, DIM), INNER), 'bo': jnp.zeros((DIM,), jnp.float32)}
    _L0_xattn_all = _L0_xattn_setup()
    _L0_xattn_in = {k: v for k, v in _L0_xattn_all.items() if k in ('cos', 'sin', 'ln_lat_g', 'ln_lat_b', 'ln_ctx_g', 'ln_ctx_b', 'Wq', 'Wkv', 'Wo', 'bo')}
    del _L0_xattn_all

    def _L0_ffn_setup():
        import jax, jax.numpy as jnp
        import numpy as np
        H, F, E_SHARED, E_ROUTED, K = (256, 1024, 1, 8, 2)

        def _expert(x, w_up, w_down):
            h = jax.nn.gelu(jnp.einsum('bsh,hf->bsf', x, w_up), approximate=False)
            return jnp.einsum('bsf,fh->bsh', h, w_down)
        key = jax.random.key(seed)
        ks = jax.random.split(key, 6)
        x = jax.random.normal(ks[0], (4, 512, H), dtype=jnp.float32)
        s = 0.02
        shared_up = jax.random.normal(ks[1], (E_SHARED, H, F), dtype=jnp.float32) * s
        shared_down = jax.random.normal(ks[2], (E_SHARED, F, H), dtype=jnp.float32) * s
        routed_up = jax.random.normal(ks[3], (E_ROUTED, H, F), dtype=jnp.float32) * s
        routed_down = jax.random.normal(ks[4], (E_ROUTED, F, H), dtype=jnp.float32) * s
        router_w = jax.random.normal(ks[5], (H, E_ROUTED), dtype=jnp.float32) * s
        return {'x': x, 'shared_up': shared_up, 'shared_down': shared_down, 'routed_up': routed_up, 'routed_down': routed_down, 'router_w': router_w}
    _L0_ffn_all = _L0_ffn_setup()
    _L0_ffn_in = {k: v for k, v in _L0_ffn_all.items() if k in ('shared_up', 'shared_down', 'routed_up', 'routed_down', 'router_w')}
    del _L0_ffn_all
    return {'x': x, 'ctx_1024': ctx_1024, 'L0_xattn_cos': _L0_xattn_in['cos'], 'L0_xattn_sin': _L0_xattn_in['sin'], 'L0_xattn_ln_lat_g': _L0_xattn_in['ln_lat_g'], 'L0_xattn_ln_lat_b': _L0_xattn_in['ln_lat_b'], 'L0_xattn_ln_ctx_g': _L0_xattn_in['ln_ctx_g'], 'L0_xattn_ln_ctx_b': _L0_xattn_in['ln_ctx_b'], 'L0_xattn_Wq': _L0_xattn_in['Wq'], 'L0_xattn_Wkv': _L0_xattn_in['Wkv'], 'L0_xattn_Wo': _L0_xattn_in['Wo'], 'L0_xattn_bo': _L0_xattn_in['bo'], 'L0_ffn_shared_up': _L0_ffn_in['shared_up'], 'L0_ffn_shared_down': _L0_ffn_in['shared_down'], 'L0_ffn_routed_up': _L0_ffn_in['routed_up'], 'L0_ffn_routed_down': _L0_ffn_in['routed_down'], 'L0_ffn_router_w': _L0_ffn_in['router_w']}

def reference(x, ctx_1024, L0_xattn_cos, L0_xattn_sin, L0_xattn_ln_lat_g, L0_xattn_ln_lat_b, L0_xattn_ln_ctx_g, L0_xattn_ln_ctx_b, L0_xattn_Wq, L0_xattn_Wkv, L0_xattn_Wo, L0_xattn_bo, L0_ffn_shared_up, L0_ffn_shared_down, L0_ffn_routed_up, L0_ffn_routed_down, L0_ffn_router_w):
    import jax
    import jax.numpy as jnp

    def _L0_xattn_ref(latents, context, cos, sin, ln_lat_g, ln_lat_b, ln_ctx_g, ln_ctx_b, Wq, Wkv, Wo, bo):
        import jax, jax.numpy as jnp
        import numpy as np
        DIM = 256
        HEADS = 16
        DHEAD = 64
        INNER = HEADS * DHEAD
        EPS = 1e-05

        def layer_norm(x, g, b):
            mu = jnp.mean(x, axis=-1, keepdims=True)
            var = jnp.mean(jnp.square(x - mu), axis=-1, keepdims=True)
            return (x - mu) * jax.lax.rsqrt(var + EPS) * g + b

        def apply_rope(x, cos, sin):
            d2 = x.shape[-1] // 2
            x1, x2 = (x[..., :d2], x[..., d2:])
            return jnp.concatenate([x1 * cos - x2 * sin, x2 * cos + x1 * sin], axis=-1)
        b, n, _ = latents.shape
        s = context.shape[1]
        lat = layer_norm(latents, ln_lat_g, ln_lat_b)
        ctx = layer_norm(context, ln_ctx_g, ln_ctx_b)
        q = (lat @ Wq).reshape(b, n, HEADS, DHEAD).transpose(0, 2, 1, 3)
        kv = ctx @ Wkv
        k, v = jnp.split(kv, 2, axis=-1)
        k = k.reshape(b, s, HEADS, DHEAD).transpose(0, 2, 1, 3)
        v = v.reshape(b, s, HEADS, DHEAD).transpose(0, 2, 1, 3)
        k = apply_rope(k, cos[None, None], sin[None, None])
        scale = DHEAD ** (-0.5)
        attn = jnp.einsum('bhnd,bhsd->bhns', q, k) * scale
        attn = jnp.clip(attn, -11.0, 11.0)
        attn = jax.nn.softmax(attn, axis=-1)
        out = jnp.einsum('bhns,bhsd->bhnd', attn, v)
        out = out.transpose(0, 2, 1, 3).reshape(b, n, INNER)
        return out @ Wo + bo

    def _L0_ffn_ref(x, shared_up, shared_down, routed_up, routed_down, router_w):
        import jax, jax.numpy as jnp
        import numpy as np
        H, F, E_SHARED, E_ROUTED, K = (256, 1024, 1, 8, 2)

        def _expert(x, w_up, w_down):
            h = jax.nn.gelu(jnp.einsum('bsh,hf->bsf', x, w_up), approximate=False)
            return jnp.einsum('bsf,fh->bsh', h, w_down)
        shared_out = jnp.zeros_like(x)
        for i in range(E_SHARED):
            shared_out = shared_out + _expert(x, shared_up[i], shared_down[i])
        probs = jax.nn.softmax(jnp.einsum('bsh,he->bse', x, router_w), axis=-1)
        top_k_prob, top_k_idx = jax.lax.top_k(probs, K)
        onehot = jax.nn.one_hot(top_k_idx, E_ROUTED, dtype=x.dtype)
        gates = jnp.einsum('bsk,bske->bse', top_k_prob, onehot)
        routed_out = jnp.zeros_like(x)
        for e in range(E_ROUTED):
            y = _expert(x, routed_up[e], routed_down[e])
            routed_out = routed_out + gates[..., e:e + 1] * y
        return shared_out + routed_out + x
    x = x + _L0_xattn_ref(_layernorm(x, axis=-1), ctx_1024, L0_xattn_cos, L0_xattn_sin, L0_xattn_ln_lat_g, L0_xattn_ln_lat_b, L0_xattn_ln_ctx_g, L0_xattn_ln_ctx_b, L0_xattn_Wq, L0_xattn_Wkv, L0_xattn_Wo, L0_xattn_bo)
    x = x + _L0_ffn_ref(_layernorm(x, axis=-1), L0_ffn_shared_up, L0_ffn_shared_down, L0_ffn_routed_up, L0_ffn_routed_down, L0_ffn_router_w)
    return x

_drawn_inputs = setup_inputs


def setup_inputs(seed=0):
    import zlib

    import numpy as np

    out = dict(_drawn_inputs(seed))
    spreads = {'L0_xattn_ln_lat_g': (1.0, 0.6),
     'L0_xattn_ln_lat_b': (0.0, 0.648),
     'L0_xattn_ln_ctx_g': (1.0, 0.2),
     'L0_xattn_ln_ctx_b': (0.0, 0.1),
     'L0_xattn_bo': (0.0, 0.1)}
    factors = {'L0_xattn_cos': 5.753,
     'L0_xattn_sin': 5.725,
     'L0_ffn_routed_up': 4.575,
     'L0_ffn_routed_down': 4.44,
     'L0_ffn_router_w': 4.952}
    for name, (base, spread) in spreads.items():
        noise = np.random.default_rng([zlib.crc32(name.encode()), seed]).standard_normal(out[name].shape)
        drawn = base * np.exp(spread * noise) if base else spread * noise
        out[name] = jnp.asarray(drawn.astype(out[name].dtype))
    for name, factor in factors.items():
        out[name] = (out[name] * factor).astype(out[name].dtype)
    return out
```

```python
from contextlib import ExitStack

import concourse.bass as bass
from concourse import mybir

F32 = mybir.dt.float32
F32R = mybir.dt.float32r
I32 = mybir.dt.int32
U32 = mybir.dt.uint32
ALU = mybir.AluOpType
ACT = mybir.ActivationFunctionType
AX = mybir.AxisListType

P = 128
ZERO = 1472
EPS = 1e-5
CLIP = 11.0
EXP_HI = 59874.141715197816
EXP_LO = 1.670170079024566e-05


class Shapes:

    def __init__(self, x, ctx, cos, Wq, routed_up):
        self.B, self.N, self.D = x.shape
        self.S = ctx.shape[1]
        self.HD = 2 * cos.shape[1]
        self.INNER = Wq.shape[1]
        self.PAIRS = self.INNER // P
        self.KD = self.D // P
        self.QT = self.N // P
        self.KT = self.S // P
        self.E = routed_up.shape[0]
        self.F = routed_up.shape[2]
        self.TILES = (2 * self.B * self.N + self.E * (self.N - 1)) // self.N
        assert 2 * self.HD == P and self.KD == 2 and self.N == 512 and self.KT == 8 and self.PAIRS == 8


def prepare(nc, sh, x, ctx_in, cos, sin, lat_g, lat_b, ctx_g, ctx_b, Wq, Wkv, Wo, wpack, ctxT, latT, keep):
    KD, KT, QT, PAIRS, D, B = sh.KD, sh.KT, sh.QT, sh.PAIRS, sh.D, sh.B
    with ExitStack() as es:
        def sb(name, shape, dt=F32):
            return es.enter_context(nc.sbuf_tensor(name, shape, dt))

        def ps(name, shape, dt=F32):
            return es.enter_context(nc.psum_tensor(name, shape, dt))

        def sem(name):
            return es.enter_context(nc.semaphore(name))

        ident, cosT, sinT, wo_hi, wo_lo = keep["ident"], keep["cosT"], keep["sinT"], keep["wo_hi"], keep["wo_lo"]
        sel, ones = keep["sel"], keep["ones"]

        w_raw = sb("w_raw", [P, KD, 3 * sh.INNER])
        w_split = sb("w_split", [P, PAIRS, 3, 2, KD, P], F32R)
        wo_raw = sb("wo_raw", [P, PAIRS, D])
        trig = sb("trig", [P, 2, KT, sh.HD // 2])
        trig4 = sb("trig4", [P, 2, KT, 4, sh.HD // 2])
        gb = sb("gb", [P, 4, KD])
        neg_half = sb("neg_half", [P, KT])
        T = [dict(
            ctx=sb(f"ctx{i}", [P, KT, D]), x=sb(f"x{i}", [P, QT, D]), xn=sb(f"xn{i}", [P, QT, D]),
            stats=sb(f"stats{i}", [P, KT, 6]), mv=sb(f"mv{i}", [P, KT, 2]), r=sb(f"r{i}", [P, KT]),
            xstats=sb(f"xstats{i}", [P, QT, 6]), xmv=sb(f"xmv{i}", [P, QT, 2]), xr=sb(f"xr{i}", [P, QT]),
            ve=sb(f"ve{i}", [P, KT]), xve=sb(f"xve{i}", [P, QT]),
            full=sb(f"full{i}", [P, KD, sh.S]), xfull=sb(f"xfull{i}", [P, KD, sh.N]),
        ) for i in range(2)]
        ctx_split = sb("ctx_split", [P, 2, KD, sh.S], F32R)
        lat_split = sb("lat_split", [P, 2, KD, sh.N], F32R)
        tp = [ps(f"tp{i}", [P, 4, P]) for i in range(8)]

        s_w = sem("s_w")
        s_const = sem("s_const")
        s_cc = sem("s_cc")
        s_trig4 = sem("s_trig4")
        s_hi = sem("s_hi")
        s_lo = sem("s_lo")
        s_wout = sem("s_wout")
        s_tabT = sem("s_tabT")
        s_tab = sem("s_tab")
        s_cin, s_xin = [sem(f"s_cin{i}") for i in range(2)], [sem(f"s_xin{i}") for i in range(2)]
        s_cstat, s_cvar, s_crstd, s_cnorm = sem("s_cstat"), sem("s_cvar"), sem("s_crstd"), sem("s_cnorm")
        s_xstat, s_xvar, s_xrstd, s_xnorm = sem("s_xstat"), sem("s_xvar"), sem("s_xrstd"), sem("s_xnorm")
        s_ctr, s_xtr = sem("s_ctr"), sem("s_xtr")
        s_cfull, s_xfull = sem("s_cfull"), sem("s_xfull")
        s_chi, s_clo, s_xhi, s_xlo = sem("s_chi"), sem("s_clo"), sem("s_xhi"), sem("s_xlo")
        s_cout, s_xout = sem("s_cout"), sem("s_xout")

        NW = 4 + 4 + 2
        block = es.enter_context(nc.Block())

        def rows(ap, b):
            return ap[b].rearrange("(p t) d -> p t d", p=P)

        @block.sync
        def _(sp):
            for n, ap in enumerate((ctx_in, x)):
                for i in range(2):
                    sp.dma_start((T[i]["ctx"] if n == 0 else T[i]["x"])[:], rows(ap, i)).then_inc((s_cin, s_xin)[n][i], 16)
            w3 = w_raw[:].rearrange("p k (t n) -> p k t n", t=3)
            sp.dma_start(w3[:, :, 0], Wkv[:, 0:sh.INNER].rearrange("(k p) n -> p k n", p=P)).then_inc(s_w, 16)
            sp.dma_start(w3[:, :, 1], Wkv[:, sh.INNER:2 * sh.INNER].rearrange("(k p) n -> p k n", p=P)).then_inc(s_w, 16)
            sp.dma_start(w3[:, :, 2], Wq.rearrange("(k p) n -> p k n", p=P)).then_inc(s_w, 16)
            sp.dma_start(wo_raw[:], Wo.rearrange("(c p) n -> p c n", p=P)).then_inc(s_w, 16)
            with nc.allow_non_contiguous_dma(reason="four vectors of 256 values"):
                for n, ap in enumerate((ctx_g, ctx_b, lat_g, lat_b)):
                    sp.dma_start(gb[:, n], ap.rearrange("(k p) -> p k", p=P)).then_inc(s_w, 16)
            for n, ap in enumerate((cos, sin)):
                sp.dma_start(trig[:, n], ap.rearrange("(p t) d -> p t d", p=P)).then_inc(s_w, 16)
            sp.wait_ge(s_lo, 2)
            for first, of, n in ((0, 0, PAIRS), (PAIRS, 0, 2)):
                sp.dma_start(wpack[first:first + n].rearrange("c p n -> p c n"),
                             w_split[:, of:of + n].rearrange("p c a b k n -> p c (a b k n)").bitcast(F32)).then_inc(s_wout, 16)
            with sp.Fori(0, B // 2) as h:
                for i in range(2):
                    b = h * 2 + i
                    sp.wait_ge(s_clo, b + 1)
                    sp.dma_start(ctxT[b], ctx_split[:].rearrange("p a k n -> p (a k n)").bitcast(F32)).then_inc(s_cout, 16)
                    sp.wait_ge(s_xlo, b + 1)
                    sp.dma_start(latT[b], lat_split[:].rearrange("p a k n -> p (a k n)").bitcast(F32)).then_inc(s_xout, 16)
                    nxt = (b + 2) % B
                    sp.wait_ge(s_ctr, 4 * b + 4)
                    sp.dma_start(T[i]["ctx"][:], rows(ctx_in, nxt)).then_inc(s_cin[i], 16)
                    sp.wait_ge(s_xtr, 2 * b + 2)
                    sp.dma_start(T[i]["x"][:], rows(x, nxt)).then_inc(s_xin[i], 16)
            sp.dma_start(ctxT[B], ctx_split[:].rearrange("p a k n -> p (a k n)").bitcast(F32)).then_inc(s_cout, 16)
            sp.dma_start(latT[B], lat_split[:].rearrange("p a k n -> p (a k n)").bitcast(F32)).then_inc(s_xout, 16)
            for s, n in ((s_wout, 2), (s_cout, B + 1), (s_xout, B + 1),
                         (s_cin[0], B // 2 + 1), (s_cin[1], B // 2 + 1), (s_xin[0], B // 2 + 1), (s_xin[1], B // 2 + 1)):
                sp.wait_ge(s, 16 * n)

        @block.gpsimd
        def _(pool):
            pool.memset(ident[:], 0.0).then_inc(s_cc, 1)
            pool.memset(neg_half[:], -0.5)
            pool.memset(ones[:], 1.0)
            pool.memset(sel[:], 0.0).then_inc(s_cc, 1)
            pool.wait_ge(s_cc, 2)
            pool.affine_select(out=ident[:], in_=ident[:], compare_op=ALU.not_equal, fill=1.0, base=0,
                               pattern=[[-1, P]], channel_multiplier=1).then_inc(s_cc, 1)
            for r in range(4):
                pool.wait_ge(s_cc, 3 + r)
                part = sel[:, (r // 2) * 64:(r // 2) * 64 + 64]
                pool.affine_select(out=part, in_=part, compare_op=ALU.not_equal, fill=1.0, base=-32 * r,
                                   pattern=[[0, 64]], channel_multiplier=1).then_inc(s_cc, 1)
            pool.wait_ge(s_cc, 7)
            pool.memset(keep["zero"][:], 0.0).then_inc(s_const, 1)
            with pool.Fori(0, B // 2) as h:
                for i in range(2):
                    b = h * 2 + i
                    t = T[i]
                    pool.wait_ge(s_cvar, b + 1)
                    pool.tensor_tensor(t["r"][:], t["ve"][:], neg_half[:], ALU.pow).then_inc(s_crstd, 1)
                    for n in range(2):
                        pool.wait_ge(s_xvar, 2 * b + 1 + n)
                        pool.tensor_tensor(t["xr"][:], t["xve"][:], neg_half[:, 0:QT], ALU.pow).then_inc(s_xrstd, 1)

        @block.vector
        def _(v):
            v.wait_ge(s_w, 16 * NW)
            half = sh.HD // 2
            for n in range(2):
                for r in range(4):
                    sign = -1.0 if n == 1 and r % 2 == 0 else 1.0
                    last = v.tensor_scalar(trig4[:, n, :, r], trig[:, n], sign, None, ALU.mult)
            last.then_inc(s_trig4, 1)
            w4 = w_raw[:].rearrange("p k (t c n) -> p t k c n", t=3, n=P)
            for t in range(3):
                for k in range(KD):
                    last = v.tensor_copy(w_split[:, :, t, 0, k], w4[:, t, k])
            v.tensor_copy(wo_hi[:], wo_raw[:]).then_inc(s_hi, 1)
            v.wait_ge(s_hi, 1)
            for t in range(3):
                for k in range(KD):
                    last = v.tensor_tensor(w_split[:, :, t, 1, k], w4[:, t, k],
                                           w_split[:, :, t, 0, k].bitcast(F32), ALU.subtract)
            last.then_inc(s_lo, 1)
            v.tensor_tensor(wo_lo[:], wo_raw[:], wo_hi[:].bitcast(F32), ALU.subtract).then_inc(s_lo, 1)

            def stats(src, st, mv, ve, tiles, s_stat, s_var, at):
                for t in range(tiles):
                    last = v.bn_stats(st[:, t], src[:, t])
                last.then_inc(s_stat, 1)
                v.wait_ge(s_stat, 2 * at + 1)
                v.memset(ve[:], EPS)
                for t in range(tiles):
                    last = v.bn_aggr(mv[:, t], st[:, t])
                last.then_inc(s_stat, 1)
                v.wait_ge(s_stat, 2 * at + 2)
                v.tensor_tensor(ve[:], mv[:, :, 1], ve[:], ALU.add).then_inc(s_var, 1)

            def apply(dst, src, mv, r, tiles, s_norm):
                for t in range(tiles):
                    last = v.tensor_scalar(dst[:, t], src[:, t], mv[:, t, 0:1], r[:, t:t + 1], ALU.subtract, ALU.mult)
                last.then_inc(s_norm, 1)

            with v.Fori(0, B // 2) as h:
                for i in range(2):
                    b = h * 2 + i
                    t = T[i]
                    v.wait_ge(s_cin[i], 16 * h + 16)
                    stats(t["ctx"], t["stats"], t["mv"], t["ve"], KT, s_cstat, s_cvar, b)
                    v.wait_ge(s_xin[i], 16 * h + 16)
                    stats(t["x"], t["xstats"], t["xmv"], t["xve"], QT, s_xstat, s_xvar, 2 * b)
                    v.wait_ge(s_crstd, b + 1)
                    apply(t["ctx"], t["ctx"], t["mv"], t["r"], KT, s_cnorm)
                    v.wait_ge(s_xrstd, 2 * b + 1)
                    apply(t["xn"], t["x"], t["xmv"], t["xr"], QT, s_xnorm)
                    v.wait_ge(s_xnorm, 2 * b + 1)
                    stats(t["xn"], t["xstats"], t["xmv"], t["xve"], QT, s_xstat, s_xvar, 2 * b + 1)
                    v.wait_ge(s_cfull, 4 * b + 4)
                    v.wait_ge(s_cout, 16 * b)
                    v.tensor_copy(ctx_split[:, 0], t["full"][:]).then_inc(s_chi, 1)
                    v.wait_ge(s_xrstd, 2 * b + 2)
                    apply(t["x"], t["xn"], t["xmv"], t["xr"], QT, s_xnorm)
                    v.wait_ge(s_chi, b + 1)
                    v.tensor_tensor(ctx_split[:, 1], t["full"][:], ctx_split[:, 0].bitcast(F32), ALU.subtract).then_inc(s_clo, 1)
                    v.wait_ge(s_xfull, 2 * b + 2)
                    v.wait_ge(s_xout, 16 * b)
                    v.tensor_copy(lat_split[:, 0], t["xfull"][:]).then_inc(s_xhi, 1)
                    v.wait_ge(s_xhi, b + 1)
                    v.tensor_tensor(lat_split[:, 1], t["xfull"][:], lat_split[:, 0].bitcast(F32), ALU.subtract).then_inc(s_xlo, 1)

        @block.tensor
        def _(pe):
            pe.wait_ge(s_const, 1)
            pe.wait_ge(s_trig4, 1)
            for n in range(2):
                for k in range(KT):
                    last = pe.transpose(tp[2 * n + k // 4][:, k % 4], trig4[:, n, k].rearrange("p r d -> p (r d)"), ident[:])
            last.then_inc(s_tabT, 1)
            pe.wait_ge(s_tab, 1)
            with pe.Fori(0, B // 2) as h:
                for i in range(2):
                    b = h * 2 + i
                    t = T[i]
                    pe.wait_ge(s_cnorm, b + 1)
                    pe.wait_ge(s_cfull, 4 * b)
                    for k in range(KD):
                        for half in range(2):
                            for j in range(4):
                                last = pe.transpose(tp[2 * k + half][:, j], t["ctx"][:, 4 * half + j, k * P:(k + 1) * P], ident[:])
                            last.then_inc(s_ctr, 1)
                    pe.wait_ge(s_xnorm, 2 * b + 2)
                    pe.wait_ge(s_xfull, 2 * b)
                    for k in range(KD):
                        for j in range(4):
                            last = pe.transpose(tp[4 + k][:, j], t["x"][:, j, k * P:(k + 1) * P], ident[:])
                        last.then_inc(s_xtr, 1)

        @block.scalar
        def _(act):
            act.wait_ge(s_tabT, 1)
            for n, dst in enumerate((cosT, sinT)):
                for k in range(2):
                    last = act.activation(dst[:, 512 * k:512 * k + 512], tp[2 * n + k][:].rearrange("p a b -> p (a b)"), ACT.Copy)
            last.then_inc(s_tab, 1)
            act.wait_ge(s_w, 16 * NW)
            with act.Fori(0, B // 2) as h:
                for i in range(2):
                    b = h * 2 + i
                    t = T[i]
                    act.wait_ge(s_clo, b)
                    for k in range(KD):
                        for half in range(2):
                            act.wait_ge(s_ctr, 4 * b + 2 * k + half + 1)
                            act.activation(t["full"][:, k, 512 * half:512 * half + 512],
                                           tp[2 * k + half][:].rearrange("p a b -> p (a b)"), ACT.Identity,
                                           bias=gb[:, 1, k:k + 1], scale=gb[:, 0, k:k + 1]).then_inc(s_cfull, 1)
                    act.wait_ge(s_xlo, b)
                    for k in range(KD):
                        act.wait_ge(s_xtr, 2 * b + k + 1)
                        act.activation(t["xfull"][:, k], tp[4 + k][:].rearrange("p a b -> p (a b)"), ACT.Identity,
                                       bias=gb[:, 3, k:k + 1], scale=gb[:, 2, k:k + 1]).then_inc(s_xfull, 1)


def attend(nc, sh, x, bo, wpack, ctxT, latT, x1, xs, keep):
    KD, KT, QT, PAIRS, D, B, N, S, HD = sh.KD, sh.KT, sh.QT, sh.PAIRS, sh.D, sh.B, sh.N, sh.S, sh.HD
    with ExitStack() as es:
        def sb(name, shape, dt=F32):
            return es.enter_context(nc.sbuf_tensor(name, shape, dt))

        def ps(name, shape, dt=F32):
            return es.enter_context(nc.psum_tensor(name, shape, dt))

        def sem(name):
            return es.enter_context(nc.semaphore(name))

        ident, cosT, sinT, wo_hi, wo_lo = keep["ident"], keep["cosT"], keep["sinT"], keep["wo_hi"], keep["wo_lo"]
        sel, ones = keep["sel"], keep["ones"]
        STEPS = KT
        PROJ = 7
        PROBS = 4

        w = [sb(f"w{i}", [P, 3, 2, KD, P], F32R) for i in range(2)]
        ctxs = sb("ctxs", [P, 2, KD, S], F32R)
        lats = sb("lats", [P, 2, KD, N], F32R)
        kT = sb("kT", [P, S])
        kT_swap = sb("kT_swap", [P, S])
        k_sin = sb("k_sin", [P, S])
        k_rope = sb("k_rope", [P, S])
        k_split = sb("k_split", [P, 2, S], F32R)
        k_st = [sb(f"k_st{i}", [P, 2, S], F32R) for i in range(2)]
        vT = sb("vT", [P, S])
        v_nat = [sb(f"v_nat{i}", [P, KT, P]) for i in range(2)]
        qT = sb("qT", [P, N])
        q_split = sb("q_split", [P, 2, N], F32R)
        q_st = [sb(f"q_st{i}", [P, 2, 2, N], F32R) for i in range(2)]
        probs = [sb(f"probs{i}", [P, 2, N]) for i in range(PROBS)]
        sums_sb = sb("sums_sb", [P, N])
        u_sb = sb("u_sb", [P, N])
        rden = sb("rden", [P, N])
        o_n = sb("o_n", [P, N])
        o_hi = sb("o_hi", [P, PAIRS, N], F32R)
        o_lo = sb("o_lo", [P, PAIRS, N], F32R)
        x_in = sb("x_in", [P, QT, D])
        x_out = sb("x_out", [P, QT, D])
        bo_bc = sb("bo_bc", [P, D])

        scores = [ps(f"scores{i}", [P, 2, N]) for i in range(2)]
        pv_ps = ps("pv_ps", [P, N])
        sums_ps = ps("sums_ps", [P, N])
        proj = [ps(f"proj{i}", [P, N]) for i in range(2)]

        s_w = [sem(f"s_w1{i}") for i in range(2)]
        s_ctx, s_lat = sem("s_ctx"), sem("s_lat")
        s_xin = sem("s_xin")
        s_bo = sem("s_bo")
        s_proj = sem("s_proj")
        s_projout = sem("s_projout")
        s_swap = sem("s_swap")
        s_rope = sem("s_rope")
        s_ksplit = sem("s_ksplit")
        s_kst = sem("s_kst")
        s_qhi = sem("s_qhi")
        s_qsplit = sem("s_qsplit")
        s_qst = sem("s_qst")
        s_scores = sem("s_scores")
        s_exp = sem("s_exp")
        s_clip = sem("s_clip")
        s_pfree = sem("s_pfree")
        s_us = sem("s_us")
        s_den = sem("s_den")
        s_rden = sem("s_rden")
        s_norm = sem("s_norm")
        s_o = sem("s_o")
        s_wo = sem("s_wo")
        s_x1 = sem("s_x1")
        s_x1r = sem("s_x1r")
        s_out = sem("s_out")
        s_zero = sem("s_zero")

        block = es.enter_context(nc.Block())

        def pairs(eng, body, tail):
            with eng.Fori(0, B) as b:
                with eng.Fori(0, PAIRS // 2 - 1) as k:
                    for u in range(2):
                        body(b * PAIRS + k * 2 + u, b, u, k * 2 + u, True, b * (PAIRS // 2) + k)
                for u in range(2):
                    p = PAIRS - 2 + u
                    body(b * PAIRS + p, b, u, p, u == 0, b * (PAIRS // 2) + PAIRS // 2 - 1)
                tail(b, b * PAIRS + PAIRS)

        @block.sync
        def _(sp):
            def load_w(p, u):
                sp.dma_start(w[u][:].rearrange("p a b k n -> p (a b k n)").bitcast(F32), wpack[p]).then_inc(s_w[u], 16)

            def load_batch(b):
                sp.dma_start(ctxs[:].rearrange("p a k n -> p (a k n)").bitcast(F32), ctxT[b]).then_inc(s_ctx, 16)
                sp.dma_start(lats[:].rearrange("p a k n -> p (a k n)").bitcast(F32), latT[b]).then_inc(s_lat, 16)

            def move(n, u):
                sp.wait_ge(s_projout, PROJ * n + 2)
                sp.wait_ge(s_ksplit, n)
                for q in range(4):
                    if q == 1 and not isinstance(n, int):
                        sp.wait_ge(s_scores, STEPS * (n - 1))
                    sp.dma_start(kT_swap[32 * q:32 * q + 32], kT[32 * (q ^ 1):32 * (q ^ 1) + 32]).then_inc(s_swap, 16)
                sp.wait_ge(s_ksplit, n + 1)
                for head in range(2):
                    for part in range(2):
                        sp.dma_start(k_st[u][64 * part:64 * part + 64, head].bitcast(F32),
                                     k_split[64 * head:64 * head + 64, part].bitcast(F32)).then_inc(s_kst, 16)
                sp.wait_ge(s_qsplit, n + 1)
                for head in range(2):
                    for twice in range(2):
                        sp.dma_start(q_st[u][64 * twice:64 * twice + 64, head].bitcast(F32),
                                     q_split[64 * head:64 * head + 64].bitcast(F32)).then_inc(s_qst, 16)

            load_w(0, 0)
            load_batch(0)
            load_w(1, 1)
            with nc.allow_non_contiguous_dma(reason="one row to all partitions"):
                sp.dma_start(bo_bc[:], bo.rearrange("(a n) -> a n", a=1).broadcast_to((P, D))).then_inc(s_bo, 16)
            move(0, 0)

            def body(c, b, u, p, more, h):
                if not more:
                    return
                sp.wait_ge(s_proj, PROJ * c + 5)
                load_w(p + 2, u)
                move(c + 1, 1 - u)

            def tail(b, c):
                sp.wait_ge(s_proj, PROJ * c - 2)
                load_batch(b + 1)
                load_w(1, 1)
                sp.wait_ge(s_x1r, b)
                sp.dma_start(x_in[:], x[b].rearrange("(p t) d -> p t d", p=P)).then_inc(s_xin, 16)
                move(c, 0)
                sp.wait_ge(s_x1r, b + 1)
                sp.dma_start(x1[b].rearrange("(p t) d -> p t d", p=P), x_out[:]).then_inc(s_out, 16)

            pairs(sp, body, tail)
            sp.wait_ge(s_out, 16 * B)
            sp.wait_ge(s_kst, 64 * (B * PAIRS + 1))
            sp.wait_ge(s_qst, 64 * (B * PAIRS + 1))
            sp.wait_ge(s_w[0], 16 * (1 + B * PAIRS // 2))
            sp.wait_ge(s_w[1], 16 * (1 + B * PAIRS // 2))

        @block.gpsimd
        def _(pool):
            flat = xs.rearrange("r n d -> (r n d)").rearrange("(c p z) -> c p z", p=P, z=ZERO)
            for c in range(flat.shape[0]):
                pool.dma_start(flat[c], keep["zero"][:]).then_inc(s_zero, 16)
            pool.wait_ge(s_zero, 16 * flat.shape[0])

        @block.tensor
        def _(pe):
            pe.sem_inc(s_pfree, PROBS)

            def project(bank, which, u, moving, col):
                n = 0
                for k in range(KD):
                    for wpart, mpart in ((0, 0), (0, 1), (1, 0)):
                        last = pe.matmul(proj[bank][:], w[u][:, which, wpart, k], moving[:, mpart, k, col:col + 512],
                                         start=n == 0, stop=n == 3 * KD - 1)
                        n += 1
                last.then_inc(s_proj, 1)

            def project_k(n, u, half, h, done):
                if half == 0:
                    pe.wait_ge(s_w[u], 16 * (h + 1))
                    pe.wait_ge(s_projout, PROJ * n)
                else:
                    pe.wait_ge(s_rden, done)
                    pe.wait_ge(s_projout, PROJ * n)
                project(half, 0, u, ctxs, 512 * half)

            def project_v(n, u, half):
                pe.wait_ge(s_projout, PROJ * n + 1 + half)
                project(half, 1, u, ctxs, 512 * half)

            def project_q(n, u):
                pe.wait_ge(s_projout, PROJ * n + 3)
                project(0, 2, u, lats, 0)

            def transpose_v(n, half):
                pe.wait_ge(s_projout, PROJ * n + 4 + half)
                for j in range(4):
                    last = pe.transpose(proj[1 - half][:, j * P:(j + 1) * P], vT[:, (4 * half + j) * P:(4 * half + j + 1) * P], ident[:])
                last.then_inc(s_proj, 1)

            def score(c, u, j):
                if j == 0:
                    pe.wait_ge(s_kst, 64 * (c + 1))
                    pe.wait_ge(s_qst, 64 * (c + 1))
                for head in range(2):
                    for part in range(2):
                        last = pe.matmul(scores[j % 2][:, head], k_st[u][:, head, j * P:(j + 1) * P],
                                         q_st[u][:, head, part], start=part == 0, stop=part == 1)
                last.then_inc(s_scores, 1)

            def weigh(c, u, j):
                pe.wait_ge(s_clip, STEPS * c + j + 1)
                if j == 0:
                    pe.wait_ge(s_us, 2 * c)
                pr = probs[j % PROBS]
                for head in range(2):
                    last = pe.matmul(pv_ps[64 * head:64 * head + 64], v_nat[u][:, j, 64 * head:64 * head + 64], pr[:, head],
                                     start=j == 0, stop=j == STEPS - 1)
                if j % 2 == 1:
                    for q in range(4):
                        last = pe.matmul(sums_ps[32 * q:32 * q + 32], ones[:], probs[(j - 1 + q % 2) % PROBS][:, q // 2],
                                         start=j == 1, stop=j == STEPS - 1)
                    last.then_inc(s_pfree, 2)

            def denominators(c):
                pe.wait_ge(s_us, 2 * c + 1)
                pe.wait_ge(s_rden, c)
                pe.matmul(proj[1][:], sel[:], sums_sb[:], start=True, stop=True).then_inc(s_den, 1)


            pe.wait_ge(s_ctx, 16)
            pe.wait_ge(s_lat, 16)
            for half in range(2):
                project_k(0, 0, half, 0, 0)
            for half in range(2):
                project_v(0, 0, half)
            project_q(0, 0)
            for half in range(2):
                transpose_v(0, half)
            pe.wait_ge(s_kst, 64)
            score(0, 0, 0)

            def body(c, b, u, p, more, h):
                n, un = c + 1, 1 - u
                for j in range(1, STEPS):
                    pe.wait_ge(s_exp, STEPS * c + j - 1)
                    if j == 1:
                        pe.wait_ge(s_x1, b)
                    score(c, u, j)
                    if more:
                        if j <= 2:
                            project_k(n, un, j - 1, h + u, c)
                        elif j <= 4:
                            project_v(n, un, j - 3)
                        elif j == 5:
                            project_q(n, un)
                        elif j == 6:
                            transpose_v(n, 0)
                    weigh(c, u, j - 1)
                if more:
                    pe.wait_ge(s_exp, STEPS * c + STEPS - 1)
                    score(n, un, 0)
                    weigh(c, u, STEPS - 1)
                    transpose_v(n, 1)
                    pe.wait_ge(s_projout, PROJ * n + 6)
                    denominators(c)
                else:
                    weigh(c, u, STEPS - 1)
                    denominators(c)

            def tail(b, c):
                pe.wait_ge(s_ctx, 16 * (b + 2))
                pe.wait_ge(s_lat, 16 * (b + 2))
                for half in range(2):
                    project_k(c, 0, half, (b + 1) * (PAIRS // 2), c)
                for half in range(2):
                    project_v(c, 0, half)
                project_q(c, 0)
                for half in range(2):
                    transpose_v(c, half)
                pe.wait_ge(s_exp, STEPS * c)
                out = scores[1][:].rearrange("p a (t n) -> p (a t) n", t=2)
                for p in range(PAIRS):
                    if p == 0:
                        pe.wait_ge(s_o, c - 1)
                    if p == PAIRS - 1:
                        pe.wait_ge(s_o, c)
                    for t in range(QT):
                        for n, (o, wo) in enumerate(((o_hi, wo_hi), (o_lo, wo_hi), (o_hi, wo_lo))):
                            last = pe.matmul(out[:, t], o[:, p, t * P:(t + 1) * P], wo[:, p],
                                             start=p == 0 and n == 0 and t % 2 == 0, stop=p == PAIRS - 1 and n == 2,
                                             skip_group_check=True)
                last.then_inc(s_wo, 1)
                score(c, 0, 0)

            pairs(pe, body, tail)

        @block.scalar
        def _(act):
            def exponentiate(c, j):
                act.wait_ge(s_scores, STEPS * c + j + 1)
                act.wait_ge(s_pfree, STEPS * c + j + 1)
                act.activation(probs[j % PROBS][:], scores[j % 2][:], ACT.Exp, scale=float(HD) ** -0.5).then_inc(s_exp, 1)

            def copy_out(n, i, u):
                act.wait_ge(s_proj, PROJ * n + i + 1)
                if i == 0:
                    act.wait_ge(s_rope, 4 * n)
                    act.wait_ge(s_swap, 64 * n)
                    act.activation(kT[:, 0:512], proj[0][:], ACT.Copy).then_inc(s_projout, 1)
                elif i == 1:
                    act.activation(kT[:, 512:1024], proj[1][:], ACT.Copy).then_inc(s_projout, 1)
                elif i < 4:
                    act.activation(vT[:, 512 * (i - 2):512 * (i - 1)], proj[i - 2][:], ACT.Copy).then_inc(s_projout, 1)
                elif i == 4:
                    act.wait_ge(s_qsplit, n)
                    act.activation(qT[:], proj[0][:], ACT.Copy).then_inc(s_projout, 1)
                else:
                    half = i - 5
                    act.activation(v_nat[u][:, 4 * half:4 * half + 4].rearrange("p t n -> p (t n)"),
                                   proj[1 - half][:], ACT.Copy).then_inc(s_projout, 1)

            for i in range(PROJ):
                copy_out(0, i, 0)
            exponentiate(0, 0)

            def copy_sums(c):
                act.wait_ge(s_pfree, STEPS * c + STEPS + PROBS)
                act.wait_ge(s_den, c)
                act.activation(sums_sb[:], sums_ps[:], ACT.Copy).then_inc(s_us, 1)
                act.wait_ge(s_norm, 2 * c)
                act.activation(u_sb[:], pv_ps[:], ACT.Copy).then_inc(s_us, 1)

            def body(c, b, u, p, more, h):
                n, un = c + 1, 1 - u
                for j in range(1, STEPS):
                    exponentiate(c, j)
                    if more and j <= 6:
                        copy_out(n, j - 1, un)
                if more:
                    exponentiate(n, 0)
                copy_sums(c)
                if more:
                    copy_out(n, 6, un)

            def tail(b, c):
                for i in range(PROJ):
                    copy_out(c, i, 0)
                exponentiate(c, 0)

            pairs(act, body, tail)

        @block.vector
        def _(v):
            def clip(c, j):
                v.wait_ge(s_exp, STEPS * c + j + 1)
                pr = probs[j % PROBS][:]
                v.tensor_scalar(pr, pr, EXP_LO, EXP_HI, ALU.max, ALU.min).then_inc(s_clip, 1)

            def rope(n, i):
                if i == 0:
                    v.wait_ge(s_projout, PROJ * n + 2)
                    v.tensor_tensor(k_rope[:], kT[:], cosT[:], ALU.mult).then_inc(s_rope, 1)
                elif i == 1:
                    v.wait_ge(s_swap, 64 * (n + 1))
                    v.tensor_tensor(k_sin[:], kT_swap[:], sinT[:], ALU.mult).then_inc(s_rope, 1)
                elif i == 2:
                    v.wait_ge(s_rope, 4 * n + 2)
                    v.tensor_tensor(k_rope[:], k_rope[:], k_sin[:], ALU.add).then_inc(s_rope, 1)
                elif i == 3:
                    v.wait_ge(s_rope, 4 * n + 3)
                    v.wait_ge(s_kst, 64 * n)
                    v.tensor_copy(k_split[:, 0], k_rope[:]).then_inc(s_rope, 1)
                else:
                    v.wait_ge(s_rope, 4 * n + 4)
                    v.tensor_tensor(k_split[:, 1], k_rope[:], k_split[:, 0].bitcast(F32), ALU.subtract).then_inc(s_ksplit, 1)

            def split_q(n):
                v.wait_ge(s_projout, PROJ * n + 5)
                v.wait_ge(s_qst, 64 * n)
                v.tensor_copy(q_split[:, 0], qT[:]).then_inc(s_qhi, 1)
                v.wait_ge(s_qhi, n + 1)
                v.tensor_tensor(q_split[:, 1], qT[:], q_split[:, 0].bitcast(F32), ALU.subtract).then_inc(s_qsplit, 1)

            def normalise(c, b, p):
                v.wait_ge(s_den, c + 1)
                v.reciprocal(rden[:], proj[1][:]).then_inc(s_rden, 1)
                v.wait_ge(s_rden, c + 1)
                v.wait_ge(s_us, 2 * c + 2)
                v.tensor_tensor(o_n[:], u_sb[:], rden[:], ALU.mult).then_inc(s_norm, 1)
                v.wait_ge(s_norm, 2 * c + 1)
                v.wait_ge(s_wo, b)
                v.tensor_copy(o_hi[:, p], o_n[:]).then_inc(s_norm, 1)
                v.wait_ge(s_norm, 2 * c + 2)
                v.tensor_tensor(o_lo[:, p], o_n[:], o_hi[:, p].bitcast(F32), ALU.subtract).then_inc(s_o, 1)

            for i in range(5):
                rope(0, i)
            split_q(0)
            clip(0, 0)

            def body(c, b, u, p, more, h):
                n = c + 1
                for j in range(1, STEPS):
                    clip(c, j)
                    if more:
                        if j in (3, 4):
                            rope(n, j - 3)
                        elif j == 5:
                            for i in (2, 3, 4):
                                rope(n, i)
                        elif j == 6:
                            split_q(n)
                if more:
                    clip(n, 0)
                normalise(c, b, p)

            def tail(b, c):
                for i in range(5):
                    rope(c, i)
                split_q(c)
                v.wait_ge(s_wo, b + 1)
                v.wait_ge(s_out, 16 * b)
                v.tensor_tensor(x_out[:], scores[1][:].rearrange("p a (t n) -> p (a t) n", t=2),
                                bo_bc[:].unsqueeze(1).broadcast_to((P, QT, D)), ALU.add).then_inc(s_x1, 1)
                v.wait_ge(s_x1, b + 1)
                v.wait_ge(s_xin, 16 * (b + 1))
                v.tensor_tensor(x_out[:], x_out[:], x_in[:], ALU.add).then_inc(s_x1r, 1)
                clip(c, 0)

            v.wait_ge(s_bo, 16)
            pairs(v, body, tail)


def normalise_tokens(nc, sh, x1, router_w, xn_d, xnT, ffn):
    KD, QT, D, B, N, E = sh.KD, sh.QT, sh.D, sh.B, sh.N, sh.E
    with ExitStack() as es:
        def sb(name, shape, dt=F32):
            return es.enter_context(nc.sbuf_tensor(name, shape, dt))

        def sem(name):
            return es.enter_context(nc.semaphore(name))

        ident, acc, logits = ffn["ident"], ffn["acc"], ffn["logits"]
        T = [dict(x=sb(f"tx{i}", [P, QT, D]), xn=sb(f"txn{i}", [P, QT, D]), stats=sb(f"tst{i}", [P, QT, 6]),
                  mv=sb(f"tmv{i}", [P, QT, 2]), ve=sb(f"tve{i}", [P, QT]), r=sb(f"tr{i}", [P, QT]),
                  xT=sb(f"txT{i}", [P, KD, N]), split=sb(f"tsplit{i}", [P, 2, KD, N], F32R)) for i in range(2)]
        rw = sb("rw", [P, KD, E])
        neg_half = sb("t_neg_half", [P, QT])
        tp = [[es.enter_context(nc.psum_tensor(f"ttp{i}{k}", [P, QT, P], F32)) for k in range(KD)] for i in range(2)]
        lg = [es.enter_context(nc.psum_tensor(f"tlg{i}", [P, QT, E], F32)) for i in range(2)]

        s_rw, s_const = sem("t_rw"), sem("t_const")
        s_in = [sem(f"t_in{i}") for i in range(2)]
        s_stat, s_var, s_rstd, s_norm = sem("t_stat"), sem("t_var"), sem("t_rstd"), sem("t_norm")
        s_acc = sem("t_acc")
        s_tr, s_cp = sem("t_tr"), sem("t_cp")
        s_hi, s_lo = sem("t_hi"), sem("t_lo")
        s_lg, s_lgout = sem("t_lg"), sem("t_lgout")
        s_stn = [sem(f"t_stn{i}") for i in range(2)]
        s_stT = [sem(f"t_stT{i}") for i in range(2)]
        block = es.enter_context(nc.Block())

        @block.sync
        def _(sp):
            for i in range(2):
                sp.dma_start(T[i]["x"][:], x1[i].rearrange("(p t) d -> p t d", p=P)).then_inc(s_in[i], 16)
            sp.dma_start(rw[:], router_w.rearrange("(k p) e -> p k e", p=P)).then_inc(s_rw, 16)
            with sp.Fori(0, B // 2) as h:
                for i in range(2):
                    b = h * 2 + i
                    sp.wait_ge(s_norm, b + 1)
                    sp.dma_start(xn_d[b].rearrange("(p t) d -> p t d", p=P), T[i]["xn"][:]).then_inc(s_stn[i], 16)
                    sp.wait_ge(s_lo, b + 1)
                    sp.dma_start(xnT[b], T[i]["split"][:].rearrange("p a k n -> p (a k n)").bitcast(F32)).then_inc(s_stT[i], 16)
                    sp.wait_ge(s_acc, b + 1)
                    sp.dma_start(T[i]["x"][:], x1[(b + 2) % B].rearrange("(p t) d -> p t d", p=P)).then_inc(s_in[i], 16)
            for i in range(2):
                sp.wait_ge(s_stn[i], 16 * (B // 2))
                sp.wait_ge(s_stT[i], 16 * (B // 2))
                sp.wait_ge(s_in[i], 16 * (B // 2 + 1))

        @block.gpsimd
        def _(pool):
            pool.memset(neg_half[:], -0.5).then_inc(s_const, 1)
            pool.wait_ge(s_const, 1)
            with pool.Fori(0, B // 2) as h:
                for i in range(2):
                    pool.wait_ge(s_var, h * 2 + i + 1)
                    pool.tensor_tensor(T[i]["r"][:], T[i]["ve"][:], neg_half[:], ALU.pow).then_inc(s_rstd, 1)

        @block.vector
        def _(v):
            def first(b, i, at):
                t = T[i]
                v.wait_ge(s_in[i], at)
                for q in range(QT):
                    last = v.bn_stats(t["stats"][:, q], t["x"][:, q])
                last.then_inc(s_stat, 1)
                v.wait_ge(s_stat, 2 * b + 1)
                v.memset(t["ve"][:], EPS)
                for q in range(QT):
                    last = v.bn_aggr(t["mv"][:, q], t["stats"][:, q])
                last.then_inc(s_stat, 1)
                v.wait_ge(s_stat, 2 * b + 2)
                v.tensor_tensor(t["ve"][:], t["mv"][:, :, 1], t["ve"][:], ALU.add).then_inc(s_var, 1)

            def second(b, i, h):
                t = T[i]
                v.wait_ge(s_rstd, b + 1)
                v.wait_ge(s_stn[i], 16 * h)
                for q in range(QT):
                    last = v.tensor_scalar(t["xn"][:, q], t["x"][:, q], t["mv"][:, q, 0:1], t["r"][:, q:q + 1], ALU.subtract, ALU.mult)
                last.then_inc(s_norm, 1)
                v.wait_ge(s_norm, b + 1)
                v.tensor_tensor(acc[:, bass.ds(b * QT, QT)], t["x"][:], t["xn"][:], ALU.add).then_inc(s_acc, 1)

            def third(b, i, h):
                t = T[i]
                v.wait_ge(s_cp, 2 * b + 2)
                v.wait_ge(s_stT[i], 16 * h)
                v.tensor_copy(t["split"][:, 0], t["xT"][:]).then_inc(s_hi, 1)
                v.wait_ge(s_hi, b + 1)
                v.tensor_tensor(t["split"][:, 1], t["xT"][:], t["split"][:, 0].bitcast(F32), ALU.subtract).then_inc(s_lo, 1)

            with v.Fori(0, B // 2) as h:
                for i in range(2):
                    first(h * 2 + i, i, 16 * h + 16)
                for i in range(2):
                    second(h * 2 + i, i, h)
                for i in range(2):
                    third(h * 2 + i, i, h)

        @block.tensor
        def _(pe):
            pe.wait_ge(s_rw, 16)
            with pe.Fori(0, B // 2) as h:
                for i in range(2):
                    b = h * 2 + i
                    t = T[i]
                    pe.wait_ge(s_norm, b + 1)
                    pe.wait_ge(s_cp, 4 * h)
                    for k in range(KD):
                        for q in range(QT):
                            last = pe.transpose(tp[i][k][:, q], t["xn"][:, q, k * P:(k + 1) * P], ident[:])
                        last.then_inc(s_tr, 1)
                for i in range(2):
                    b = h * 2 + i
                    t = T[i]
                    pe.wait_ge(s_cp, 2 * b + 2)
                    pe.wait_ge(s_lgout, 2 * h)
                    for q in range(QT):
                        for k in range(KD):
                            last = pe.matmul(lg[i][:, q], t["xT"][:, k, q * P:(q + 1) * P], rw[:, k], start=k == 0, stop=k == KD - 1)
                    last.then_inc(s_lg, 1)

        @block.scalar
        def _(act):
            with act.Fori(0, B // 2) as h:
                for i in range(2):
                    b = h * 2 + i
                    act.wait_ge(s_lo, 2 * h)
                    act.wait_ge(s_lg, 2 * h)
                    for k in range(KD):
                        act.wait_ge(s_tr, 2 * b + k + 1)
                        act.activation(T[i]["xT"][:, k], tp[i][k][:].rearrange("p a b -> p (a b)"), ACT.Copy).then_inc(s_cp, 1)
                for i in range(2):
                    b = h * 2 + i
                    act.wait_ge(s_lg, b + 1)
                    act.activation(logits[:, bass.ds(b * QT, QT)], lg[i][:], ACT.Copy).then_inc(s_lgout, 1)


def experts(nc, sh, xn_d, xnT, xs, ys, shared_up, shared_down, routed_up, routed_down, out, ffn):
    KD, QT, D, B, N, E, F = sh.KD, sh.QT, sh.D, sh.B, sh.N, sh.E, sh.F
    FT = F // P
    NT = B * QT
    TILES = sh.TILES
    with ExitStack() as es:
        def sb(name, shape, dt=F32):
            return es.enter_context(nc.sbuf_tensor(name, shape, dt))

        def sem(name):
            return es.enter_context(nc.semaphore(name))

        ident, acc, logits = ffn["ident"], ffn["acc"], ffn["logits"]
        raw = [[sb(f"raw{i}{n}", [P, KD * F]) for n in range(2)] for i in range(2)]
        up = [sb(f"up{i}", [P, 2, KD * F], F32R) for i in range(2)]
        down = [sb(f"down{i}", [P, 2, KD * F], F32R) for i in range(2)]
        xT = [sb(f"xT{i}", [P, 2, KD, N], F32R) for i in range(2)]
        rows = [sb(f"rows{i}", [P, QT, D]) for i in range(2)]
        hid = [sb(f"hid{i}", [P, N]) for i in range(2)]
        hid_split = [sb(f"hid_split{i}", [P, 2, N], F32R) for i in range(4)]
        y_sb = sb("y_sb", [P, QT, D])
        tri = sb("tri", [P, P])
        all_ones = sb("all_ones", [P, P])
        before = sb("before", [P, E, E])
        steps_n = sb("steps_n", [P, E, E])
        tile_no = sb("tile_no", [P, TILES, E - 1])
        probs = sb("r_probs", [P, NT, E])
        mx, tot, rtot = sb("r_mx", [P, NT]), sb("r_tot", [P, NT]), sb("r_rtot", [P, NT])
        rank = sb("r_rank", [P, NT, E])
        sel0, sel1, both = sb("r_sel0", [P, NT, E]), sb("r_sel1", [P, NT, E]), sb("r_both", [P, NT, E])
        gate = [sb(f"gate{i}", [P, NT]) for i in range(2)]
        counts_et = sb("r_counts", [P, E, NT])
        run = sb("r_run", [P, E, NT])
        n_tiles, ends, base, count = sb("r_nt", [P, E]), sb("r_ends", [P, E]), sb("r_base", [P, E]), sb("r_cnt", [P, E])
        ones_e = sb("r_ones", [P, E * NT])
        pos = sb("r_pos", [P, NT, E])
        idx = [sb(f"idx{i}", [P, NT], I32) for i in range(2)]
        tmp = sb("r_tmp", [P, NT, E])
        posf = sb("r_posf", [P, NT])
        tile_e = sb("tile_e", [P, TILES])
        tile_ei = sb("tile_ei", [P, TILES], I32)

        pair_big = raw[1][0][:].rearrange("p (t e f) -> p t e f", e=E, f=E)
        eq_big = raw[1][1][:].rearrange("p (t e f) -> p t e f", e=E, f=E)

        gat = [[raw[i][n][:, 0:QT * D].rearrange("p (t d) -> p t d", d=D) for n in range(2)] for i in range(2)]

        def ps(name, shape):
            return es.enter_context(nc.psum_tensor(name, shape, F32))

        hp = [ps(f"hp{i}", [P, N]) for i in range(4)]
        yp = ps("yp", [P, QT, D])
        tp = [ps(f"ftp{k}", [P, QT, P]) for k in range(KD)]

        s_cc, s_const = sem("f_cc"), sem("f_const")
        s_r = sem("f_r")
        s_re = sem("f_re")
        s_rm = sem("f_rm")
        s_idx = sem("f_idx")
        s_stage = [sem(f"f_stage{i}") for i in range(2)]
        s_scat = [sem(f"f_scat{i}") for i in range(2)]
        s_scatall = sem("f_scatall")
        s_raw = [sem(f"f_raw{i}") for i in range(2)]
        s_shT = [sem(f"f_shT{i}") for i in range(2)]
        s_rows = [sem(f"f_rows{i}") for i in range(2)]
        s_whi, s_wlo = sem("f_whi"), sem("f_wlo")
        s_tr = sem("f_tr")
        s_xhi, s_xlo = sem("f_xhi"), sem("f_xlo")
        s_up = sem("f_up")
        s_hhi, s_hlo = sem("f_hhi"), sem("f_hlo")
        s_dn = sem("f_dn")
        s_y = sem("f_y")
        s_yout = sem("f_yout")
        s_gat = [sem(f"f_gat{i}") for i in range(2)]
        s_comb = sem("f_comb")
        s_out = sem("f_out")
        s_half = sem("f_half")
        block = es.enter_context(nc.Block())

        @block.sync
        def _(sp):
            def load_raw(i, up_ap, down_ap):
                sp.dma_start(raw[i][0][:].rearrange("p (k f) -> p k f", k=KD), up_ap.rearrange("(k p) f -> p k f", p=P)).then_inc(s_raw[i], 16)
                sp.dma_start(raw[i][1][:].rearrange("p (c n) -> p c n", n=D), down_ap.rearrange("(c p) n -> p c n", p=P)).then_inc(s_raw[i], 16)

            def load_expert(r, i):
                e = sp.value_load(tile_ei[0:1, bass.ds(r, 1)], min_val=0, max_val=E - 1)
                load_raw(i, routed_up[e], routed_down[e])

            def load_rows(r, i):
                sp.dma_start(rows[i][:], xs[r].rearrange("(p t) d -> p t d", p=P)).then_inc(s_rows[i], 16)

            def load_shared(b, i):
                sp.dma_start(xT[i][:].rearrange("p a k n -> p (a k n)").bitcast(F32), xnT[b]).then_inc(s_shT[i], 16)

            load_raw(0, shared_up[0], shared_down[0])
            load_shared(0, 0)
            load_shared(1, 1)

            sp.wait_ge(s_idx, 1)
            sp.wait_ge(s_wlo, FT)
            load_expert(0, 0)
            load_expert(1, 1)
            with sp.Fori(0, B // 2 - 1) as h:
                for i in range(2):
                    b = h * 2 + i
                    sp.wait_ge(s_up, FT * b + FT)
                    load_shared(b + 2, i)
            sp.wait_ge(s_scatall, 1)
            load_rows(0, 0)
            load_rows(1, 1)

            def store(r):
                sp.wait_ge(s_y, B + r + 1)
                sp.dma_start(ys[r].rearrange("(p t) d -> p t d", p=P), y_sb[:]).then_inc(s_yout, 16)

            with sp.Fori(0, TILES // 2 - 1) as k:
                for i in range(2):
                    r = k * 2 + i
                    sp.wait_ge(s_wlo, FT * (r + 2))
                    load_expert(r + 2, i)
                    sp.wait_ge(s_tr, r + 1)
                    load_rows(r + 2, i)
                    store(r)
            r = TILES - 3
            sp.wait_ge(s_wlo, FT * (r + 2))
            load_expert(r + 2, r % 2)
            sp.wait_ge(s_tr, r + 1)
            load_rows(r + 2, r % 2)
            for r in range(TILES - 3, TILES):
                store(r)
            sp.wait_ge(s_yout, 16 * TILES)
            with sp.Fori(0, B // 2) as h:
                for i in range(2):
                    b = h * 2 + i
                    sp.wait_ge(s_comb, b + 1)
                    sp.dma_start(out[b].rearrange("(p t) d -> p t d", p=P), acc[:, bass.ds(b * QT, QT)]).then_inc(s_out, 16)
            sp.wait_ge(s_out, 16 * B)

        @block.gpsimd
        def _(pool):
            pool.memset(tri[:], 1.0)
            pool.memset(all_ones[:], 1.0)
            pool.memset(ones_e[:], 1.0)
            pool.memset(before[:], 1.0)
            pool.iota(steps_n[:], pattern=[[0, E], [N, E]], base=0, channel_multiplier=0, allow_small_or_imprecise_dtypes=True)
            pool.iota(tile_no[:], pattern=[[1, TILES], [0, E - 1]], base=0, channel_multiplier=0,
                      allow_small_or_imprecise_dtypes=True).then_inc(s_cc, 1)
            pool.wait_ge(s_cc, 1)
            pool.affine_select(out=tri[:], in_=tri[:], compare_op=ALU.is_gt, fill=0.0, base=0,
                               pattern=[[1, P]], channel_multiplier=-1).then_inc(s_cc, 1)
            pool.affine_select(out=before[:], in_=before[:], compare_op=ALU.is_gt, fill=0.0, base=0,
                               pattern=[[1, E], [-1, E]], channel_multiplier=0).then_inc(s_cc, 1)
            pool.wait_ge(s_cc, 3)
            pool.memset(posf[:], 0.0).then_inc(s_const, 1)
            for b in range(B):
                i = b % 2
                if b >= 2:
                    pool.wait_ge(s_scat[i], 16 * 2 * QT * (b // 2))
                pool.dma_start(rows[i][:], xn_d[b].rearrange("(p t) d -> p t d", p=P)).then_inc(s_stage[i], 16)
                if b == 0:
                    pool.wait_ge(s_idx, 1)
                pool.wait_ge(s_stage[i], 16 * (b // 2 + 1))
                for t in range(QT):
                    for n in range(2):
                        pool.indirect_dma_start(xs.rearrange("r n d -> (r n) d"),
                                                bass.IndirectOffsetOnAxis(ap=idx[n][:, b * QT + t:b * QT + t + 1], axis=0),
                                                rows[i][:, t], None).then_inc(s_scat[i], 16)
            for i in range(2):
                pool.wait_ge(s_scat[i], 16 * 2 * QT * (B // 2))
            pool.sem_inc(s_scatall, 1)
            pool.wait_ge(s_y, B + TILES)
            pool.wait_ge(s_yout, 16 * TILES)
            for b in range(B):
                i = b % 2
                if b >= 2:
                    pool.wait_ge(s_comb, b - 1)
                for t in range(QT):
                    for n in range(2):
                        pool.indirect_dma_start(gat[i][n][:, t], None, ys.rearrange("r n d -> (r n) d"),
                                                bass.IndirectOffsetOnAxis(ap=idx[n][:, b * QT + t:b * QT + t + 1], axis=0)
                                                ).then_inc(s_gat[i], 16)

        def tiles(eng, body):
            with eng.Fori(0, B // 2 - 1) as h:
                body(h * 2, 0, None, "shared", None, h)
                body(h * 2 + 1, 1, None, "shared", None, h + 1)
            body(B - 2, 0, None, "shared", None, B // 2 - 1)
            body(B - 1, 1, None, "routed", 0, 0)
            with eng.Fori(0, TILES // 2) as k:
                body(B + k * 2, 0, k * 2, "routed", k * 2 + 1, k)
                body(B + k * 2 + 1, 1, k * 2 + 1, "routed", k * 2 + 2, k + 1)
            body(B + TILES - 1, 0, TILES - 1, None, None, None)

        @block.tensor
        def _(pe):
            pe.wait_ge(s_const, 1)
            pe.wait_ge(s_r, R_BOTH)
            pe.matmul(hp[0][:, 0:NT * E], tri[:], both[:].rearrange("p t e -> p (t e)"), start=True, stop=True)
            pe.matmul(hp[1][:, 0:NT * E], all_ones[:], both[:].rearrange("p t e -> p (t e)"), start=True, stop=True).then_inc(s_rm, 1)

            def up_product(u, wu, f, read):
                pe.wait_ge(s_hhi, read)
                n = 0
                for k in range(KD):
                    for wp, xp in ((0, 0), (0, 1), (1, 0)):
                        last = pe.matmul(hp[f % 4][:], up[wu][:, wp, k * F + f * P:k * F + (f + 1) * P], xT[u][:, xp, k],
                                         start=n == 0, stop=n == 3 * KD - 1)
                        n += 1
                last.then_inc(s_up, 1)

            def down_product(T, wu, f, r):
                pe.wait_ge(s_hlo, FT * T + f + 1)
                if f == 0:
                    pe.wait_ge(s_y, T)
                    if r is not None:
                        pe.wait_ge(s_wlo, FT * (r + 2))
                hs = hid_split[f % 4]
                for t in range(QT):
                    for n, (hpart, wp) in enumerate(((0, 0), (1, 0), (0, 1))):
                        last = pe.matmul(yp[:, t], hs[:, hpart, t * P:(t + 1) * P], down[wu][:, wp, f * D:(f + 1) * D],
                                         start=f == 0 and n == 0 and t % 2 == 0, stop=f == FT - 1 and n == 2, skip_group_check=True)
                last.then_inc(s_dn, 1)

            def transpose_rows(r, u, k):
                pe.wait_ge(s_rows[u], 16 * (k + 1))
                pe.wait_ge(s_xlo, r)
                for kd in range(KD):
                    for q in range(QT):
                        last = pe.transpose(tp[kd][:, q], rows[u][:, q, kd * P:(kd + 1) * P], ident[:])
                last.then_inc(s_tr, 1)

            pe.wait_ge(s_r, R_READ)
            pe.wait_ge(s_wlo, FT)
            pe.wait_ge(s_shT[0], 16)
            for f in range(2):
                up_product(0, 0, f, 0)

            def body(T, u, r, nxt, n, k):
                wu = 0 if r is None else 1 - u
                for f in range(2, FT):
                    up_product(u, wu, f, FT * T + max(f - 3, 0))
                    down_product(T, wu, f - 2, r)
                    if f == 4 and nxt == "routed":
                        transpose_rows(n, 1 - u, k)
                if nxt == "shared":
                    pe.wait_ge(s_shT[1 - u], 16 * k + 16)
                elif nxt == "routed":
                    pe.wait_ge(s_xlo, n + 1)
                    pe.wait_ge(s_wlo, FT * (n + 1) + FT // 2)
                for f in range(2):
                    if nxt is not None:
                        up_product(1 - u, 0 if nxt == "shared" else u, f, FT * (T + 1) + f - 3)
                    down_product(T, wu, FT - 2 + f, r)

            tiles(pe, body)

        @block.scalar
        def _(act):
            act.wait_ge(s_r, R_MAXED)
            act.activation(probs[:], probs[:], ACT.Exp).then_inc(s_re, 1)

            def weight_chunk(u, wu, f):
                n, q = f // 4, f % 4
                act.activation((up, down)[n][wu][:, 0, 512 * q:512 * q + 512], raw[u][n][:, 512 * q:512 * q + 512],
                               ACT.Copy).then_inc(s_whi, 1)

            def hidden(g, f):
                act.wait_ge(s_up, g + 1)
                act.activation(hid[f % 2][:], hp[f % 4][:], ACT.Gelu)
                act.activation(hid_split[f % 4][:, 0], hp[f % 4][:], ACT.Gelu).then_inc(s_hhi, 1)

            act.wait_ge(s_raw[0], 32)
            for f in range(FT):
                weight_chunk(0, 0, f)
            for f in range(2):
                hidden(f, f)

            def body(T, u, r, nxt, n, k):
                for f in range(2, FT + (0 if nxt is None else 2)):
                    act.wait_ge(s_hlo, FT * T + f - 1)
                    act.wait_ge(s_dn, FT * T + max(f - 3, 0))
                    hidden(FT * T + f, f % FT)
                    if nxt == "routed":
                        if f == 2:
                            act.wait_ge(s_dn, FT * T)
                            act.wait_ge(s_raw[1 - u], 32 * k + (64 if u == 1 else 32))
                        weight_chunk(1 - u, u, f - 2)
                if r is not None:
                    act.wait_ge(s_dn, FT * T + FT)
                    act.wait_ge(s_yout, 16 * r)
                    act.activation(y_sb[:], yp[:], ACT.Copy).then_inc(s_y, 1)

            tiles(act, body)

        @block.vector
        def _(v):
            step = [0]

            def then(ins):
                step[0] += 1
                ins.then_inc(s_r, 1)
                v.wait_ge(s_r, step[0])

            v.wait_ge(s_const, 1)

            def over_e(ap):
                return ap.unsqueeze(2).broadcast_to((P, NT, E))

            then(v.tensor_reduce(mx[:], logits[:], AX.X, ALU.max))
            then(v.tensor_tensor(probs[:], logits[:], over_e(mx[:]), ALU.subtract))
            assert step[0] == R_MAXED
            v.wait_ge(s_re, 1)
            then(v.tensor_reduce(tot[:], probs[:], AX.X, ALU.add))
            then(v.reciprocal(rtot[:], tot[:]))
            then(v.tensor_tensor(probs[:], probs[:], over_e(rtot[:]), ALU.mult))
            mine = probs[:].unsqueeze(3).broadcast_to((P, NT, E, E))
            other = probs[:].unsqueeze(2).broadcast_to((P, NT, E, E))
            v.tensor_tensor(pair_big, other, mine, ALU.is_gt)
            then(v.tensor_tensor(eq_big, other, mine, ALU.is_equal))
            then(v.tensor_tensor(eq_big, eq_big, before[:].unsqueeze(1).broadcast_to((P, NT, E, E)), ALU.mult))
            then(v.tensor_tensor(pair_big, pair_big, eq_big, ALU.add))
            then(v.tensor_reduce(rank[:], pair_big, AX.X, ALU.add))
            v.tensor_scalar(sel0[:], rank[:], 0.0, None, ALU.is_equal)
            v.tensor_scalar(sel1[:], rank[:], 1.0, None, ALU.is_equal)
            then(v.tensor_scalar(both[:], rank[:], 2.0, None, ALU.is_lt))
            assert step[0] == R_BOTH
            for n, s in enumerate((sel0, sel1)):
                then(v.tensor_tensor(tmp[:], s[:], probs[:], ALU.mult))
                then(v.tensor_reduce(gate[n][:], tmp[:], AX.X, ALU.add))
            v.wait_ge(s_rm, 1)
            counts = hp[1][:, 0:NT * E].rearrange("p (t e) -> p e t", e=E)
            then(v.tensor_copy(counts_et[:], counts))
            flat = "p e t -> p (e t)"
            then(v.tensor_tensor_scan(run[:].rearrange(flat), ones_e[:], counts_et[:].rearrange(flat), 0.0, ALU.mult, ALU.add))
            v.tensor_copy(count[:, 0:1], run[:, 0, NT - 1:NT])
            then(v.tensor_tensor(count[:, 1:E], run[:, 1:E, NT - 1], run[:, 0:E - 1, NT - 1], ALU.subtract))
            cmp = tmp[:, 0:E]
            then(v.tensor_tensor(cmp, count[:].unsqueeze(2).broadcast_to((P, E, E)), steps_n[:], ALU.is_gt))
            then(v.tensor_reduce(n_tiles[:], cmp, AX.X, ALU.add))
            then(v.tensor_tensor_scan(ends[:], ones_e[:, 0:E], n_tiles[:], 0.0, ALU.mult, ALU.add))
            then(v.tensor_tensor(base[:], ends[:], n_tiles[:], ALU.subtract))
            then(v.tensor_scalar(base[:], base[:], float(N), None, ALU.mult))
            then(v.tensor_tensor(base[:, 1:E], base[:, 1:E], run[:, 0:E - 1, NT - 1], ALU.subtract))
            then(v.tensor_tensor(run[:], run[:], counts_et[:], ALU.subtract))
            then(v.tensor_tensor(run[:], run[:], base[:].unsqueeze(2).broadcast_to((P, E, NT)), ALU.add))
            then(v.tensor_tensor(pos[:], hp[0][:, 0:NT * E].rearrange("p (t e) -> p t e", e=E),
                                 run[:].rearrange("p e t -> p t e"), ALU.add))
            assert step[0] == R_READ
            for n, s in enumerate((sel0, sel1)):
                then(v.tensor_tensor(tmp[:], s[:], pos[:], ALU.mult))
                then(v.tensor_reduce(posf[:], tmp[:], AX.X, ALU.add))
                then(v.tensor_copy(idx[n][:], posf[:]))
            te = rank[:].rearrange("p t e -> p (t e)")[:, 0:TILES * (E - 1)].rearrange("p (t e) -> p t e", e=E - 1)
            then(v.tensor_tensor(te, ends[:, 0:E - 1].unsqueeze(1).broadcast_to((P, TILES, E - 1)), tile_no[:], ALU.is_le))
            then(v.tensor_reduce(tile_e[:], te, AX.X, ALU.add))
            v.tensor_copy(tile_ei[:], tile_e[:]).then_inc(s_idx, 1)

            def weight_chunk(u, wu, f, at):
                n, q = f // 4, f % 4
                v.wait_ge(s_whi, at + f + 1)
                dst = (up, down)[n][wu]
                v.tensor_tensor(dst[:, 1, 512 * q:512 * q + 512], raw[u][n][:, 512 * q:512 * q + 512],
                                dst[:, 0, 512 * q:512 * q + 512].bitcast(F32), ALU.subtract).then_inc(s_wlo, 1)

            def hidden(g, f):
                v.wait_ge(s_hhi, g + 1)
                v.tensor_tensor(hid_split[f % 4][:, 1], hid[f % 2][:], hid_split[f % 4][:, 0].bitcast(F32),
                                ALU.subtract).then_inc(s_hlo, 1)

            def split_rows(r, u, T):
                v.wait_ge(s_tr, r + 1)
                v.wait_ge(s_up, FT * T)
                for k in range(KD):
                    last = v.tensor_copy(xT[u][:, 0, k], tp[k][:].rearrange("p a b -> p (a b)"))
                last.then_inc(s_xhi, 1)
                v.wait_ge(s_xhi, r + 1)
                for k in range(KD):
                    last = v.tensor_tensor(xT[u][:, 1, k], tp[k][:].rearrange("p a b -> p (a b)"),
                                           xT[u][:, 0, k].bitcast(F32), ALU.subtract)
                last.then_inc(s_xlo, 1)

            for f in range(FT):
                weight_chunk(0, 0, f, 0)
            for f in range(2):
                hidden(f, f)

            def body(T, u, r, nxt, n, k):
                for f in range(2, FT + (0 if nxt is None else 2)):
                    hidden(FT * T + f, f % FT)
                    if nxt == "routed":
                        weight_chunk(1 - u, u, f - 2, FT * (n + 1))
                        if f == 6:
                            split_rows(n, 1 - u, T)
                if r is None:
                    v.wait_ge(s_dn, FT * T + FT)
                    part = acc[:, bass.ds(T * QT, QT)]
                    v.tensor_tensor(part, yp[:], part, ALU.add).then_inc(s_y, 1)

            tiles(v, body)
            for b in range(B):
                i = b % 2
                v.wait_ge(s_gat[i], 16 * 2 * QT * (b // 2 + 1))
                if b == 0:
                    v.wait_ge(s_y, B + TILES)
                for n in range(2):
                    for t in range(QT):
                        q = b * QT + t
                        last = v.scalar_tensor_tensor(acc[:, q], gat[i][n][:, t], gate[n][:, q:q + 1], acc[:, q], ALU.mult, ALU.add)
                    if n == 0:
                        last.then_inc(s_half, 1)
                        v.wait_ge(s_half, b + 1)
                last.then_inc(s_comb, 1)


R_MAXED = 2
R_BOTH = 10
R_READ = 26


def build(nc, x, ctx_1024, cos, sin, lat_g, lat_b, ctx_g, ctx_b, Wq, Wkv, Wo, bo,
          shared_up, shared_down, routed_up, routed_down, router_w, out):
    sh = Shapes(x, ctx_1024, cos, Wq, routed_up)
    KD, PAIRS, B, N, D = sh.KD, sh.PAIRS, sh.B, sh.N, sh.D

    def dram(name, shape):
        return nc.dram_tensor(name, shape, F32, kind="Internal").ap()

    wpack = dram("wpack", (PAIRS + 2, P, 3 * 2 * KD * P))
    ctxT = dram("ctx_parts", (B + 1, P, 2 * KD * sh.S))
    latT = dram("lat_parts", (B + 1, P, 2 * KD * N))
    x1 = dram("attended", (B, N, D))
    xn_d = dram("normed", (B, N, D))
    xnT = dram("normedT", (B, P, 2 * KD * N))
    xs = dram("sorted_rows", (sh.TILES, N, D))
    ys = dram("sorted_results", (sh.TILES, N, D))
    with ExitStack() as es:
        def sb(name, shape, dt=F32):
            return es.enter_context(nc.sbuf_tensor(name, shape, dt))

        ident = sb("ident", [P, P])
        with ExitStack() as es1:
            def sb1(name, shape, dt=F32):
                return es1.enter_context(nc.sbuf_tensor(name, shape, dt))

            keep = dict(ident=ident, cosT=sb1("cosT", [P, sh.S]), sinT=sb1("sinT", [P, sh.S]),
                        wo_hi=sb1("wo_hi", [P, PAIRS, D], F32R), wo_lo=sb1("wo_lo", [P, PAIRS, D], F32R),
                        sel=sb1("sel", [P, P]), ones=sb1("ones", [P, 32]), zero=sb1("zero", [P, ZERO]))
            prepare(nc, sh, x, ctx_1024, cos, sin, lat_g, lat_b, ctx_g, ctx_b, Wq, Wkv, Wo, wpack, ctxT, latT, keep)
            attend(nc, sh, x, bo, wpack, ctxT, latT, x1, xs, keep)
        ffn = dict(ident=ident, acc=sb("acc", [P, B * sh.QT, D]), logits=sb("logits", [P, B * sh.QT, sh.E]))
        normalise_tokens(nc, sh, x1, router_w, xn_d, xnT, ffn)
        experts(nc, sh, xn_d, xnT, xs, ys, shared_up, shared_down, routed_up, routed_down, out, ffn)


_INS = ["x", "ctx_1024", "L0_xattn_cos", "L0_xattn_sin", "L0_xattn_ln_lat_g", "L0_xattn_ln_lat_b",
        "L0_xattn_ln_ctx_g", "L0_xattn_ln_ctx_b", "L0_xattn_Wq", "L0_xattn_Wkv", "L0_xattn_Wo", "L0_xattn_bo",
        "L0_ffn_shared_up", "L0_ffn_shared_down", "L0_ffn_routed_up", "L0_ffn_routed_down", "L0_ffn_router_w"]


def kernel(**inputs):
    import numpy as np
    import concourse.bacc as bacc
    from concourse.bass_utils import run_bass_kernel_spmd

    nc = bacc.Bacc("TRN2", target_bir_lowering=False, num_devices=1)
    arrays, args = {}, []
    for name in _INS:
        a = np.ascontiguousarray(inputs[name])
        arrays[name] = a
        args.append(nc.dram_tensor(name, a.shape, mybir.dt.from_np(a.dtype), kind="ExternalInput").ap())
    out = nc.dram_tensor("out", inputs["x"].shape, F32, kind="ExternalOutput").ap()
    build(nc, *args, out)
    return run_bass_kernel_spmd(nc, [arrays], core_ids=[0]).results[0]["out"]
```

```python
from contextlib import ExitStack

import concourse.bass as bass
from concourse import mybir

F32 = mybir.dt.float32
F32R = mybir.dt.float32r
I32 = mybir.dt.int32
U32 = mybir.dt.uint32
ALU = mybir.AluOpType
ACT = mybir.ActivationFunctionType
AX = mybir.AxisListType

P = 128
ZERO = 1472
EPS = 1e-5
CLIP = 11.0
EXP_HI = 59874.141715197816
EXP_LO = 1.670170079024566e-05


class Shapes:

    def __init__(self, x, ctx, cos, Wq, routed_up):
        self.B, self.N, self.D = x.shape
        self.S = ctx.shape[1]
        self.HD = 2 * cos.shape[1]
        self.INNER = Wq.shape[1]
        self.PAIRS = self.INNER // P
        self.KD = self.D // P
        self.QT = self.N // P
        self.KT = self.S // P
        self.E = routed_up.shape[0]
        self.F = routed_up.shape[2]
        self.TILES = (2 * self.B * self.N + self.E * (self.N - 1)) // self.N
        assert 2 * self.HD == P and self.KD == 2 and self.N == 512 and self.KT == 8 and self.PAIRS == 8


def prepare(nc, sh, x, ctx_in, cos, sin, lat_g, lat_b, ctx_g, ctx_b, Wq, Wkv, Wo, wpack, ctxT, latT, keep):
    KD, KT, QT, PAIRS, D, B = sh.KD, sh.KT, sh.QT, sh.PAIRS, sh.D, sh.B
    with ExitStack() as es:
        def sb(name, shape, dt=F32):
            return es.enter_context(nc.sbuf_tensor(name, shape, dt))

        def ps(name, shape, dt=F32):
            return es.enter_context(nc.psum_tensor(name, shape, dt))

        def sem(name):
            return es.enter_context(nc.semaphore(name))

        ident, cosT, sinT, wo, ones = keep["ident"], keep["cosT"], keep["sinT"], keep["wo"], keep["ones"]

        w_raw = sb("w_raw", [P, KD, 3 * sh.INNER])
        w_split = sb("w_split", [P, PAIRS, 3, 2, KD, P], F32R)
        trig = sb("trig", [P, 2, KT, sh.HD // 2])
        trig4 = sb("trig4", [P, 2, KT, 4, sh.HD // 2])
        gb = sb("gb", [P, 4, KD])
        neg_half = sb("neg_half", [P, KT])
        T = [dict(
            ctx=sb(f"ctx{i}", [P, KT, D]), x=sb(f"x{i}", [P, QT, D]), xn=sb(f"xn{i}", [P, QT, D]),
            stats=sb(f"stats{i}", [P, KT, 6]), mv=sb(f"mv{i}", [P, KT, 2]), r=sb(f"r{i}", [P, KT]),
            xstats=sb(f"xstats{i}", [P, QT, 6]), xmv=sb(f"xmv{i}", [P, QT, 2]), xr=sb(f"xr{i}", [P, QT]),
            ve=sb(f"ve{i}", [P, KT]), xve=sb(f"xve{i}", [P, QT]),
            full=sb(f"full{i}", [P, KD, sh.S]), xfull=sb(f"xfull{i}", [P, KD, sh.N]),
        ) for i in range(2)]
        ctx_split = sb("ctx_split", [P, 2, KD, sh.S], F32R)
        lat_split = sb("lat_split", [P, 2, KD, sh.N], F32R)
        tp = [ps(f"tp{i}", [P, 4, P]) for i in range(8)]

        s_w = sem("s_w")
        s_const = sem("s_const")
        s_cc = sem("s_cc")
        s_trig4 = sem("s_trig4")
        s_hi = sem("s_hi")
        s_lo = sem("s_lo")
        s_wout = sem("s_wout")
        s_tabT = sem("s_tabT")
        s_tab = sem("s_tab")
        s_cin, s_xin = [sem(f"s_cin{i}") for i in range(2)], [sem(f"s_xin{i}") for i in range(2)]
        s_cstat, s_cvar, s_crstd, s_cnorm = sem("s_cstat"), sem("s_cvar"), sem("s_crstd"), sem("s_cnorm")
        s_xstat, s_xvar, s_xrstd, s_xnorm = sem("s_xstat"), sem("s_xvar"), sem("s_xrstd"), sem("s_xnorm")
        s_ctr, s_xtr = sem("s_ctr"), sem("s_xtr")
        s_cfull, s_xfull = sem("s_cfull"), sem("s_xfull")
        s_chi, s_clo, s_xhi, s_xlo = sem("s_chi"), sem("s_clo"), sem("s_xhi"), sem("s_xlo")
        s_cout, s_xout = sem("s_cout"), sem("s_xout")

        NW = 4 + 4 + 2
        block = es.enter_context(nc.Block())

        def rows(ap, b):
            return ap[b].rearrange("(p t) d -> p t d", p=P)

        @block.sync
        def _(sp):
            for n, ap in enumerate((ctx_in, x)):
                for i in range(2):
                    sp.dma_start((T[i]["ctx"] if n == 0 else T[i]["x"])[:], rows(ap, i)).then_inc((s_cin, s_xin)[n][i], 16)
            w3 = w_raw[:].rearrange("p k (t n) -> p k t n", t=3)
            sp.dma_start(w3[:, :, 0], Wkv[:, 0:sh.INNER].rearrange("(k p) n -> p k n", p=P)).then_inc(s_w, 16)
            sp.dma_start(w3[:, :, 2], Wkv[:, sh.INNER:2 * sh.INNER].rearrange("(k p) n -> p k n", p=P)).then_inc(s_w, 16)
            sp.dma_start(w3[:, :, 1], Wq.rearrange("(k p) n -> p k n", p=P)).then_inc(s_w, 16)
            sp.dma_start(wo[:], Wo.rearrange("(c p) n -> p c n", p=P)).then_inc(s_w, 16)
            with nc.allow_non_contiguous_dma(reason="four vectors of 256 values"):
                for n, ap in enumerate((ctx_g, ctx_b, lat_g, lat_b)):
                    sp.dma_start(gb[:, n], ap.rearrange("(k p) -> p k", p=P)).then_inc(s_w, 16)
            for n, ap in enumerate((cos, sin)):
                sp.dma_start(trig[:, n], ap.rearrange("(p t) d -> p t d", p=P)).then_inc(s_w, 16)
            sp.wait_ge(s_lo, 1)
            sp.dma_start(wpack.rearrange("c p n -> p c n"),
                         w_split[:].rearrange("p c a b k n -> p c (a b k n)").bitcast(F32)).then_inc(s_wout, 16)
            with sp.Fori(0, B // 2) as h:
                for i in range(2):
                    b = h * 2 + i
                    sp.wait_ge(s_clo, b + 1)
                    sp.dma_start(ctxT[b], ctx_split[:].rearrange("p a k n -> p (a k n)").bitcast(F32)).then_inc(s_cout, 16)
                    sp.wait_ge(s_xlo, b + 1)
                    sp.dma_start(latT[b], lat_split[:].rearrange("p a k n -> p (a k n)").bitcast(F32)).then_inc(s_xout, 16)
                    nxt = (b + 2) % B
                    sp.wait_ge(s_ctr, 4 * b + 4)
                    sp.dma_start(T[i]["ctx"][:], rows(ctx_in, nxt)).then_inc(s_cin[i], 16)
                    sp.wait_ge(s_xtr, 2 * b + 2)
                    sp.dma_start(T[i]["x"][:], rows(x, nxt)).then_inc(s_xin[i], 16)
            sp.dma_start(ctxT[B], ctx_split[:].rearrange("p a k n -> p (a k n)").bitcast(F32)).then_inc(s_cout, 16)
            sp.dma_start(latT[B], lat_split[:].rearrange("p a k n -> p (a k n)").bitcast(F32)).then_inc(s_xout, 16)
            for s, n in ((s_wout, 1), (s_cout, B + 1), (s_xout, B + 1),
                         (s_cin[0], B // 2 + 1), (s_cin[1], B // 2 + 1), (s_xin[0], B // 2 + 1), (s_xin[1], B // 2 + 1)):
                sp.wait_ge(s, 16 * n)

        @block.gpsimd
        def _(pool):
            pool.memset(ident[:], 0.0).then_inc(s_cc, 1)
            pool.memset(neg_half[:], -0.5)
            pool.memset(ones[:], 1.0)
            pool.wait_ge(s_cc, 1)
            pool.affine_select(out=ident[:], in_=ident[:], compare_op=ALU.not_equal, fill=1.0, base=0,
                               pattern=[[-1, P]], channel_multiplier=1).then_inc(s_cc, 1)
            pool.wait_ge(s_cc, 2)
            pool.memset(keep["zero"][:], 0.0).then_inc(s_const, 1)
            with pool.Fori(0, B // 2) as h:
                for i in range(2):
                    b = h * 2 + i
                    t = T[i]
                    pool.wait_ge(s_cvar, b + 1)
                    pool.tensor_tensor(t["r"][:], t["ve"][:], neg_half[:], ALU.pow).then_inc(s_crstd, 1)
                    for n in range(2):
                        pool.wait_ge(s_xvar, 2 * b + 1 + n)
                        pool.tensor_tensor(t["xr"][:], t["xve"][:], neg_half[:, 0:QT], ALU.pow).then_inc(s_xrstd, 1)

        @block.vector
        def _(v):
            v.wait_ge(s_w, 16 * NW)
            half = sh.HD // 2
            for n in range(2):
                for r in range(4):
                    sign = -1.0 if n == 1 and r % 2 == 0 else 1.0
                    last = v.tensor_scalar(trig4[:, n, :, r], trig[:, n], sign, None, ALU.mult)
            last.then_inc(s_trig4, 1)
            w4 = w_raw[:].rearrange("p k (t c n) -> p t k c n", t=3, n=P)
            for t in range(3):
                for k in range(KD):
                    last = v.tensor_copy(w_split[:, :, t, 0, k], w4[:, t, k])
            last.then_inc(s_hi, 1)
            v.wait_ge(s_hi, 1)
            for t in range(3):
                for k in range(KD):
                    last = v.tensor_tensor(w_split[:, :, t, 1, k], w4[:, t, k],
                                           w_split[:, :, t, 0, k].bitcast(F32), ALU.subtract)
            last.then_inc(s_lo, 1)

            def stats(src, st, mv, ve, tiles, s_stat, s_var, at):
                for t in range(tiles):
                    last = v.bn_stats(st[:, t], src[:, t])
                last.then_inc(s_stat, 1)
                v.wait_ge(s_stat, 2 * at + 1)
                v.memset(ve[:], EPS)
                for t in range(tiles):
                    last = v.bn_aggr(mv[:, t], st[:, t])
                last.then_inc(s_stat, 1)
                v.wait_ge(s_stat, 2 * at + 2)
                v.tensor_tensor(ve[:], mv[:, :, 1], ve[:], ALU.add).then_inc(s_var, 1)

            def apply(dst, src, mv, r, tiles, s_norm):
                for t in range(tiles):
                    last = v.tensor_scalar(dst[:, t], src[:, t], mv[:, t, 0:1], r[:, t:t + 1], ALU.subtract, ALU.mult)
                last.then_inc(s_norm, 1)

            with v.Fori(0, B // 2) as h:
                for i in range(2):
                    b = h * 2 + i
                    t = T[i]
                    v.wait_ge(s_cin[i], 16 * h + 16)
                    stats(t["ctx"], t["stats"], t["mv"], t["ve"], KT, s_cstat, s_cvar, b)
                    v.wait_ge(s_xin[i], 16 * h + 16)
                    stats(t["x"], t["xstats"], t["xmv"], t["xve"], QT, s_xstat, s_xvar, 2 * b)
                    v.wait_ge(s_crstd, b + 1)
                    apply(t["ctx"], t["ctx"], t["mv"], t["r"], KT, s_cnorm)
                    v.wait_ge(s_xrstd, 2 * b + 1)
                    apply(t["xn"], t["x"], t["xmv"], t["xr"], QT, s_xnorm)
                    v.wait_ge(s_xnorm, 2 * b + 1)
                    stats(t["xn"], t["xstats"], t["xmv"], t["xve"], QT, s_xstat, s_xvar, 2 * b + 1)
                    v.wait_ge(s_cfull, 4 * b + 4)
                    v.wait_ge(s_cout, 16 * b)
                    v.tensor_copy(ctx_split[:, 0], t["full"][:]).then_inc(s_chi, 1)
                    v.wait_ge(s_xrstd, 2 * b + 2)
                    apply(t["x"], t["xn"], t["xmv"], t["xr"], QT, s_xnorm)
                    v.wait_ge(s_chi, b + 1)
                    v.tensor_tensor(ctx_split[:, 1], t["full"][:], ctx_split[:, 0].bitcast(F32), ALU.subtract).then_inc(s_clo, 1)
                    v.wait_ge(s_xfull, 2 * b + 2)
                    v.wait_ge(s_xout, 16 * b)
                    v.tensor_copy(lat_split[:, 0], t["xfull"][:]).then_inc(s_xhi, 1)
                    v.wait_ge(s_xhi, b + 1)
                    v.tensor_tensor(lat_split[:, 1], t["xfull"][:], lat_split[:, 0].bitcast(F32), ALU.subtract).then_inc(s_xlo, 1)

        @block.tensor
        def _(pe):
            pe.wait_ge(s_const, 1)
            pe.wait_ge(s_trig4, 1)
            for n in range(2):
                for k in range(KT):
                    last = pe.transpose(tp[2 * n + k // 4][:, k % 4], trig4[:, n, k].rearrange("p r d -> p (r d)"), ident[:])
            last.then_inc(s_tabT, 1)
            pe.wait_ge(s_tab, 1)
            with pe.Fori(0, B // 2) as h:
                for i in range(2):
                    b = h * 2 + i
                    t = T[i]
                    pe.wait_ge(s_cnorm, b + 1)
                    pe.wait_ge(s_cfull, 4 * b)
                    for k in range(KD):
                        for half in range(2):
                            for j in range(4):
                                last = pe.transpose(tp[2 * k + half][:, j], t["ctx"][:, 4 * half + j, k * P:(k + 1) * P], ident[:])
                            last.then_inc(s_ctr, 1)
                    pe.wait_ge(s_xnorm, 2 * b + 2)
                    pe.wait_ge(s_xfull, 2 * b)
                    for k in range(KD):
                        for j in range(4):
                            last = pe.transpose(tp[4 + k][:, j], t["x"][:, j, k * P:(k + 1) * P], ident[:])
                        last.then_inc(s_xtr, 1)

        @block.scalar
        def _(act):
            act.wait_ge(s_tabT, 1)
            for n, dst in enumerate((cosT, sinT)):
                for k in range(2):
                    last = act.activation(dst[:, 512 * k:512 * k + 512], tp[2 * n + k][:].rearrange("p a b -> p (a b)"), ACT.Copy)
            last.then_inc(s_tab, 1)
            act.wait_ge(s_w, 16 * NW)
            with act.Fori(0, B // 2) as h:
                for i in range(2):
                    b = h * 2 + i
                    t = T[i]
                    act.wait_ge(s_clo, b)
                    for k in range(KD):
                        for half in range(2):
                            act.wait_ge(s_ctr, 4 * b + 2 * k + half + 1)
                            act.activation(t["full"][:, k, 512 * half:512 * half + 512],
                                           tp[2 * k + half][:].rearrange("p a b -> p (a b)"), ACT.Identity,
                                           bias=gb[:, 1, k:k + 1], scale=gb[:, 0, k:k + 1]).then_inc(s_cfull, 1)
                    act.wait_ge(s_xlo, b)
                    for k in range(KD):
                        act.wait_ge(s_xtr, 2 * b + k + 1)
                        act.activation(t["xfull"][:, k], tp[4 + k][:].rearrange("p a b -> p (a b)"), ACT.Identity,
                                       bias=gb[:, 3, k:k + 1], scale=gb[:, 2, k:k + 1]).then_inc(s_xfull, 1)


def attend(nc, sh, x, bo, wpack, ctxT, latT, x1, xs, keep):
    KD, KT, QT, PAIRS, D, B, N, S, HD = sh.KD, sh.KT, sh.QT, sh.PAIRS, sh.D, sh.B, sh.N, sh.S, sh.HD
    with ExitStack() as es:
        def sb(name, shape, dt=F32):
            return es.enter_context(nc.sbuf_tensor(name, shape, dt))

        def ps(name, shape, dt=F32):
            return es.enter_context(nc.psum_tensor(name, shape, dt))

        def sem(name):
            return es.enter_context(nc.semaphore(name))

        cosT, sinT, wo, ones = keep["cosT"], keep["sinT"], keep["wo"], keep["ones"]
        STEPS = KT
        PROBS = 4
        DUOS = PAIRS // 2
        VBANKS = KT // 2

        USES = (("k", 0), ("k", 1), ("v", 0), ("v", 1), ("q", 0))
        USE_STEP = (0, 1, 2, 3, 5)
        FIRST = 2 * 3 + VBANKS
        BATCH_USES = PAIRS * len(USES) + 2
        assert BATCH_USES % 2 == 0

        def uses_before(b, p):
            return b * BATCH_USES + (FIRST + len(USES) * p)

        def bank(p, i):
            return (FIRST + len(USES) * p + i) % 2

        w = [sb(f"w{i}", [P, 2, 2, KD, P], F32R) for i in range(2)]
        wv = sb("wv", [P, DUOS, 2, KD, 2 * P], F32R)
        HS = S // 2
        ctxs = [sb(f"ctxs{i}", [P, 2, KD, HS], F32R) for i in range(2)]
        lats = sb("lats", [P, 2, KD, N], F32R)
        kT = sb("kT", [P, S])
        kT_swap = sb("kT_swap", [P, S])
        k_rope = sb("k_rope", [P, S])
        k_split = sb("k_split", [P, 2, S], F32R)
        k_st = [sb(f"k_st{i}", [P, 2, S], F32R) for i in range(2)]
        v_nat = [sb(f"v_nat{i}", [P, KT, 2 * P]) for i in range(2)]
        qT = sb("qT", [P, N])
        q_split = sb("q_split", [P, 2, N], F32R)
        q_st = [sb(f"q_st{i}", [P, 2, 2, N], F32R) for i in range(2)]
        probs = [sb(f"probs{i}", [P, 2, N]) for i in range(PROBS)]
        p_sum = sb("p_sum", [P, 2, N])
        u_sb = sb("u_sb", [P, N])
        rden = sb("rden", [P, N])
        o = sb("o", [P, PAIRS, N])
        x_in = sb("x_in", [P, QT, D])
        x_out = sb("x_out", [P, QT, D])
        bo_bc = sb("bo_bc", [P, D])

        scores = [ps(f"scores{i}", [P, 2, N]) for i in range(2)]
        pv_ps = ps("pv_ps", [P, N])
        den_ps = ps("den_ps", [P, N])
        proj = [ps(f"proj{i}", [P, N]) for i in range(2)]

        s_w = [sem(f"s_w1{i}") for i in range(2)]
        s_wv = sem("s_wv")
        s_ctx, s_lat = [sem(f"s_ctx{i}") for i in range(2)], sem("s_lat")
        s_xin = sem("s_xin")
        s_bo = sem("s_bo")
        s_proj = sem("s_proj")
        s_projout = sem("s_projout")
        s_swap = sem("s_swap")
        s_cos, s_sin = sem("s_cos"), sem("s_sin")
        s_rope = sem("s_rope")
        s_khi, s_klo = sem("s_khi"), sem("s_klo")
        s_kst = sem("s_kst")
        s_qhi, s_qlo = sem("s_qhi"), sem("s_qlo")
        s_qst = sem("s_qst")
        s_scores = sem("s_scores")
        s_exp = sem("s_exp")
        s_clip = sem("s_clip")
        s_pv = sem("s_pv")
        s_add = sem("s_add")
        s_u = sem("s_u")
        s_den = sem("s_den")
        s_rden = sem("s_rden")
        s_o = sem("s_o")
        s_bias = sem("s_bias")
        s_x1 = sem("s_x1")
        s_out = sem("s_out")
        s_zero = sem("s_zero")

        block = es.enter_context(nc.Block())

        def batches(eng, slot, tail):
            with eng.Fori(0, B) as b:
                for p in range(PAIRS):
                    slot(b, p)
                tail(b)

        @block.sync
        def _(sp):
            def load_w(p, i):
                sp.dma_start(w[i][:].rearrange("p a b k n -> p (a b k n)").bitcast(F32),
                             wpack[p, :, 0:4 * KD * P]).then_inc(s_w[i], 16)

            def load_ctx(b, half):
                src = ctxT[b].rearrange("p (a k n) -> p a k n", a=2, k=KD)[:, :, :, HS * half:HS * half + HS]
                sp.dma_start(ctxs[half][:].bitcast(F32), src).then_inc(s_ctx[half], 16)

            def load_lat(b):
                sp.dma_start(lats[:].rearrange("p a k n -> p (a k n)").bitcast(F32), latT[b]).then_inc(s_lat, 16)

            def exchange():
                for q in range(4):
                    sp.dma_start(kT_swap[32 * q:32 * q + 32], kT[32 * (q ^ 1):32 * (q ^ 1) + 32]).then_inc(s_swap, 16)

            def stack_k(i):
                for head in range(2):
                    for part in range(2):
                        sp.dma_start(k_st[i][64 * part:64 * part + 64, head].bitcast(F32),
                                     k_split[64 * head:64 * head + 64, part].bitcast(F32)).then_inc(s_kst, 16)

            def stack_q(i):
                for head in range(2):
                    for twice in range(2):
                        sp.dma_start(q_st[i][64 * twice:64 * twice + 64, head].bitcast(F32),
                                     q_split[64 * head:64 * head + 64].bitcast(F32)).then_inc(s_qst, 16)

            load_w(0, 0)
            load_ctx(0, 0)
            load_ctx(0, 1)
            load_lat(0)
            load_w(1, 1)
            for p in range(PAIRS):
                half = slice(P * (p % 2), P * (p % 2) + P)
                sp.dma_start(wv[:, p // 2, :, :, half].bitcast(F32),
                             wpack[p, :, 4 * KD * P:].rearrange("p (a k n) -> p a k n", a=2, k=KD)).then_inc(s_wv, 16)
            with nc.allow_non_contiguous_dma(reason="one row to all partitions"):
                sp.dma_start(bo_bc[:], bo.rearrange("(a n) -> a n", a=1).broadcast_to((P, D))).then_inc(s_bo, 16)
            for i in range(2):
                sp.wait_ge(s_projout, 3 * i + 2)
                exchange()
                sp.wait_ge(s_proj, 3 * i + 3)
                load_w(2 + i, i)
                sp.wait_ge(s_qlo, i + 1)
                stack_q(i)
                sp.wait_ge(s_klo, i + 1)
                stack_k(i)

            def slot(b, p):
                sp.wait_ge(s_projout, uses_before(b, p) + 2)
                exchange()
                if p == PAIRS - 3:
                    load_ctx(b + 1, 0)
                    sp.wait_ge(s_proj, uses_before(b, p) + 4)
                    load_ctx(b + 1, 1)
                sp.wait_ge(s_proj, uses_before(b, p) + 5)
                load_w((p + 4) % PAIRS, p % 2)
                if p == PAIRS - 3:
                    load_lat(b + 1)
                sp.wait_ge(s_klo, b * PAIRS + (p + 3))
                stack_k(p % 2)
                sp.wait_ge(s_qlo, b * PAIRS + (p + 3))
                stack_q(p % 2)
                if p == 0:
                    sp.dma_start(x_in[:], x[b].rearrange("(p t) d -> p t d", p=P)).then_inc(s_xin, 16)

            def tail(b):
                sp.wait_ge(s_x1, b + 1)
                sp.dma_start(x1[b].rearrange("(p t) d -> p t d", p=P), x_out[:]).then_inc(s_out, 16)

            batches(sp, slot, tail)
            sp.wait_ge(s_out, 16 * B)
            sp.wait_ge(s_lat, 16 * (B + 1))
            sp.wait_ge(s_kst, 64 * (B * PAIRS + 2))
            sp.wait_ge(s_qst, 64 * (B * PAIRS + 2))
            for i in range(2):
                sp.wait_ge(s_ctx[i], 16 * (B + 1))
                sp.wait_ge(s_w[i], 16 * (2 + B * PAIRS // 2))

        @block.gpsimd
        def _(pool):
            flat = xs.rearrange("r n d -> (r n d)").rearrange("(c p z) -> c p z", p=P, z=ZERO)
            for c in range(flat.shape[0]):
                pool.dma_start(flat[c], keep["zero"][:]).then_inc(s_zero, 16)

            def times_sin():
                pool.tensor_tensor(kT_swap[:], kT_swap[:], sinT[:], ALU.mult).then_inc(s_sin, 1)

            for i in range(2):
                pool.wait_ge(s_swap, 64 * (i + 1))
                times_sin()

            def slot(b, p):
                pool.wait_ge(s_swap, b * (64 * PAIRS) + 64 * (p + 3))
                times_sin()

            batches(pool, slot, lambda b: None)
            pool.wait_ge(s_zero, 16 * flat.shape[0])

        @block.tensor
        def _(pe):
            pe.sem_inc(s_pv, PROBS)

            def products(out, stationary, moving):
                n = 0
                for k in range(KD):
                    for a, m in ((0, 0), (0, 1), (1, 0)):
                        last = pe.matmul(out, stationary(a, k), moving(m, k), start=n == 0, stop=n == 3 * KD - 1)
                        n += 1
                return last

            def project(i, to, which, rows):
                products(proj[to][:], lambda a, k: w[i][:, which, a, k],
                         lambda m, k: rows[:, m, k]).then_inc(s_proj, 1)

            def project_v(duo, vbank, to):
                for t in range(2):
                    tile = slice((2 * (vbank % 2) + t) * P, (2 * (vbank % 2) + t + 1) * P)
                    last = products(proj[to][:, 256 * t:256 * t + 256], lambda a, k: ctxs[vbank // 2][:, a, k, tile],
                                    lambda m, k: wv[:, duo, m, k])
                last.then_inc(s_proj, 1)

            def score(i, j):
                for head in range(2):
                    for part in range(2):
                        last = pe.matmul(scores[j % 2][:, head], k_st[i][:, head, j * P:(j + 1) * P],
                                         q_st[i][:, head, part], start=part == 0, stop=part == 1)
                last.then_inc(s_scores, 1)

            for half in range(2):
                pe.wait_ge(s_ctx[half], 16)
            pe.wait_ge(s_lat, 16)
            for i in range(2):
                pe.wait_ge(s_w[i], 16)
                for n in range(3):
                    if 3 * i + n >= 2:
                        pe.wait_ge(s_projout, 3 * i + n - 1)
                    project(i, (3 * i + n) % 2, n // 2, ctxs[n] if n < 2 else lats)
            pe.wait_ge(s_wv, 16 * PAIRS)
            for n in range(VBANKS):
                pe.wait_ge(s_projout, n + 5)
                project_v(0, n, n % 2)
            pe.wait_ge(s_kst, 64)
            pe.wait_ge(s_qst, 64)
            for j in range(2):
                score(0, j)

            def slot(b, p):
                first = uses_before(b, p)
                def ahead(j):
                    pe.wait_ge(s_exp, b * (PAIRS * STEPS) + (p * STEPS + j + 1))
                    if j == STEPS - 2:
                        pe.wait_ge(s_kst, b * (64 * PAIRS) + 64 * (p + 2))
                        pe.wait_ge(s_qst, b * (64 * PAIRS) + 64 * (p + 2))
                    if j < STEPS - 2:
                        score(p % 2, j + 2)
                    else:
                        score((p + 1) % 2, j + 2 - STEPS)

                def projections(j):
                    if j not in USE_STEP:
                        return
                    i = USE_STEP.index(j)
                    kind, n = USES[i]
                    if i == 0:
                        pe.wait_ge(s_w[p % 2], b * (16 * PAIRS // 2) + 16 * (p // 2 + 2))
                    if p == PAIRS - 2 and kind == "k":
                        pe.wait_ge(s_ctx[n], b * 16 + 32)
                    if p == PAIRS - 2 and kind == "q":
                        pe.wait_ge(s_lat, b * 16 + 32)
                    pe.wait_ge(s_projout, first + (i - 1))
                    if kind == "v":
                        project_v((p // 2 + 1) % DUOS, 2 * (p % 2) + n, bank(p, i))
                    else:
                        project(p % 2, bank(p, i), 0 if kind == "k" else 1, ctxs[n] if kind == "k" else lats)

                def weigh(j):
                    pe.wait_ge(s_clip, b * (PAIRS * STEPS) + (p * STEPS + j + 1))
                    if j == 0:
                        pe.wait_ge(s_u, b * PAIRS + (p + 1))
                        pe.wait_ge(s_projout, first)
                    for head in range(2):
                        cols = P * (p % 2) + 64 * head
                        last = pe.matmul(pv_ps[64 * head:64 * head + 64], v_nat[p // 2 % 2][:, j, cols:cols + 64],
                                         probs[j % PROBS][:, head], start=j == 0, stop=j == STEPS - 1)
                    last.then_inc(s_pv, 1)

                for j in range(STEPS):
                    ahead(j)
                    projections(j)
                    weigh(j)
                pe.wait_ge(s_add, b * (PAIRS * STEPS) + (p * STEPS + STEPS + PROBS))
                pe.wait_ge(s_rden, b * PAIRS + (p + 1))
                for head in range(2):
                    last = pe.matmul(den_ps[64 * head:64 * head + 64], ones[:], p_sum[:, head], start=True, stop=True)
                last.then_inc(s_den, 1)

            def tail(b):
                for i in range(2):
                    out = proj[bank(PAIRS, i)]
                    pe.wait_ge(s_projout, uses_before(b, PAIRS) + (i - 1))
                    for p in range(PAIRS):
                        if p == PAIRS - 1:
                            pe.wait_ge(s_o, b * PAIRS + (PAIRS + 1))
                        for t in range(2):
                            last = pe.matmul(out[:, 256 * t:256 * t + 256], o[:, p, (2 * i + t) * P:(2 * i + t + 1) * P],
                                             wo[:, p], start=p == 0 and t == 0, stop=p == PAIRS - 1, skip_group_check=True)
                    last.then_inc(s_proj, 1)

            batches(pe, slot, tail)

        @block.scalar
        def _(act):
            act.sem_inc(s_u, 1)

            def exponentiate(j):
                act.activation(probs[j % PROBS][:], scores[j % 2][:], ACT.Exp, scale=float(HD) ** -0.5).then_inc(s_exp, 1)

            def copy_k(half, src):
                act.activation(kT[:, 512 * half:512 * half + 512], proj[src][:], ACT.Copy).then_inc(s_projout, 1)

            def copy_q(src):
                act.activation(q_split[:, 0], proj[src][:], ACT.Copy).then_inc(s_qhi, 1)
                act.activation(qT[:], proj[src][:], ACT.Copy).then_inc(s_projout, 1)

            def copy_v(i, vbank, src):
                act.activation(v_nat[i][:, 2 * vbank:2 * vbank + 2].rearrange("p t n -> p (t n)"),
                               proj[src][:], ACT.Copy).then_inc(s_projout, 1)

            for i in range(2):
                for n in range(3):
                    act.wait_ge(s_proj, 3 * i + n + 1)
                    if i == 1 and n == 0:
                        act.wait_ge(s_rope, 1)
                    if i == 1 and n == 2:
                        act.wait_ge(s_qst, 64)
                    if n < 2:
                        copy_k(n, (3 * i + n) % 2)
                    else:
                        copy_q((3 * i + n) % 2)
            for n in range(VBANKS):
                act.wait_ge(s_proj, n + 7)
                copy_v(0, n, n % 2)
            for j in range(2):
                act.wait_ge(s_scores, j + 1)
                exponentiate(j)

            def slot(b, p):
                first = uses_before(b, p)
                for j in range(STEPS):
                    g = p * STEPS + j + 2
                    act.wait_ge(s_scores, b * (PAIRS * STEPS) + (g + 1))
                    act.wait_ge(s_pv, b * (PAIRS * STEPS) + (g + 1))
                    act.wait_ge(s_add, b * (PAIRS * STEPS) + (g + 1))
                    exponentiate(g % STEPS)
                    if j in USE_STEP:
                        i = USE_STEP.index(j)
                        kind, n = USES[i]
                        act.wait_ge(s_proj, first + i + 1)
                        if kind == "k":
                            if n == 0:
                                act.wait_ge(s_rope, b * PAIRS + (p + 2))
                            copy_k(n, bank(p, i))
                        elif kind == "q":
                            act.wait_ge(s_qst, b * (64 * PAIRS) + 64 * (p + 2))
                            copy_q(bank(p, i))
                        else:
                            if n == 0:
                                act.wait_ge(s_pv, b * (PAIRS * STEPS) + (p * STEPS + PROBS))
                            copy_v((p // 2 + 1) % 2, 2 * (p % 2) + n, bank(p, i))
                act.wait_ge(s_pv, b * (PAIRS * STEPS) + (p * STEPS + STEPS + PROBS))
                act.wait_ge(s_o, b * PAIRS + (p + 1))
                act.activation(u_sb[:], pv_ps[:], ACT.Copy).then_inc(s_u, 1)

            def tail(b):
                for i in range(2):
                    act.wait_ge(s_proj, uses_before(b, PAIRS) + (i + 1))
                    if i == 0:
                        act.wait_ge(s_out, b * 16)
                    act.activation(x_out[:, 2 * i:2 * i + 2].rearrange("p t d -> p (t d)"),
                                   proj[bank(PAIRS, i)][:], ACT.Copy).then_inc(s_projout, 1)

            batches(act, slot, tail)

        @block.vector
        def _(v):
            v.sem_inc(s_add, PROBS)
            v.sem_inc(s_rden, 1)
            v.sem_inc(s_o, 1)

            def clip(j):
                pr = probs[j % PROBS][:]
                v.tensor_scalar(pr, pr, EXP_LO, EXP_HI, ALU.max, ALU.min).then_inc(s_clip, 1)

            def times_cos():
                v.tensor_tensor(k_rope[:], kT[:], cosT[:], ALU.mult).then_inc(s_cos, 1)

            def add_rope():
                v.tensor_tensor(k_rope[:], k_rope[:], kT_swap[:], ALU.add).then_inc(s_rope, 1)

            def high_k():
                v.tensor_copy(k_split[:, 0], k_rope[:]).then_inc(s_khi, 1)

            def low_k():
                v.tensor_tensor(k_split[:, 1], k_rope[:], k_split[:, 0].bitcast(F32), ALU.subtract).then_inc(s_klo, 1)

            def low_q():
                v.tensor_tensor(q_split[:, 1], qT[:], q_split[:, 0].bitcast(F32), ALU.subtract).then_inc(s_qlo, 1)

            for i in range(2):
                v.wait_ge(s_projout, 3 * i + 2)
                if i == 1:
                    v.wait_ge(s_klo, 1)
                times_cos()
                v.wait_ge(s_projout, 3 * i + 3)
                low_q()
                v.wait_ge(s_sin, i + 1)
                v.wait_ge(s_cos, i + 1)
                add_rope()
                v.wait_ge(s_rope, i + 1)
                if i == 1:
                    v.wait_ge(s_kst, 64)
                high_k()
                v.wait_ge(s_khi, i + 1)
                low_k()
            for j in range(2):
                v.wait_ge(s_exp, j + 1)
                clip(j)
            v.wait_ge(s_bo, 16)

            def slot(b, p):
                first, n = uses_before(b, p), b * PAIRS
                for j in range(STEPS):
                    g = p * STEPS + j
                    v.wait_ge(s_exp, b * (PAIRS * STEPS) + (g + 3))
                    clip((j + 2) % STEPS)
                    if j < STEPS - 1:
                        v.wait_ge(s_clip, b * (PAIRS * STEPS) + (g + 2))
                        before = probs[0] if j == 0 else p_sum
                        if j == 0:
                            v.wait_ge(s_den, n + p) if p else None
                        else:
                            v.wait_ge(s_add, b * (PAIRS * STEPS) + (g + 1 + PROBS))
                        v.tensor_tensor(p_sum[:], before[:], probs[(j + 1) % PROBS][:], ALU.add).then_inc(s_add, 2 if j == 0 else 1)
                    if j == 2:
                        v.wait_ge(s_projout, first + 2)
                        times_cos()
                    elif j == 4:
                        v.wait_ge(s_sin, n + (p + 3))
                        v.wait_ge(s_cos, n + (p + 3))
                        add_rope()
                    elif j == 5:
                        v.wait_ge(s_rope, n + (p + 3))
                        v.wait_ge(s_kst, b * (64 * PAIRS) + 64 * (p + 2))
                        high_k()
                    elif j == 6:
                        v.wait_ge(s_khi, n + (p + 3))
                        low_k()
                        v.wait_ge(s_projout, first + 5)
                        low_q()
                    if p == 1 and j == 5:
                        v.wait_ge(s_xin, b * 16 + 16)
                        v.tensor_tensor(x_in[:], x_in[:], bo_bc[:].unsqueeze(1).broadcast_to((P, QT, D)), ALU.add).then_inc(s_bias, 1)
                v.wait_ge(s_den, n + (p + 1))
                v.reciprocal(rden[:], den_ps[:]).then_inc(s_rden, 1)
                v.wait_ge(s_rden, n + (p + 2))
                v.wait_ge(s_u, n + (p + 2))
                if p == 0:
                    v.wait_ge(s_proj, uses_before(b, 0))
                v.tensor_tensor(o[:, p], u_sb[:], rden[:], ALU.mult).then_inc(s_o, 1)

            def tail(b):
                v.wait_ge(s_projout, uses_before(b, PAIRS) + 2)
                v.wait_ge(s_bias, b + 1)
                v.tensor_tensor(x_out[:], x_out[:], x_in[:], ALU.add).then_inc(s_x1, 1)

            batches(v, slot, tail)


def normalise_tokens(nc, sh, x1, router_w, xn_d, xnT, ffn):
    KD, QT, D, B, N, E = sh.KD, sh.QT, sh.D, sh.B, sh.N, sh.E
    with ExitStack() as es:
        def sb(name, shape, dt=F32):
            return es.enter_context(nc.sbuf_tensor(name, shape, dt))

        def sem(name):
            return es.enter_context(nc.semaphore(name))

        ident, acc, logits = ffn["ident"], ffn["acc"], ffn["logits"]
        T = [dict(x=sb(f"tx{i}", [P, QT, D]), xn=sb(f"txn{i}", [P, QT, D]), stats=sb(f"tst{i}", [P, QT, 6]),
                  mv=sb(f"tmv{i}", [P, QT, 2]), ve=sb(f"tve{i}", [P, QT]), r=sb(f"tr{i}", [P, QT]),
                  xT=sb(f"txT{i}", [P, KD, N]), split=sb(f"tsplit{i}", [P, 2, KD, N], F32R)) for i in range(2)]
        rw = sb("rw", [P, KD, E])
        neg_half = sb("t_neg_half", [P, QT])
        tp = [[es.enter_context(nc.psum_tensor(f"ttp{i}{k}", [P, QT, P], F32)) for k in range(KD)] for i in range(2)]
        lg = [es.enter_context(nc.psum_tensor(f"tlg{i}", [P, QT, E], F32)) for i in range(2)]

        s_rw, s_const = sem("t_rw"), sem("t_const")
        s_in = [sem(f"t_in{i}") for i in range(2)]
        s_stat, s_var, s_rstd, s_norm = sem("t_stat"), sem("t_var"), sem("t_rstd"), sem("t_norm")
        s_acc = sem("t_acc")
        s_tr, s_cp = sem("t_tr"), sem("t_cp")
        s_hi, s_lo = sem("t_hi"), sem("t_lo")
        s_lg, s_lgout = sem("t_lg"), sem("t_lgout")
        s_stn = [sem(f"t_stn{i}") for i in range(2)]
        s_stT = [sem(f"t_stT{i}") for i in range(2)]
        block = es.enter_context(nc.Block())

        @block.sync
        def _(sp):
            for i in range(2):
                sp.dma_start(T[i]["x"][:], x1[i].rearrange("(p t) d -> p t d", p=P)).then_inc(s_in[i], 16)
            sp.dma_start(rw[:], router_w.rearrange("(k p) e -> p k e", p=P)).then_inc(s_rw, 16)
            with sp.Fori(0, B // 2) as h:
                for i in range(2):
                    b = h * 2 + i
                    sp.wait_ge(s_norm, b + 1)
                    sp.dma_start(xn_d[b].rearrange("(p t) d -> p t d", p=P), T[i]["xn"][:]).then_inc(s_stn[i], 16)
                    sp.wait_ge(s_lo, b + 1)
                    sp.dma_start(xnT[b], T[i]["split"][:].rearrange("p a k n -> p (a k n)").bitcast(F32)).then_inc(s_stT[i], 16)
                    sp.wait_ge(s_acc, b + 1)
                    sp.dma_start(T[i]["x"][:], x1[(b + 2) % B].rearrange("(p t) d -> p t d", p=P)).then_inc(s_in[i], 16)
            for i in range(2):
                sp.wait_ge(s_stn[i], 16 * (B // 2))
                sp.wait_ge(s_stT[i], 16 * (B // 2))
                sp.wait_ge(s_in[i], 16 * (B // 2 + 1))

        @block.gpsimd
        def _(pool):
            pool.memset(neg_half[:], -0.5).then_inc(s_const, 1)
            pool.wait_ge(s_const, 1)
            with pool.Fori(0, B // 2) as h:
                for i in range(2):
                    pool.wait_ge(s_var, h * 2 + i + 1)
                    pool.tensor_tensor(T[i]["r"][:], T[i]["ve"][:], neg_half[:], ALU.pow).then_inc(s_rstd, 1)

        @block.vector
        def _(v):
            def first(b, i, at):
                t = T[i]
                v.wait_ge(s_in[i], at)
                for q in range(QT):
                    last = v.bn_stats(t["stats"][:, q], t["x"][:, q])
                last.then_inc(s_stat, 1)
                v.wait_ge(s_stat, 2 * b + 1)
                v.memset(t["ve"][:], EPS)
                for q in range(QT):
                    last = v.bn_aggr(t["mv"][:, q], t["stats"][:, q])
                last.then_inc(s_stat, 1)
                v.wait_ge(s_stat, 2 * b + 2)
                v.tensor_tensor(t["ve"][:], t["mv"][:, :, 1], t["ve"][:], ALU.add).then_inc(s_var, 1)

            def second(b, i, h):
                t = T[i]
                v.wait_ge(s_rstd, b + 1)
                v.wait_ge(s_stn[i], 16 * h)
                for q in range(QT):
                    last = v.tensor_scalar(t["xn"][:, q], t["x"][:, q], t["mv"][:, q, 0:1], t["r"][:, q:q + 1], ALU.subtract, ALU.mult)
                last.then_inc(s_norm, 1)
                v.wait_ge(s_norm, b + 1)
                v.tensor_tensor(acc[:, bass.ds(b * QT, QT)], t["x"][:], t["xn"][:], ALU.add).then_inc(s_acc, 1)

            def third(b, i, h):
                t = T[i]
                v.wait_ge(s_cp, 2 * b + 2)
                v.wait_ge(s_stT[i], 16 * h)
                v.tensor_copy(t["split"][:, 0], t["xT"][:]).then_inc(s_hi, 1)
                v.wait_ge(s_hi, b + 1)
                v.tensor_tensor(t["split"][:, 1], t["xT"][:], t["split"][:, 0].bitcast(F32), ALU.subtract).then_inc(s_lo, 1)

            with v.Fori(0, B // 2) as h:
                for i in range(2):
                    first(h * 2 + i, i, 16 * h + 16)
                for i in range(2):
                    second(h * 2 + i, i, h)
                for i in range(2):
                    third(h * 2 + i, i, h)

        @block.tensor
        def _(pe):
            pe.wait_ge(s_rw, 16)
            with pe.Fori(0, B // 2) as h:
                for i in range(2):
                    b = h * 2 + i
                    t = T[i]
                    pe.wait_ge(s_norm, b + 1)
                    pe.wait_ge(s_cp, 4 * h)
                    for k in range(KD):
                        for q in range(QT):
                            last = pe.transpose(tp[i][k][:, q], t["xn"][:, q, k * P:(k + 1) * P], ident[:])
                        last.then_inc(s_tr, 1)
                for i in range(2):
                    b = h * 2 + i
                    t = T[i]
                    pe.wait_ge(s_cp, 2 * b + 2)
                    pe.wait_ge(s_lgout, 2 * h)
                    for q in range(QT):
                        for k in range(KD):
                            last = pe.matmul(lg[i][:, q], t["xT"][:, k, q * P:(q + 1) * P], rw[:, k], start=k == 0, stop=k == KD - 1)
                    last.then_inc(s_lg, 1)

        @block.scalar
        def _(act):
            with act.Fori(0, B // 2) as h:
                for i in range(2):
                    b = h * 2 + i
                    act.wait_ge(s_lo, 2 * h)
                    act.wait_ge(s_lg, 2 * h)
                    for k in range(KD):
                        act.wait_ge(s_tr, 2 * b + k + 1)
                        act.activation(T[i]["xT"][:, k], tp[i][k][:].rearrange("p a b -> p (a b)"), ACT.Copy).then_inc(s_cp, 1)
                for i in range(2):
                    b = h * 2 + i
                    act.wait_ge(s_lg, b + 1)
                    act.activation(logits[:, bass.ds(b * QT, QT)], lg[i][:], ACT.Copy).then_inc(s_lgout, 1)


def experts(nc, sh, xn_d, xnT, xs, ys, shared_up, shared_down, routed_up, routed_down, out, ffn):
    KD, QT, D, B, N, E, F = sh.KD, sh.QT, sh.D, sh.B, sh.N, sh.E, sh.F
    FT = F // P
    NT = B * QT
    TILES = sh.TILES
    with ExitStack() as es:
        def sb(name, shape, dt=F32):
            return es.enter_context(nc.sbuf_tensor(name, shape, dt))

        def sem(name):
            return es.enter_context(nc.semaphore(name))

        ident, acc, logits = ffn["ident"], ffn["acc"], ffn["logits"]
        raw = [[sb(f"raw{i}{n}", [P, KD * F]) for n in range(2)] for i in range(2)]
        up = [sb(f"up{i}", [P, 2, KD * F], F32R) for i in range(2)]
        down = [sb(f"down{i}", [P, 2, KD * F], F32R) for i in range(2)]
        xT = [sb(f"xT{i}", [P, 2, KD, N], F32R) for i in range(2)]
        rows = [sb(f"rows{i}", [P, QT, D]) for i in range(2)]
        hid = [sb(f"hid{i}", [P, N]) for i in range(2)]
        hid_split = [sb(f"hid_split{i}", [P, 2, N], F32R) for i in range(4)]
        y_sb = sb("y_sb", [P, QT, D])
        tri = sb("tri", [P, P])
        all_ones = sb("all_ones", [P, P])
        before = sb("before", [P, E, E])
        steps_n = sb("steps_n", [P, E, E])
        tile_no = sb("tile_no", [P, TILES, E - 1])
        probs = sb("r_probs", [P, NT, E])
        mx, tot, rtot = sb("r_mx", [P, NT]), sb("r_tot", [P, NT]), sb("r_rtot", [P, NT])
        rank = sb("r_rank", [P, NT, E])
        sel0, sel1, both = sb("r_sel0", [P, NT, E]), sb("r_sel1", [P, NT, E]), sb("r_both", [P, NT, E])
        gate = [sb(f"gate{i}", [P, NT]) for i in range(2)]
        counts_et = sb("r_counts", [P, E, NT])
        run = sb("r_run", [P, E, NT])
        n_tiles, ends, base, count = sb("r_nt", [P, E]), sb("r_ends", [P, E]), sb("r_base", [P, E]), sb("r_cnt", [P, E])
        ones_e = sb("r_ones", [P, E * NT])
        pos = sb("r_pos", [P, NT, E])
        idx = [sb(f"idx{i}", [P, NT], I32) for i in range(2)]
        tmp = sb("r_tmp", [P, NT, E])
        posf = sb("r_posf", [P, NT])
        tile_e = sb("tile_e", [P, TILES])
        tile_ei = sb("tile_ei", [P, TILES], I32)

        pair_big = raw[1][0][:].rearrange("p (t e f) -> p t e f", e=E, f=E)
        eq_big = raw[1][1][:].rearrange("p (t e f) -> p t e f", e=E, f=E)

        gat = [[raw[i][n][:, 0:QT * D].rearrange("p (t d) -> p t d", d=D) for n in range(2)] for i in range(2)]

        def ps(name, shape):
            return es.enter_context(nc.psum_tensor(name, shape, F32))

        hp = [ps(f"hp{i}", [P, N]) for i in range(4)]
        yp = ps("yp", [P, QT, D])
        tp = [ps(f"ftp{k}", [P, QT, P]) for k in range(KD)]

        s_cc, s_const = sem("f_cc"), sem("f_const")
        s_r = sem("f_r")
        s_re = sem("f_re")
        s_rm = sem("f_rm")
        s_idx = sem("f_idx")
        s_stage = [sem(f"f_stage{i}") for i in range(2)]
        s_scat = [sem(f"f_scat{i}") for i in range(2)]
        s_scatall = sem("f_scatall")
        s_raw = [sem(f"f_raw{i}") for i in range(2)]
        s_shT = [sem(f"f_shT{i}") for i in range(2)]
        s_rows = [sem(f"f_rows{i}") for i in range(2)]
        s_whi, s_wlo = sem("f_whi"), sem("f_wlo")
        s_tr = sem("f_tr")
        s_xhi, s_xlo = sem("f_xhi"), sem("f_xlo")
        s_up = sem("f_up")
        s_hhi, s_hlo = sem("f_hhi"), sem("f_hlo")
        s_dn = sem("f_dn")
        s_y = sem("f_y")
        s_yout = sem("f_yout")
        s_gat = [sem(f"f_gat{i}") for i in range(2)]
        s_comb = sem("f_comb")
        s_out = sem("f_out")
        s_half = sem("f_half")
        block = es.enter_context(nc.Block())

        @block.sync
        def _(sp):
            def load_raw(i, up_ap, down_ap):
                sp.dma_start(raw[i][0][:].rearrange("p (k f) -> p k f", k=KD), up_ap.rearrange("(k p) f -> p k f", p=P)).then_inc(s_raw[i], 16)
                sp.dma_start(raw[i][1][:].rearrange("p (c n) -> p c n", n=D), down_ap.rearrange("(c p) n -> p c n", p=P)).then_inc(s_raw[i], 16)

            def load_expert(r, i):
                e = sp.value_load(tile_ei[0:1, bass.ds(r, 1)], min_val=0, max_val=E - 1)
                load_raw(i, routed_up[e], routed_down[e])

            def load_rows(r, i):
                sp.dma_start(rows[i][:], xs[r].rearrange("(p t) d -> p t d", p=P)).then_inc(s_rows[i], 16)

            def load_shared(b, i):
                sp.dma_start(xT[i][:].rearrange("p a k n -> p (a k n)").bitcast(F32), xnT[b]).then_inc(s_shT[i], 16)

            load_raw(0, shared_up[0], shared_down[0])
            load_shared(0, 0)
            load_shared(1, 1)

            sp.wait_ge(s_idx, 1)
            sp.wait_ge(s_wlo, FT)
            load_expert(0, 0)
            load_expert(1, 1)
            with sp.Fori(0, B // 2 - 1) as h:
                for i in range(2):
                    b = h * 2 + i
                    sp.wait_ge(s_up, FT * b + FT)
                    load_shared(b + 2, i)
            sp.wait_ge(s_scatall, 1)
            load_rows(0, 0)
            load_rows(1, 1)

            def store(r):
                sp.wait_ge(s_y, B + r + 1)
                sp.dma_start(ys[r].rearrange("(p t) d -> p t d", p=P), y_sb[:]).then_inc(s_yout, 16)

            with sp.Fori(0, TILES // 2 - 1) as k:
                for i in range(2):
                    r = k * 2 + i
                    sp.wait_ge(s_wlo, FT * (r + 2))
                    load_expert(r + 2, i)
                    sp.wait_ge(s_tr, r + 1)
                    load_rows(r + 2, i)
                    store(r)
            r = TILES - 3
            sp.wait_ge(s_wlo, FT * (r + 2))
            load_expert(r + 2, r % 2)
            sp.wait_ge(s_tr, r + 1)
            load_rows(r + 2, r % 2)
            for r in range(TILES - 3, TILES):
                store(r)
            sp.wait_ge(s_yout, 16 * TILES)
            with sp.Fori(0, B // 2) as h:
                for i in range(2):
                    b = h * 2 + i
                    sp.wait_ge(s_comb, b + 1)
                    sp.dma_start(out[b].rearrange("(p t) d -> p t d", p=P), acc[:, bass.ds(b * QT, QT)]).then_inc(s_out, 16)
            sp.wait_ge(s_out, 16 * B)

        @block.gpsimd
        def _(pool):
            pool.memset(tri[:], 1.0)
            pool.memset(all_ones[:], 1.0)
            pool.memset(ones_e[:], 1.0)
            pool.memset(before[:], 1.0)
            pool.iota(steps_n[:], pattern=[[0, E], [N, E]], base=0, channel_multiplier=0, allow_small_or_imprecise_dtypes=True)
            pool.iota(tile_no[:], pattern=[[1, TILES], [0, E - 1]], base=0, channel_multiplier=0,
                      allow_small_or_imprecise_dtypes=True).then_inc(s_cc, 1)
            pool.wait_ge(s_cc, 1)
            pool.affine_select(out=tri[:], in_=tri[:], compare_op=ALU.is_gt, fill=0.0, base=0,
                               pattern=[[1, P]], channel_multiplier=-1).then_inc(s_cc, 1)
            pool.affine_select(out=before[:], in_=before[:], compare_op=ALU.is_gt, fill=0.0, base=0,
                               pattern=[[1, E], [-1, E]], channel_multiplier=0).then_inc(s_cc, 1)
            pool.wait_ge(s_cc, 3)
            pool.memset(posf[:], 0.0).then_inc(s_const, 1)
            for b in range(B):
                i = b % 2
                if b >= 2:
                    pool.wait_ge(s_scat[i], 16 * 2 * QT * (b // 2))
                pool.dma_start(rows[i][:], xn_d[b].rearrange("(p t) d -> p t d", p=P)).then_inc(s_stage[i], 16)
                if b == 0:
                    pool.wait_ge(s_idx, 1)
                pool.wait_ge(s_stage[i], 16 * (b // 2 + 1))
                for t in range(QT):
                    for n in range(2):
                        pool.indirect_dma_start(xs.rearrange("r n d -> (r n) d"),
                                                bass.IndirectOffsetOnAxis(ap=idx[n][:, b * QT + t:b * QT + t + 1], axis=0),
                                                rows[i][:, t], None).then_inc(s_scat[i], 16)
            for i in range(2):
                pool.wait_ge(s_scat[i], 16 * 2 * QT * (B // 2))
            pool.sem_inc(s_scatall, 1)
            pool.wait_ge(s_y, B + TILES)
            pool.wait_ge(s_yout, 16 * TILES)
            for b in range(B):
                i = b % 2
                if b >= 2:
                    pool.wait_ge(s_comb, b - 1)
                for t in range(QT):
                    for n in range(2):
                        pool.indirect_dma_start(gat[i][n][:, t], None, ys.rearrange("r n d -> (r n) d"),
                                                bass.IndirectOffsetOnAxis(ap=idx[n][:, b * QT + t:b * QT + t + 1], axis=0)
                                                ).then_inc(s_gat[i], 16)

        def tiles(eng, body):
            with eng.Fori(0, B // 2 - 1) as h:
                body(h * 2, 0, None, "shared", None, h)
                body(h * 2 + 1, 1, None, "shared", None, h + 1)
            body(B - 2, 0, None, "shared", None, B // 2 - 1)
            body(B - 1, 1, None, "routed", 0, 0)
            with eng.Fori(0, TILES // 2) as k:
                body(B + k * 2, 0, k * 2, "routed", k * 2 + 1, k)
                body(B + k * 2 + 1, 1, k * 2 + 1, "routed", k * 2 + 2, k + 1)
            body(B + TILES - 1, 0, TILES - 1, None, None, None)

        @block.tensor
        def _(pe):
            pe.wait_ge(s_const, 1)
            pe.wait_ge(s_r, R_BOTH)
            pe.matmul(hp[0][:, 0:NT * E], tri[:], both[:].rearrange("p t e -> p (t e)"), start=True, stop=True)
            pe.matmul(hp[1][:, 0:NT * E], all_ones[:], both[:].rearrange("p t e -> p (t e)"), start=True, stop=True).then_inc(s_rm, 1)

            def up_product(u, wu, f, read):
                pe.wait_ge(s_hhi, read)
                n = 0
                for k in range(KD):
                    for wp, xp in ((0, 0), (0, 1), (1, 0)):
                        last = pe.matmul(hp[f % 4][:], up[wu][:, wp, k * F + f * P:k * F + (f + 1) * P], xT[u][:, xp, k],
                                         start=n == 0, stop=n == 3 * KD - 1)
                        n += 1
                last.then_inc(s_up, 1)

            def down_product(T, wu, f, r):
                pe.wait_ge(s_hlo, FT * T + f + 1)
                if f == 0:
                    pe.wait_ge(s_y, T)
                    if r is not None:
                        pe.wait_ge(s_wlo, FT * (r + 2))
                hs = hid_split[f % 4]
                for t in range(QT):
                    for n, (hpart, wp) in enumerate(((0, 0), (1, 0), (0, 1))):
                        last = pe.matmul(yp[:, t], hs[:, hpart, t * P:(t + 1) * P], down[wu][:, wp, f * D:(f + 1) * D],
                                         start=f == 0 and n == 0 and t % 2 == 0, stop=f == FT - 1 and n == 2, skip_group_check=True)
                last.then_inc(s_dn, 1)

            def transpose_rows(r, u, k):
                pe.wait_ge(s_rows[u], 16 * (k + 1))
                pe.wait_ge(s_xlo, r)
                for kd in range(KD):
                    for q in range(QT):
                        last = pe.transpose(tp[kd][:, q], rows[u][:, q, kd * P:(kd + 1) * P], ident[:])
                last.then_inc(s_tr, 1)

            pe.wait_ge(s_r, R_READ)
            pe.wait_ge(s_wlo, FT)
            pe.wait_ge(s_shT[0], 16)
            for f in range(2):
                up_product(0, 0, f, 0)

            def body(T, u, r, nxt, n, k):
                wu = 0 if r is None else 1 - u
                for f in range(2, FT):
                    up_product(u, wu, f, FT * T + max(f - 3, 0))
                    down_product(T, wu, f - 2, r)
                    if f == 4 and nxt == "routed":
                        transpose_rows(n, 1 - u, k)
                if nxt == "shared":
                    pe.wait_ge(s_shT[1 - u], 16 * k + 16)
                elif nxt == "routed":
                    pe.wait_ge(s_xlo, n + 1)
                    pe.wait_ge(s_wlo, FT * (n + 1) + FT // 2)
                for f in range(2):
                    if nxt is not None:
                        up_product(1 - u, 0 if nxt == "shared" else u, f, FT * (T + 1) + f - 3)
                    down_product(T, wu, FT - 2 + f, r)

            tiles(pe, body)

        @block.scalar
        def _(act):
            act.wait_ge(s_r, R_MAXED)
            act.activation(probs[:], probs[:], ACT.Exp).then_inc(s_re, 1)

            def weight_chunk(u, wu, f):
                n, q = f // 4, f % 4
                act.activation((up, down)[n][wu][:, 0, 512 * q:512 * q + 512], raw[u][n][:, 512 * q:512 * q + 512],
                               ACT.Copy).then_inc(s_whi, 1)

            def hidden(g, f):
                act.wait_ge(s_up, g + 1)
                act.activation(hid[f % 2][:], hp[f % 4][:], ACT.Gelu)
                act.activation(hid_split[f % 4][:, 0], hp[f % 4][:], ACT.Gelu).then_inc(s_hhi, 1)

            act.wait_ge(s_raw[0], 32)
            for f in range(FT):
                weight_chunk(0, 0, f)
            for f in range(2):
                hidden(f, f)

            def body(T, u, r, nxt, n, k):
                for f in range(2, FT + (0 if nxt is None else 2)):
                    act.wait_ge(s_hlo, FT * T + f - 1)
                    act.wait_ge(s_dn, FT * T + max(f - 3, 0))
                    hidden(FT * T + f, f % FT)
                    if nxt == "routed":
                        if f == 2:
                            act.wait_ge(s_dn, FT * T)
                            act.wait_ge(s_raw[1 - u], 32 * k + (64 if u == 1 else 32))
                        weight_chunk(1 - u, u, f - 2)
                if r is not None:
                    act.wait_ge(s_dn, FT * T + FT)
                    act.wait_ge(s_yout, 16 * r)
                    act.activation(y_sb[:], yp[:], ACT.Copy).then_inc(s_y, 1)

            tiles(act, body)

        @block.vector
        def _(v):
            step = [0]

            def then(ins):
                step[0] += 1
                ins.then_inc(s_r, 1)
                v.wait_ge(s_r, step[0])

            v.wait_ge(s_const, 1)

            def over_e(ap):
                return ap.unsqueeze(2).broadcast_to((P, NT, E))

            then(v.tensor_reduce(mx[:], logits[:], AX.X, ALU.max))
            then(v.tensor_tensor(probs[:], logits[:], over_e(mx[:]), ALU.subtract))
            assert step[0] == R_MAXED
            v.wait_ge(s_re, 1)
            then(v.tensor_reduce(tot[:], probs[:], AX.X, ALU.add))
            then(v.reciprocal(rtot[:], tot[:]))
            then(v.tensor_tensor(probs[:], probs[:], over_e(rtot[:]), ALU.mult))
            mine = probs[:].unsqueeze(3).broadcast_to((P, NT, E, E))
            other = probs[:].unsqueeze(2).broadcast_to((P, NT, E, E))
            v.tensor_tensor(pair_big, other, mine, ALU.is_gt)
            then(v.tensor_tensor(eq_big, other, mine, ALU.is_equal))
            then(v.tensor_tensor(eq_big, eq_big, before[:].unsqueeze(1).broadcast_to((P, NT, E, E)), ALU.mult))
            then(v.tensor_tensor(pair_big, pair_big, eq_big, ALU.add))
            then(v.tensor_reduce(rank[:], pair_big, AX.X, ALU.add))
            v.tensor_scalar(sel0[:], rank[:], 0.0, None, ALU.is_equal)
            v.tensor_scalar(sel1[:], rank[:], 1.0, None, ALU.is_equal)
            then(v.tensor_scalar(both[:], rank[:], 2.0, None, ALU.is_lt))
            assert step[0] == R_BOTH
            for n, s in enumerate((sel0, sel1)):
                then(v.tensor_tensor(tmp[:], s[:], probs[:], ALU.mult))
                then(v.tensor_reduce(gate[n][:], tmp[:], AX.X, ALU.add))
            v.wait_ge(s_rm, 1)
            counts = hp[1][:, 0:NT * E].rearrange("p (t e) -> p e t", e=E)
            then(v.tensor_copy(counts_et[:], counts))
            flat = "p e t -> p (e t)"
            then(v.tensor_tensor_scan(run[:].rearrange(flat), ones_e[:], counts_et[:].rearrange(flat), 0.0, ALU.mult, ALU.add))
            v.tensor_copy(count[:, 0:1], run[:, 0, NT - 1:NT])
            then(v.tensor_tensor(count[:, 1:E], run[:, 1:E, NT - 1], run[:, 0:E - 1, NT - 1], ALU.subtract))
            cmp = tmp[:, 0:E]
            then(v.tensor_tensor(cmp, count[:].unsqueeze(2).broadcast_to((P, E, E)), steps_n[:], ALU.is_gt))
            then(v.tensor_reduce(n_tiles[:], cmp, AX.X, ALU.add))
            then(v.tensor_tensor_scan(ends[:], ones_e[:, 0:E], n_tiles[:], 0.0, ALU.mult, ALU.add))
            then(v.tensor_tensor(base[:], ends[:], n_tiles[:], ALU.subtract))
            then(v.tensor_scalar(base[:], base[:], float(N), None, ALU.mult))
            then(v.tensor_tensor(base[:, 1:E], base[:, 1:E], run[:, 0:E - 1, NT - 1], ALU.subtract))
            then(v.tensor_tensor(run[:], run[:], counts_et[:], ALU.subtract))
            then(v.tensor_tensor(run[:], run[:], base[:].unsqueeze(2).broadcast_to((P, E, NT)), ALU.add))
            then(v.tensor_tensor(pos[:], hp[0][:, 0:NT * E].rearrange("p (t e) -> p t e", e=E),
                                 run[:].rearrange("p e t -> p t e"), ALU.add))
            assert step[0] == R_READ
            for n, s in enumerate((sel0, sel1)):
                then(v.tensor_tensor(tmp[:], s[:], pos[:], ALU.mult))
                then(v.tensor_reduce(posf[:], tmp[:], AX.X, ALU.add))
                then(v.tensor_copy(idx[n][:], posf[:]))
            te = rank[:].rearrange("p t e -> p (t e)")[:, 0:TILES * (E - 1)].rearrange("p (t e) -> p t e", e=E - 1)
            then(v.tensor_tensor(te, ends[:, 0:E - 1].unsqueeze(1).broadcast_to((P, TILES, E - 1)), tile_no[:], ALU.is_le))
            then(v.tensor_reduce(tile_e[:], te, AX.X, ALU.add))
            v.tensor_copy(tile_ei[:], tile_e[:]).then_inc(s_idx, 1)

            def weight_chunk(u, wu, f, at):
                n, q = f // 4, f % 4
                v.wait_ge(s_whi, at + f + 1)
                dst = (up, down)[n][wu]
                v.tensor_tensor(dst[:, 1, 512 * q:512 * q + 512], raw[u][n][:, 512 * q:512 * q + 512],
                                dst[:, 0, 512 * q:512 * q + 512].bitcast(F32), ALU.subtract).then_inc(s_wlo, 1)

            def hidden(g, f):
                v.wait_ge(s_hhi, g + 1)
                v.tensor_tensor(hid_split[f % 4][:, 1], hid[f % 2][:], hid_split[f % 4][:, 0].bitcast(F32),
                                ALU.subtract).then_inc(s_hlo, 1)

            def split_rows(r, u, T):
                v.wait_ge(s_tr, r + 1)
                v.wait_ge(s_up, FT * T)
                for k in range(KD):
                    last = v.tensor_copy(xT[u][:, 0, k], tp[k][:].rearrange("p a b -> p (a b)"))
                last.then_inc(s_xhi, 1)
                v.wait_ge(s_xhi, r + 1)
                for k in range(KD):
                    last = v.tensor_tensor(xT[u][:, 1, k], tp[k][:].rearrange("p a b -> p (a b)"),
                                           xT[u][:, 0, k].bitcast(F32), ALU.subtract)
                last.then_inc(s_xlo, 1)

            for f in range(FT):
                weight_chunk(0, 0, f, 0)
            for f in range(2):
                hidden(f, f)

            def body(T, u, r, nxt, n, k):
                for f in range(2, FT + (0 if nxt is None else 2)):
                    hidden(FT * T + f, f % FT)
                    if nxt == "routed":
                        weight_chunk(1 - u, u, f - 2, FT * (n + 1))
                        if f == 6:
                            split_rows(n, 1 - u, T)
                if r is None:
                    v.wait_ge(s_dn, FT * T + FT)
                    part = acc[:, bass.ds(T * QT, QT)]
                    v.tensor_tensor(part, yp[:], part, ALU.add).then_inc(s_y, 1)

            tiles(v, body)
            for b in range(B):
                i = b % 2
                v.wait_ge(s_gat[i], 16 * 2 * QT * (b // 2 + 1))
                if b == 0:
                    v.wait_ge(s_y, B + TILES)
                for n in range(2):
                    for t in range(QT):
                        q = b * QT + t
                        last = v.scalar_tensor_tensor(acc[:, q], gat[i][n][:, t], gate[n][:, q:q + 1], acc[:, q], ALU.mult, ALU.add)
                    if n == 0:
                        last.then_inc(s_half, 1)
                        v.wait_ge(s_half, b + 1)
                last.then_inc(s_comb, 1)


R_MAXED = 2
R_BOTH = 10
R_READ = 26


def build(nc, x, ctx_1024, cos, sin, lat_g, lat_b, ctx_g, ctx_b, Wq, Wkv, Wo, bo,
          shared_up, shared_down, routed_up, routed_down, router_w, out):
    sh = Shapes(x, ctx_1024, cos, Wq, routed_up)
    KD, PAIRS, B, N, D = sh.KD, sh.PAIRS, sh.B, sh.N, sh.D

    def dram(name, shape):
        return nc.dram_tensor(name, shape, F32, kind="Internal").ap()

    wpack = dram("wpack", (PAIRS, P, 3 * 2 * KD * P))
    ctxT = dram("ctx_parts", (B + 1, P, 2 * KD * sh.S))
    latT = dram("lat_parts", (B + 1, P, 2 * KD * N))
    x1 = dram("attended", (B, N, D))
    xn_d = dram("normed", (B, N, D))
    xnT = dram("normedT", (B, P, 2 * KD * N))
    xs = dram("sorted_rows", (sh.TILES, N, D))
    ys = dram("sorted_results", (sh.TILES, N, D))
    with ExitStack() as es:
        def sb(name, shape, dt=F32):
            return es.enter_context(nc.sbuf_tensor(name, shape, dt))

        ident = sb("ident", [P, P])
        with ExitStack() as es1:
            def sb1(name, shape, dt=F32):
                return es1.enter_context(nc.sbuf_tensor(name, shape, dt))

            keep = dict(ident=ident, cosT=sb1("cosT", [P, sh.S]), sinT=sb1("sinT", [P, sh.S]),
                        wo=sb1("wo", [P, PAIRS, D]), ones=sb1("ones", [P, sh.HD]), zero=sb1("zero", [P, ZERO]))
            prepare(nc, sh, x, ctx_1024, cos, sin, lat_g, lat_b, ctx_g, ctx_b, Wq, Wkv, Wo, wpack, ctxT, latT, keep)
            attend(nc, sh, x, bo, wpack, ctxT, latT, x1, xs, keep)
        ffn = dict(ident=ident, acc=sb("acc", [P, B * sh.QT, D]), logits=sb("logits", [P, B * sh.QT, sh.E]))
        normalise_tokens(nc, sh, x1, router_w, xn_d, xnT, ffn)
        experts(nc, sh, xn_d, xnT, xs, ys, shared_up, shared_down, routed_up, routed_down, out, ffn)


_INS = ["x", "ctx_1024", "L0_xattn_cos", "L0_xattn_sin", "L0_xattn_ln_lat_g", "L0_xattn_ln_lat_b",
        "L0_xattn_ln_ctx_g", "L0_xattn_ln_ctx_b", "L0_xattn_Wq", "L0_xattn_Wkv", "L0_xattn_Wo", "L0_xattn_bo",
        "L0_ffn_shared_up", "L0_ffn_shared_down", "L0_ffn_routed_up", "L0_ffn_routed_down", "L0_ffn_router_w"]


def kernel(**inputs):
    import numpy as np
    import concourse.bacc as bacc
    from concourse.bass_utils import run_bass_kernel_spmd

    nc = bacc.Bacc("TRN2", target_bir_lowering=False, num_devices=1)
    arrays, args = {}, []
    for name in _INS:
        a = np.ascontiguousarray(inputs[name])
        arrays[name] = a
        args.append(nc.dram_tensor(name, a.shape, mybir.dt.from_np(a.dtype), kind="ExternalInput").ap())
    out = nc.dram_tensor("out", inputs["x"].shape, F32, kind="ExternalOutput").ap()
    build(nc, *args, out)
    return run_bass_kernel_spmd(nc, [arrays], core_ids=[0]).results[0]["out"]
```

```python
from contextlib import ExitStack

import concourse.bass as bass
from concourse import mybir

F32 = mybir.dt.float32
F32R = mybir.dt.float32r
I32 = mybir.dt.int32
ALU = mybir.AluOpType
ACT = mybir.ActivationFunctionType
AX = mybir.AxisListType

P = 128
ZERO = 368
EPS = 1e-5
CLIP = 11.0
EXP_HI = 59874.141715197816
EXP_LO = 1.670170079024566e-05


class Shapes:

    def __init__(self, x, ctx, cos, Wq, routed_up):
        self.B, self.N, self.D = x.shape
        self.S = ctx.shape[1]
        self.HD = 2 * cos.shape[1]
        self.INNER = Wq.shape[1]
        self.PAIRS = self.INNER // P
        self.KD = self.D // P
        self.QT = self.N // P
        self.KT = self.S // P
        self.E = routed_up.shape[0]
        self.F = routed_up.shape[2]
        self.TILES = (2 * self.B * self.N + self.E * (self.N - 1)) // self.N
        assert 2 * self.HD == P and self.KD == 2 and self.N == 512 and self.KT == 8 and self.PAIRS == 8


def prepare(nc, sh, x, ctx_in, cos, sin, lat_g, lat_b, ctx_g, ctx_b, Wq, Wkv, Wo, wpack, ctxT, latT, keep):
    KD, KT, QT, PAIRS, D, B = sh.KD, sh.KT, sh.QT, sh.PAIRS, sh.D, sh.B
    with ExitStack() as es:
        def sb(name, shape, dt=F32):
            return es.enter_context(nc.sbuf_tensor(name, shape, dt))

        def ps(name, shape, dt=F32):
            return es.enter_context(nc.psum_tensor(name, shape, dt))

        def sem(name):
            return es.enter_context(nc.semaphore(name))

        ident, cosT, sinT, wo, ones = keep["ident"], keep["cosT"], keep["sinT"], keep["wo"], keep["ones"]

        w_raw = sb("w_raw", [P, KD, 3 * sh.INNER])
        w_split = sb("w_split", [P, PAIRS, 3, 2, KD, P], F32R)
        trig = sb("trig", [P, 2, KT, sh.HD // 2])
        trig4 = sb("trig4", [P, 2, KT, 4, sh.HD // 2])
        gb = sb("gb", [P, 4, KD])
        neg_half = sb("neg_half", [P, KT])
        T = [dict(
            ctx=sb(f"ctx{i}", [P, KT, D]), x=sb(f"x{i}", [P, QT, D]), xn=sb(f"xn{i}", [P, QT, D]),
            stats=sb(f"stats{i}", [P, KT, 6]), mv=sb(f"mv{i}", [P, KT, 2]), r=sb(f"r{i}", [P, KT]),
            xstats=sb(f"xstats{i}", [P, QT, 6]), xmv=sb(f"xmv{i}", [P, QT, 2]), xr=sb(f"xr{i}", [P, QT]),
            shift=sb(f"shift{i}", [P, KT]), ve=sb(f"ve{i}", [P, KT]), xve=sb(f"xve{i}", [P, QT]),
            full=sb(f"full{i}", [P, KD, sh.S]), xfull=sb(f"xfull{i}", [P, KD, sh.N]),
        ) for i in range(2)]
        ctx_split = [sb(f"ctx_split{i}", [P, 2, KD, sh.S], F32R) for i in range(2)]
        lat_split = [sb(f"lat_split{i}", [P, 2, KD, sh.N], F32R) for i in range(2)]
        tp = [ps(f"tp{i}", [P, 4, P]) for i in range(8)]

        s_tabin, s_wo, s_w = sem("s_tabin"), sem("s_wo"), [sem(f"s_w_{i}") for i in range(3)]
        s_const = sem("s_const")
        s_cc = sem("s_cc")
        s_trig4 = sem("s_trig4")
        s_hi = sem("s_hi")
        s_lo = sem("s_lo")
        s_wout = sem("s_wout")
        s_tabT = sem("s_tabT")
        s_tab = sem("s_tab")
        s_cin, s_xin = [sem(f"s_cin{i}") for i in range(2)], [sem(f"s_xin{i}") for i in range(2)]
        s_cstat, s_cvar, s_crstd, s_cnorm = sem("s_cstat"), sem("s_cvar"), sem("s_crstd"), sem("s_cnorm")
        s_cshift = sem("s_cshift")
        s_xstat, s_xvar, s_xrstd, s_xnorm = sem("s_xstat"), sem("s_xvar"), sem("s_xrstd"), sem("s_xnorm")
        s_ctr, s_xtr = sem("s_ctr"), sem("s_xtr")
        s_cfull, s_xfull = sem("s_cfull"), sem("s_xfull")
        s_clo, s_xlo = [sem(f"s_clo{i}") for i in range(2)], sem("s_xlo")
        s_cout = [sem(f"s_cout{i}") for i in range(2)]
        s_xout = [sem(f"s_xout{i}") for i in range(2)]

        w4 = w_raw[:].rearrange("p k (t c n) -> p t k c n", t=3, n=P)
        block = es.enter_context(nc.Block())

        def rows(ap, b):
            return ap[b].rearrange("(p t) d -> p t d", p=P)

        @block.sync
        def _(sp):
            for i in range(2):
                sp.sem_inc(s_cout[i], 16)
                sp.sem_inc(s_xout[i], 16)
            with nc.allow_non_contiguous_dma(reason="four vectors of 256 values"):
                for n, ap in enumerate((ctx_g, ctx_b, lat_g, lat_b)):
                    sp.dma_start(gb[:, n], ap.rearrange("(k p) -> p k", p=P)).then_inc(s_tabin, 16)
            for n, ap in enumerate((cos, sin)):
                sp.dma_start(trig[:, n], ap.rearrange("(p t) d -> p t d", p=P)).then_inc(s_tabin, 16)
            w3 = w_raw[:].rearrange("p k (t n) -> p k t n", t=3)
            for n, ap in enumerate((Wkv[:, 0:sh.INNER], Wq, Wkv[:, sh.INNER:2 * sh.INNER])):
                sp.dma_start(w3[:, :, n], ap.rearrange("(k p) n -> p k n", p=P)).then_inc(s_w[n], 16)
            for i in range(2):
                sp.dma_start(T[i]["ctx"][:], rows(ctx_in, i)).then_inc(s_cin[i], 16)
                sp.dma_start(T[i]["x"][:], rows(x, i)).then_inc(s_xin[i], 16)
            sp.dma_start(wo[:], Wo.rearrange("(c p) n -> p c n", p=P)).then_inc(s_wo, 16)
            sp.wait_ge(s_lo, 1)
            sp.dma_start(wpack.rearrange("c p n -> p c n"),
                         w_split[:].rearrange("p c a b k n -> p c (a b k n)").bitcast(F32)).then_inc(s_wout, 16)

            def two(h, more):
                if more:
                    for i in range(2):
                        sp.wait_ge(s_ctr, 8 * h + 4 * i + 4)
                        sp.dma_start(T[i]["ctx"][:], rows(ctx_in, h * 2 + (i + 2))).then_inc(s_cin[i], 16)
                    for i in range(2):
                        sp.wait_ge(s_xtr, 4 * h + 2 * i + 2)
                        sp.dma_start(T[i]["x"][:], rows(x, h * 2 + (i + 2))).then_inc(s_xin[i], 16)
                for i in range(2):
                    sp.wait_ge(s_clo[i], h + 2)
                    sp.dma_start(ctxT[h * 2 + i], ctx_split[i][:].rearrange("p a k n -> p (a k n)").bitcast(F32)).then_inc(s_cout[i], 16)
                for i in range(2):
                    sp.wait_ge(s_xlo, 2 * h + i + 2)
                    sp.dma_start(latT[h * 2 + i], lat_split[i][:].rearrange("p a k n -> p (a k n)").bitcast(F32)).then_inc(s_xout[i], 16)

            with sp.Fori(0, B // 2 - 1) as h:
                two(h, True)
            two(B // 2 - 1, False)
            sp.wait_ge(s_wout, 16)
            sp.wait_ge(s_wo, 16)
            for i in range(2):
                sp.wait_ge(s_cout[i], 16 * (B // 2 + 1))
                sp.wait_ge(s_xout[i], 16 * (B // 2 + 1))

        @block.gpsimd
        def _(pool):
            for i in range(2):
                pool.sem_inc(s_clo[i], 1)
            pool.memset(ident[:], 0.0).then_inc(s_cc, 1)
            pool.memset(neg_half[:], -0.5)
            pool.memset(ones[:], 1.0)
            pool.wait_ge(s_cc, 1)
            pool.affine_select(out=ident[:], in_=ident[:], compare_op=ALU.not_equal, fill=1.0, base=0,
                               pattern=[[-1, P]], channel_multiplier=1).then_inc(s_cc, 1)
            pool.wait_ge(s_cc, 2)
            pool.memset(keep["zero"][:], 0.0).then_inc(s_const, 1)
            with pool.Fori(0, B // 2) as h:
                for i in range(2):
                    t = T[i]
                    pool.wait_ge(s_cvar, 2 * h + i + 1)
                    pool.tensor_tensor(t["r"][:], t["ve"][:], neg_half[:], ALU.pow).then_inc(s_crstd, 1)
                    pool.wait_ge(s_xvar, 4 * h + i + 1)
                    pool.tensor_tensor(t["xr"][:], t["xve"][:], neg_half[:, 0:QT], ALU.pow).then_inc(s_xrstd, 1)
                for i in range(2):
                    t = T[i]
                    pool.wait_ge(s_xvar, 4 * h + i + 3)
                    pool.tensor_tensor(t["xr"][:], t["xve"][:], neg_half[:, 0:QT], ALU.pow).then_inc(s_xrstd, 1)
                for i in range(2):
                    pool.wait_ge(s_cfull, 8 * h + 4 * i + 5)
                    pool.tensor_tensor(ctx_split[i][:, 1], T[i]["full"][:], ctx_split[i][:, 0].bitcast(F32),
                                       ALU.subtract).then_inc(s_clo[i], 1)

        @block.vector
        def _(v):
            v.sem_inc(s_xlo, 1)
            v.wait_ge(s_tabin, 16 * 6)
            half = sh.HD // 2
            for n in range(2):
                for r in range(4):
                    sign = -1.0 if n == 1 and r % 2 == 0 else 1.0
                    last = v.tensor_scalar(trig4[:, n, :, r], trig[:, n], sign, None, ALU.mult)
            last.then_inc(s_trig4, 1)
            for t in range(3):
                for k in range(KD):
                    v.wait_ge(s_hi, t * KD + k + 1)
                    last = v.tensor_tensor(w_split[:, :, t, 1, k], w4[:, t, k],
                                           w_split[:, :, t, 0, k].bitcast(F32), ALU.subtract)
            last.then_inc(s_lo, 1)

            def stats(src, st, mv, ve, tiles, s_stat, s_var, at):
                for t in range(tiles):
                    last = v.bn_stats(st[:, t], src[:, t])
                last.then_inc(s_stat, 1)
                v.wait_ge(s_stat, 2 * at + 1)
                v.memset(ve[:], EPS)
                for t in range(tiles):
                    last = v.bn_aggr(mv[:, t], st[:, t])
                last.then_inc(s_stat, 1)
                v.wait_ge(s_stat, 2 * at + 2)
                v.tensor_tensor(ve[:], mv[:, :, 1], ve[:], ALU.add).then_inc(s_var, 1)

            def apply(dst, src, mv, r, tiles, s_norm):
                for t in range(tiles):
                    last = v.tensor_scalar(dst[:, t], src[:, t], mv[:, t, 0:1], r[:, t:t + 1], ALU.subtract, ALU.mult)
                last.then_inc(s_norm, 1)

            def low_x(h):
                for i in range(2):
                    v.wait_ge(s_xfull, 4 * h + 2 * i + 3)
                    v.tensor_tensor(lat_split[i][:, 1], T[i]["xfull"][:], lat_split[i][:, 0].bitcast(F32),
                                    ALU.subtract).then_inc(s_xlo, 1)

            def two(h):
                def stats_ctx(i):
                    v.wait_ge(s_cin[i], 16 * h + 16)
                    stats(T[i]["ctx"], T[i]["stats"], T[i]["mv"], T[i]["ve"], KT, s_cstat, s_cvar, 2 * h + i)

                def shift_ctx(i):
                    v.wait_ge(s_crstd, 2 * h + i + 1)
                    v.scalar_tensor_tensor(T[i]["shift"][:], T[i]["mv"][:, :, 0], -1.0, T[i]["r"][:], ALU.mult, ALU.mult).then_inc(s_cshift, 1)

                def stats_x(i):
                    v.wait_ge(s_xin[i], 16 * h + 16)
                    stats(T[i]["x"], T[i]["xstats"], T[i]["xmv"], T[i]["xve"], QT, s_xstat, s_xvar, 4 * h + i)

                def apply_x(i):
                    v.wait_ge(s_xrstd, 4 * h + i + 1)
                    apply(T[i]["xn"], T[i]["x"], T[i]["xmv"], T[i]["xr"], QT, s_xnorm)

                stats_ctx(0)
                stats_x(0)
                shift_ctx(0)
                stats_ctx(1)
                if not isinstance(h, int):
                    low_x(h - 1)
                apply_x(0)
                stats_x(1)
                shift_ctx(1)
                apply_x(1)
                for i in range(2):
                    t = T[i]
                    v.wait_ge(s_xnorm, 4 * h + i + 1)
                    stats(t["xn"], t["xstats"], t["xmv"], t["xve"], QT, s_xstat, s_xvar, 4 * h + i + 2)
                for i in range(2):
                    t = T[i]
                    v.wait_ge(s_xrstd, 4 * h + i + 3)
                    apply(t["x"], t["xn"], t["xmv"], t["xr"], QT, s_xnorm)

            two(0)
            with v.Fori(1, B // 2) as h:
                two(h)
            low_x(B // 2 - 1)

        @block.tensor
        def _(pe):
            pe.wait_ge(s_const, 1)
            pe.wait_ge(s_trig4, 1)
            for n in range(2):
                for k in range(KT):
                    last = pe.transpose(tp[2 * n + k // 4][:, k % 4], trig4[:, n, k].rearrange("p r d -> p (r d)"), ident[:])
            last.then_inc(s_tabT, 1)
            pe.wait_ge(s_tab, 1)
            with pe.Fori(0, B // 2) as h:
                for i in range(2):
                    pe.wait_ge(s_cnorm, 2 * h + i + 1)
                    pe.wait_ge(s_cfull, 8 * h + 4 * i + 1)
                    for k in range(KD):
                        for half in range(2):
                            for j in range(4):
                                last = pe.transpose(tp[2 * k + half][:, j], T[i]["ctx"][:, 4 * half + j, k * P:(k + 1) * P], ident[:])
                            last.then_inc(s_ctr, 1)
                for i in range(2):
                    pe.wait_ge(s_xnorm, 4 * h + i + 3)
                    pe.wait_ge(s_xfull, 4 * h + 2 * i + 1)
                    for k in range(KD):
                        for j in range(4):
                            last = pe.transpose(tp[4 + k][:, j], T[i]["x"][:, j, k * P:(k + 1) * P], ident[:])
                        last.then_inc(s_xtr, 1)

        @block.scalar
        def _(act):
            act.wait_ge(s_tabT, 1)
            for n, dst in enumerate((cosT, sinT)):
                for k in range(2):
                    last = act.activation(dst[:, 512 * k:512 * k + 512], tp[2 * n + k][:].rearrange("p a b -> p (a b)"), ACT.Copy)
            last.then_inc(s_tab, 1)
            act.sem_inc(s_cfull, 1)
            act.sem_inc(s_xfull, 1)
            for t in range(3):
                act.wait_ge(s_w[t], 16)
                for k in range(KD):
                    act.activation(w_split[:, :, t, 0, k], w4[:, t, k], ACT.Copy).then_inc(s_hi, 1)
            act.wait_ge(s_tabin, 16 * 6)

            def scale_shift(full, split, k, cols, src, n):
                how = dict(bias=gb[:, n + 1, k:k + 1], scale=gb[:, n, k:k + 1])
                act.activation(full[:, k, cols], src[:].rearrange("p a b -> p (a b)"), ACT.Identity, **how)
                return act.activation(split[:, 0, k, cols], src[:].rearrange("p a b -> p (a b)"), ACT.Identity, **how)

            with act.Fori(0, B // 2) as h:
                for i in range(2):
                    act.wait_ge(s_cshift, 2 * h + i + 1)
                    for j in range(KT):
                        last = act.activation(T[i]["ctx"][:, j], T[i]["ctx"][:, j], ACT.Identity,
                                              bias=T[i]["shift"][:, j:j + 1], scale=T[i]["r"][:, j:j + 1])
                    last.then_inc(s_cnorm, 1)
                for i in range(2):
                    act.wait_ge(s_clo[i], h + 1)
                    act.wait_ge(s_cout[i], 16 * h + 16)
                    for k in range(KD):
                        for half in range(2):
                            act.wait_ge(s_ctr, 8 * h + 4 * i + 2 * k + half + 1)
                            scale_shift(T[i]["full"], ctx_split[i], k, slice(512 * half, 512 * half + 512),
                                        tp[2 * k + half], 0).then_inc(s_cfull, 1)
                for i in range(2):
                    act.wait_ge(s_xlo, 2 * h + 1)
                    act.wait_ge(s_xout[i], 16 * h + 16)
                    for k in range(KD):
                        act.wait_ge(s_xtr, 4 * h + 2 * i + k + 1)
                        scale_shift(T[i]["xfull"], lat_split[i], k, slice(0, sh.N), tp[4 + k], 2).then_inc(s_xfull, 1)


def attend(nc, sh, x, bo, router_w, wpack, ctxT, latT, start, xn_d, xnT, xs, keep):
    KD, KT, QT, PAIRS, D, B, N, S, HD, E = sh.KD, sh.KT, sh.QT, sh.PAIRS, sh.D, sh.B, sh.N, sh.S, sh.HD, sh.E
    with ExitStack() as es:
        def sb(name, shape, dt=F32):
            return es.enter_context(nc.sbuf_tensor(name, shape, dt))

        def ps(name, shape, dt=F32):
            return es.enter_context(nc.psum_tensor(name, shape, dt))

        def sem(name):
            return es.enter_context(nc.semaphore(name))

        ident, cosT, sinT, wo, ones, logits = (keep[n] for n in ("ident", "cosT", "sinT", "wo", "ones", "logits"))
        STEPS = KT
        PROBS = 4
        DUOS = PAIRS // 2
        VBANKS = KT // 2

        USES = [(("k", 0), ("k", 1), ("v", 0), ("v", 1), ("q", 0))] * PAIRS
        USE_STEP = [(0, 1, 2, 3, 5)] * PAIRS
        NORM = 3
        USES[NORM] += (("t", 0), ("t", 1))
        USE_STEP[NORM] = (0, 1, 2, 3, 4, 5, 6)
        FIRST = 2 * 3 + VBANKS
        BATCH_USES = sum(len(u) for u in USES) + 2
        assert BATCH_USES % 2 == 0

        def uses_before(b, p):
            return b * BATCH_USES + (FIRST + sum(len(u) for u in USES[:p]))

        def bank(p, i):
            return (FIRST + sum(len(u) for u in USES[:p]) + i) % 2

        w = [sb(f"w{i}", [P, 2, 2, KD, P], F32R) for i in range(2)]
        wv = sb("wv", [P, DUOS, 2, KD, 2 * P], F32R)
        HS = S // 2
        ctxs = [sb(f"ctxs{i}", [P, 2, KD, HS], F32R) for i in range(2)]
        lats = sb("lats", [P, 2, KD, N], F32R)
        kT = sb("kT", [P, S])
        kT_swap = sb("kT_swap", [P, S])
        k_rope = sb("k_rope", [P, S])
        k_split = sb("k_split", [P, 2, S], F32R)
        k_st = [sb(f"k_st{i}", [P, 2, S], F32R) for i in range(2)]
        v_nat = [sb(f"v_nat{i}", [P, KT, 2 * P]) for i in range(2)]
        qT = sb("qT", [P, N])
        q_split = sb("q_split", [P, 2, N], F32R)
        q_st = [sb(f"q_st{i}", [P, 2, 2, N], F32R) for i in range(2)]
        probs = [sb(f"probs{i}", [P, 2, N]) for i in range(PROBS)]
        p_sum = sb("p_sum", [P, 2, N])
        u_sb = sb("u_sb", [P, N])
        rden = sb("rden", [P, N])
        o = sb("o", [P, PAIRS, N])
        x_in = sb("x_in", [P, QT, D])
        x_out = sb("x_out", [P, QT, D])
        xn = sb("xn", [P, QT, D])
        xn_T = sb("xn_T", [P, KD, N])
        xn_split = sb("xn_split", [P, 2, KD, N], F32R)
        n_stats, n_mv = sb("n_stats", [P, QT, 6]), sb("n_mv", [P, QT, 2])
        n_var, n_rstd, neg_half = sb("n_var", [P, QT]), sb("n_rstd", [P, QT]), sb("a_neg_half", [P, QT])
        rw = sb("rw", [P, KD, E])
        bo_bc = sb("bo_bc", [P, D])

        scores = [ps(f"scores{i}", [P, 2, N]) for i in range(2)]
        pv_ps = ps("pv_ps", [P, N])
        den_ps = ps("den_ps", [P, N])
        proj = [ps(f"proj{i}", [P, N]) for i in range(2)]

        s_w = [sem(f"s_w1{i}") for i in range(2)]
        s_wv = sem("s_wv")
        s_ctx, s_lat = [sem(f"s_ctx{i}") for i in range(2)], sem("s_lat")
        s_xin = sem("s_xin")
        s_bo = sem("s_bo")
        s_proj = sem("s_proj")
        s_projout = sem("s_projout")
        s_swap = sem("s_swap")
        s_cos, s_sin = sem("s_cos"), sem("s_sin")
        s_rope = sem("s_rope")
        s_khi, s_klo = sem("s_khi"), sem("s_klo")
        s_kst = sem("s_kst")
        s_qhi, s_qlo = sem("s_qhi"), sem("s_qlo")
        s_qst = sem("s_qst")
        s_scores = sem("s_scores")
        s_exp = sem("s_exp")
        s_clip = sem("s_clip")
        s_pv = sem("s_pv")
        s_add = sem("s_add")
        s_u = sem("s_u")
        s_den = sem("s_den")
        s_rden = sem("s_rden")
        s_o = sem("s_o")
        s_bias = sem("s_bias")
        s_x1 = sem("s_x1")
        s_zeroed = sem("s_zeroed")
        s_nstat, s_nvar, s_nrstd = sem("s_nstat"), sem("s_nvar"), sem("s_nrstd")
        s_xn = sem("s_xn")
        s_start = sem("s_start")
        s_xnlo = sem("s_xnlo")
        s_lg, s_lgout = sem("s_lg"), sem("s_lgout")
        s_rw = sem("s_rw")
        s_out = sem("s_out")
        s_xnout, s_xnTout = sem("s_xnout"), sem("s_xnTout")
        s_zero = sem("s_zero")

        block = es.enter_context(nc.Block())

        def batches(eng, slot, tail):
            with eng.Fori(0, B) as b:
                for p in range(PAIRS):
                    slot(b, p)
                tail(b)

        @block.sync
        def _(sp):
            def load_w(p, i):
                sp.dma_start(w[i][:].rearrange("p a b k n -> p (a b k n)").bitcast(F32),
                             wpack[p, :, 0:4 * KD * P]).then_inc(s_w[i], 16)

            def load_ctx(b, half):
                src = ctxT[b].rearrange("p (a k n) -> p a k n", a=2, k=KD)[:, :, :, HS * half:HS * half + HS]
                sp.dma_start(ctxs[half][:].bitcast(F32), src).then_inc(s_ctx[half], 16)

            def load_lat(b):
                sp.dma_start(lats[:].rearrange("p a k n -> p (a k n)").bitcast(F32), latT[b]).then_inc(s_lat, 16)

            def exchange():
                for q in range(4):
                    sp.dma_start(kT_swap[32 * q:32 * q + 32], kT[32 * (q ^ 1):32 * (q ^ 1) + 32]).then_inc(s_swap, 16)

            def stack_k(i):
                for head in range(2):
                    for part in range(2):
                        sp.dma_start(k_st[i][64 * part:64 * part + 64, head].bitcast(F32),
                                     k_split[64 * head:64 * head + 64, part].bitcast(F32)).then_inc(s_kst, 16)

            def stack_q(i):
                for head in range(2):
                    for twice in range(2):
                        sp.dma_start(q_st[i][64 * twice:64 * twice + 64, head].bitcast(F32),
                                     q_split[64 * head:64 * head + 64].bitcast(F32)).then_inc(s_qst, 16)

            load_w(0, 0)
            load_ctx(0, 0)
            load_ctx(0, 1)
            load_lat(0)
            load_w(1, 1)
            for p in range(PAIRS):
                half = slice(P * (p % 2), P * (p % 2) + P)
                sp.dma_start(wv[:, p // 2, :, :, half].bitcast(F32),
                             wpack[p, :, 4 * KD * P:].rearrange("p (a k n) -> p a k n", a=2, k=KD)).then_inc(s_wv, 16)
            with nc.allow_non_contiguous_dma(reason="one row to all partitions"):
                sp.dma_start(bo_bc[:], bo.rearrange("(a n) -> a n", a=1).broadcast_to((P, D))).then_inc(s_bo, 16)
                sp.dma_start(rw[:], router_w.rearrange("(k p) e -> p k e", p=P)).then_inc(s_rw, 16)
            sp.sem_inc(s_xnout, 16)
            sp.sem_inc(s_xnTout, 16)
            for i in range(2):
                sp.wait_ge(s_projout, 3 * i + 2)
                exchange()
                sp.wait_ge(s_proj, 3 * i + 3)
                load_w(2 + i, i)
                sp.wait_ge(s_qlo, i + 1)
                stack_q(i)
                sp.wait_ge(s_klo, i + 1)
                stack_k(i)

            def store_norm(to, n):
                sp.wait_ge(s_xn, n)
                sp.dma_start(xn_d[to].rearrange("(p t) d -> p t d", p=P), xn[:]).then_inc(s_xnout, 16)
                sp.wait_ge(s_start, n)
                sp.dma_start(start[to].rearrange("(p t) d -> p t d", p=P), x_out[:]).then_inc(s_out, 16)

            def store_parts(to, n):
                sp.wait_ge(s_xnlo, n)
                sp.dma_start(xnT[to], xn_split[:].rearrange("p a k n -> p (a k n)").bitcast(F32)).then_inc(s_xnTout, 16)

            def slot(b, p):
                sp.wait_ge(s_projout, uses_before(b, p) + 2)
                exchange()
                if p == PAIRS - 3:
                    load_ctx((b + 1) % B, 0)
                    sp.wait_ge(s_proj, uses_before(b, p) + 4)
                    load_ctx((b + 1) % B, 1)
                sp.wait_ge(s_proj, uses_before(b, p) + 5)
                load_w((p + 4) % PAIRS, p % 2)
                if p == PAIRS - 3:
                    load_lat((b + 1) % B)
                sp.wait_ge(s_klo, b * PAIRS + (p + 3))
                stack_k(p % 2)
                sp.wait_ge(s_qlo, b * PAIRS + (p + 3))
                stack_q(p % 2)
                if p == 0:
                    sp.dma_start(x_in[:], x[b].rearrange("(p t) d -> p t d", p=P)).then_inc(s_xin, 16)

                if p == NORM:
                    store_norm((b + (B - 1)) % B, b + 1)
                if p == NORM + 1:
                    store_parts((b + (B - 1)) % B, b + 1)

            batches(sp, slot, lambda b: None)
            store_norm(B - 1, B + 1)
            store_parts(B - 1, B + 1)
            sp.wait_ge(s_rw, 16)
            sp.wait_ge(s_out, 16 * (B + 1))
            sp.wait_ge(s_xnout, 16 * (B + 2))
            sp.wait_ge(s_xnTout, 16 * (B + 2))
            sp.wait_ge(s_lat, 16 * (B + 1))
            sp.wait_ge(s_kst, 64 * (B * PAIRS + 2))
            sp.wait_ge(s_qst, 64 * (B * PAIRS + 2))
            for i in range(2):
                sp.wait_ge(s_ctx[i], 16 * (B + 1))
                sp.wait_ge(s_w[i], 16 * (2 + B * PAIRS // 2))

        @block.gpsimd
        def _(pool):
            flat = xs.rearrange("r n d -> (r n d)").rearrange("(c p z) -> c p z", p=P, z=ZERO)
            PARTS = flat.shape[0] // B
            assert PARTS * B == flat.shape[0] and PARTS <= PAIRS
            pool.memset(neg_half[:], -0.5)
            pool.memset(x_out[:], 0.0).then_inc(s_zeroed, 1)
            pool.wait_ge(s_zeroed, 1)

            def rstd(n):
                pool.wait_ge(s_nvar, n)
                pool.tensor_tensor(n_rstd[:], n_var[:], neg_half[:], ALU.pow).then_inc(s_nrstd, 1)

            def low_norm(first):
                pool.wait_ge(s_projout, first + 2)
                pool.tensor_tensor(xn_split[:, 1], xn_T[:], xn_split[:, 0].bitcast(F32), ALU.subtract).then_inc(s_xnlo, 1)

            def times_sin():
                pool.tensor_tensor(kT_swap[:], kT_swap[:], sinT[:], ALU.mult).then_inc(s_sin, 1)

            for i in range(2):
                pool.wait_ge(s_swap, 64 * (i + 1))
                times_sin()

            def slot(b, p):
                pool.wait_ge(s_swap, b * (64 * PAIRS) + 64 * (p + 3))
                times_sin()
                if p < PARTS:
                    pool.dma_start(flat[b * PARTS + p], keep["zero"][:]).then_inc(s_zero, 16)
                if p == NORM - 2:
                    rstd(b + 1)
                if p == NORM:
                    low_norm(uses_before(b, p) + 5)

            batches(pool, slot, lambda b: None)
            rstd(B + 1)
            low_norm(uses_before(B, 0))
            pool.wait_ge(s_zero, 16 * flat.shape[0])

        @block.tensor
        def _(pe):
            pe.sem_inc(s_pv, PROBS)

            def products(out, stationary, moving):
                n = 0
                for k in range(KD):
                    for a, m in ((0, 0), (0, 1), (1, 0)):
                        last = pe.matmul(out, stationary(a, k), moving(m, k), start=n == 0, stop=n == 3 * KD - 1)
                        n += 1
                return last

            def project(i, to, which, rows):
                products(proj[to][:], lambda a, k: w[i][:, which, a, k],
                         lambda m, k: rows[:, m, k]).then_inc(s_proj, 1)

            def project_v(duo, vbank, to):
                for t in range(2):
                    tile = slice((2 * (vbank % 2) + t) * P, (2 * (vbank % 2) + t + 1) * P)
                    last = products(proj[to][:, 256 * t:256 * t + 256], lambda a, k: ctxs[vbank // 2][:, a, k, tile],
                                    lambda m, k: wv[:, duo, m, k])
                last.then_inc(s_proj, 1)

            def score(i, j):
                for head in range(2):
                    for part in range(2):
                        last = pe.matmul(scores[j % 2][:, head], k_st[i][:, head, j * P:(j + 1) * P],
                                         q_st[i][:, head, part], start=part == 0, stop=part == 1)
                last.then_inc(s_scores, 1)

            for half in range(2):
                pe.wait_ge(s_ctx[half], 16)
            pe.wait_ge(s_lat, 16)
            for i in range(2):
                pe.wait_ge(s_w[i], 16)
                for n in range(3):
                    if 3 * i + n >= 2:
                        pe.wait_ge(s_projout, 3 * i + n - 1)
                    project(i, (3 * i + n) % 2, n // 2, ctxs[n] if n < 2 else lats)
            pe.wait_ge(s_wv, 16 * PAIRS)
            for n in range(VBANKS):
                pe.wait_ge(s_projout, n + 5)
                project_v(0, n, n % 2)
            pe.wait_ge(s_kst, 64)
            pe.wait_ge(s_qst, 64)
            for j in range(2):
                score(0, j)
            pe.wait_ge(s_rw, 16)

            def transpose_norm(k, to, n):
                pe.wait_ge(s_xn, n)
                for t in range(QT):
                    last = pe.transpose(proj[to][:, t * P:(t + 1) * P], xn[:, t, k * P:(k + 1) * P], ident[:])
                last.then_inc(s_proj, 1)

            def route(ready, pairs_before):
                pe.wait_ge(s_projout, ready)
                pe.wait_ge(s_rden, pairs_before)
                for t in range(QT):
                    for k in range(KD):
                        last = pe.matmul(den_ps[:, t * E:(t + 1) * E], xn_T[:, k, t * P:(t + 1) * P], rw[:, k],
                                         start=k == 0, stop=k == KD - 1)
                last.then_inc(s_lg, 1)

            def slot(b, p):
                first = uses_before(b, p)
                def ahead(j):
                    pe.wait_ge(s_exp, b * (PAIRS * STEPS) + (p * STEPS + j + 1))
                    if j == STEPS - 2:
                        pe.wait_ge(s_kst, b * (64 * PAIRS) + 64 * (p + 2))
                        pe.wait_ge(s_qst, b * (64 * PAIRS) + 64 * (p + 2))
                    if j < STEPS - 2:
                        score(p % 2, j + 2)
                    else:
                        score((p + 1) % 2, j + 2 - STEPS)

                def projections(j):
                    if p == NORM + 1 and j == 4:
                        route(first, b * PAIRS + (p + 1))
                    if j not in USE_STEP[p]:
                        return
                    i = USE_STEP[p].index(j)
                    kind, n = USES[p][i]
                    if i == 0:
                        pe.wait_ge(s_w[p % 2], b * (16 * PAIRS // 2) + 16 * (p // 2 + 2))
                    if p == PAIRS - 2 and kind == "k":
                        pe.wait_ge(s_ctx[n], b * 16 + 32)
                    if p == PAIRS - 2 and kind == "q":
                        pe.wait_ge(s_lat, b * 16 + 32)
                    pe.wait_ge(s_projout, first + (i - 1))
                    if kind == "t":
                        transpose_norm(n, bank(p, i), b + 1)
                    elif kind == "v":
                        project_v((p // 2 + 1) % DUOS, 2 * (p % 2) + n, bank(p, i))
                    else:
                        project(p % 2, bank(p, i), 0 if kind == "k" else 1, ctxs[n] if kind == "k" else lats)

                def weigh(j):
                    pe.wait_ge(s_clip, b * (PAIRS * STEPS) + (p * STEPS + j + 1))
                    if j == 0:
                        pe.wait_ge(s_u, b * PAIRS + (p + 1))
                        pe.wait_ge(s_projout, first)
                    for head in range(2):
                        cols = P * (p % 2) + 64 * head
                        last = pe.matmul(pv_ps[64 * head:64 * head + 64], v_nat[p // 2 % 2][:, j, cols:cols + 64],
                                         probs[j % PROBS][:, head], start=j == 0, stop=j == STEPS - 1)
                    last.then_inc(s_pv, 1)

                for j in range(STEPS):
                    ahead(j)
                    projections(j)
                    weigh(j)
                pe.wait_ge(s_add, b * (PAIRS * STEPS) + (p * STEPS + STEPS + PROBS))
                pe.wait_ge(s_rden, b * PAIRS + (p + 1))
                if p == NORM + 1:
                    pe.wait_ge(s_lgout, b + 1)
                for head in range(2):
                    last = pe.matmul(den_ps[64 * head:64 * head + 64], ones[:], p_sum[:, head], start=True, stop=True)
                last.then_inc(s_den, 1)

            def tail(b):
                for i in range(2):
                    out = proj[bank(PAIRS, i)]
                    pe.wait_ge(s_projout, uses_before(b, PAIRS) + (i - 1))
                    for p in range(PAIRS):
                        if p == PAIRS - 1:
                            pe.wait_ge(s_o, b * PAIRS + (PAIRS + 1))
                        for t in range(2):
                            last = pe.matmul(out[:, 256 * t:256 * t + 256], o[:, p, (2 * i + t) * P:(2 * i + t + 1) * P],
                                             wo[:, p], start=p == 0 and t == 0, stop=p == PAIRS - 1, skip_group_check=True)
                    last.then_inc(s_proj, 1)

            batches(pe, slot, tail)
            for k in range(KD):
                pe.wait_ge(s_projout, uses_before(B, 0) + (k - 1))
                transpose_norm(k, bank(0, k), B + 1)
            route(uses_before(B, 0) + 2, B * PAIRS + 1)

        @block.scalar
        def _(act):
            act.sem_inc(s_u, 1)

            def exponentiate(j):
                act.activation(probs[j % PROBS][:], scores[j % 2][:], ACT.Exp, scale=float(HD) ** -0.5).then_inc(s_exp, 1)

            def copy_k(half, src):
                act.activation(kT[:, 512 * half:512 * half + 512], proj[src][:], ACT.Copy).then_inc(s_projout, 1)

            def copy_q(src):
                act.activation(q_split[:, 0], proj[src][:], ACT.Copy).then_inc(s_qhi, 1)
                act.activation(qT[:], proj[src][:], ACT.Copy).then_inc(s_projout, 1)

            def copy_v(i, vbank, src):
                act.activation(v_nat[i][:, 2 * vbank:2 * vbank + 2].rearrange("p t n -> p (t n)"),
                               proj[src][:], ACT.Copy).then_inc(s_projout, 1)

            for i in range(2):
                for n in range(3):
                    act.wait_ge(s_proj, 3 * i + n + 1)
                    if i == 1 and n == 0:
                        act.wait_ge(s_rope, 1)
                    if i == 1 and n == 2:
                        act.wait_ge(s_qst, 64)
                    if n < 2:
                        copy_k(n, (3 * i + n) % 2)
                    else:
                        copy_q((3 * i + n) % 2)
            for n in range(VBANKS):
                act.wait_ge(s_proj, n + 7)
                copy_v(0, n, n % 2)
            for j in range(2):
                act.wait_ge(s_scores, j + 1)
                exponentiate(j)

            def copy_norm(k, src):
                act.activation(xn_split[:, 0, k], proj[src][:], ACT.Copy)
                act.activation(xn_T[:, k], proj[src][:], ACT.Copy).then_inc(s_projout, 1)

            def copy_logits(to, n):
                act.wait_ge(s_lg, n)
                act.activation(logits[:, bass.ds(to * QT, QT)], den_ps[:, 0:QT * E].rearrange("p (t e) -> p t e", e=E),
                               ACT.Copy).then_inc(s_lgout, 1)

            def slot(b, p):
                first = uses_before(b, p)
                for j in range(STEPS):
                    g = p * STEPS + j + 2
                    act.wait_ge(s_scores, b * (PAIRS * STEPS) + (g + 1))
                    act.wait_ge(s_pv, b * (PAIRS * STEPS) + (g + 1))
                    act.wait_ge(s_add, b * (PAIRS * STEPS) + (g + 1))
                    exponentiate(g % STEPS)
                    if p == NORM + 1 and j == 4:
                        copy_logits((b + (B - 1)) % B, b + 1)
                    if j in USE_STEP[p]:
                        i = USE_STEP[p].index(j)
                        kind, n = USES[p][i]
                        act.wait_ge(s_proj, first + i + 1)
                        if kind == "k":
                            if n == 0:
                                act.wait_ge(s_rope, b * PAIRS + (p + 2))
                            copy_k(n, bank(p, i))
                        elif kind == "q":
                            act.wait_ge(s_qst, b * (64 * PAIRS) + 64 * (p + 2))
                            copy_q(bank(p, i))
                        elif kind == "t":
                            if n == 0:
                                act.wait_ge(s_xnTout, b * 16 + 16)
                            copy_norm(n, bank(p, i))
                        else:
                            if n == 0:
                                act.wait_ge(s_pv, b * (PAIRS * STEPS) + (p * STEPS + PROBS))
                            copy_v((p // 2 + 1) % 2, 2 * (p % 2) + n, bank(p, i))
                act.wait_ge(s_pv, b * (PAIRS * STEPS) + (p * STEPS + STEPS + PROBS))
                act.wait_ge(s_o, b * PAIRS + (p + 1))
                act.activation(u_sb[:], pv_ps[:], ACT.Copy).then_inc(s_u, 1)

            def tail(b):
                for i in range(2):
                    act.wait_ge(s_proj, uses_before(b, PAIRS) + (i + 1))
                    if i == 0:
                        act.wait_ge(s_out, b * 16 + 16)
                    act.activation(x_out[:, 2 * i:2 * i + 2].rearrange("p t d -> p (t d)"),
                                   proj[bank(PAIRS, i)][:], ACT.Copy).then_inc(s_projout, 1)

            batches(act, slot, tail)
            act.wait_ge(s_xnTout, 16 * (B + 1))
            for k in range(KD):
                act.wait_ge(s_proj, uses_before(B, 0) + k + 1)
                copy_norm(k, bank(0, k))
            copy_logits(B - 1, B + 1)

        @block.vector
        def _(v):
            v.sem_inc(s_add, PROBS)
            v.sem_inc(s_rden, 1)
            v.sem_inc(s_o, 1)

            def clip(j):
                pr = probs[j % PROBS][:]
                v.tensor_scalar(pr, pr, EXP_LO, EXP_HI, ALU.max, ALU.min).then_inc(s_clip, 1)

            def times_cos():
                v.tensor_tensor(k_rope[:], kT[:], cosT[:], ALU.mult).then_inc(s_cos, 1)

            def add_rope():
                v.tensor_tensor(k_rope[:], k_rope[:], kT_swap[:], ALU.add).then_inc(s_rope, 1)

            def high_k():
                v.tensor_copy(k_split[:, 0], k_rope[:]).then_inc(s_khi, 1)

            def low_k():
                v.tensor_tensor(k_split[:, 1], k_rope[:], k_split[:, 0].bitcast(F32), ALU.subtract).then_inc(s_klo, 1)

            def low_q():
                v.tensor_tensor(q_split[:, 1], qT[:], q_split[:, 0].bitcast(F32), ALU.subtract).then_inc(s_qlo, 1)

            for i in range(2):
                v.wait_ge(s_projout, 3 * i + 2)
                if i == 1:
                    v.wait_ge(s_klo, 1)
                times_cos()
                v.wait_ge(s_projout, 3 * i + 3)
                low_q()
                v.wait_ge(s_sin, i + 1)
                v.wait_ge(s_cos, i + 1)
                add_rope()
                v.wait_ge(s_rope, i + 1)
                if i == 1:
                    v.wait_ge(s_kst, 64)
                high_k()
                v.wait_ge(s_khi, i + 1)
                low_k()
            for j in range(2):
                v.wait_ge(s_exp, j + 1)
                clip(j)
            v.wait_ge(s_bo, 16)

            def norm_stats(m):
                for t in range(QT):
                    last = v.bn_stats(n_stats[:, t], x_out[:, t])
                last.then_inc(s_nstat, 1)
                v.wait_ge(s_nstat, 2 * m - 1)
                v.memset(n_var[:], EPS)
                for t in range(QT):
                    last = v.bn_aggr(n_mv[:, t], n_stats[:, t])
                last.then_inc(s_nstat, 1)
                v.wait_ge(s_nstat, 2 * m)
                v.tensor_tensor(n_var[:], n_mv[:, :, 1], n_var[:], ALU.add).then_inc(s_nvar, 1)

            def norm(m):
                v.wait_ge(s_nrstd, m)
                v.wait_ge(s_xnout, 16 * m)
                for t in range(QT):
                    last = v.tensor_scalar(xn[:, t], x_out[:, t], n_mv[:, t, 0:1], n_rstd[:, t:t + 1], ALU.subtract, ALU.mult)
                last.then_inc(s_xn, 1)

            def add_norm(m):
                v.wait_ge(s_xn, m)
                v.tensor_tensor(x_out[:], x_out[:], xn[:], ALU.add).then_inc(s_start, 1)

            v.wait_ge(s_zeroed, 1)

            def slot(b, p):
                first, n = uses_before(b, p), b * PAIRS
                def clip_ahead(j):
                    v.wait_ge(s_exp, b * (PAIRS * STEPS) + (p * STEPS + j + 3))
                    clip((j + 2) % STEPS)

                def add_up(j):
                    g = b * (PAIRS * STEPS) + (p * STEPS + j + 2)
                    v.wait_ge(s_clip, g)
                    if j == 0:
                        v.tensor_tensor(p_sum[:], probs[0][:], probs[1][:], ALU.add).then_inc(s_add, 2)
                    else:
                        v.wait_ge(s_add, g - 1 + PROBS)
                        v.tensor_tensor(p_sum[:], p_sum[:], probs[(j + 1) % PROBS][:], ALU.add).then_inc(s_add, 1)

                for j in range(STEPS):
                    if j < STEPS - 2:
                        clip_ahead(j)
                        add_up(j)
                    elif j == STEPS - 2:
                        add_up(j)
                        clip_ahead(j)
                    else:
                        clip_ahead(j)
                    if j == 2:
                        v.wait_ge(s_projout, first + 2)
                        times_cos()
                    elif j == 4:
                        v.wait_ge(s_sin, n + (p + 3))
                        v.wait_ge(s_cos, n + (p + 3))
                        add_rope()
                    elif j == 5:
                        v.wait_ge(s_rope, n + (p + 3))
                        v.wait_ge(s_kst, b * (64 * PAIRS) + 64 * (p + 2))
                        high_k()
                    elif j == 6:
                        v.wait_ge(s_khi, n + (p + 3))
                        low_k()
                        v.wait_ge(s_projout, first + 5)
                        low_q()
                    if p == NORM - 2 and j == 1:
                        norm_stats(b + 1)
                    if p == NORM - 1 and j == 1:
                        norm(b + 1)
                    if p == NORM - 1 and j == 3:
                        add_norm(b + 1)
                    if p == 1 and j == 5:
                        v.wait_ge(s_xin, b * 16 + 16)
                        v.tensor_tensor(x_in[:], x_in[:], bo_bc[:].unsqueeze(1).broadcast_to((P, QT, D)), ALU.add).then_inc(s_bias, 1)
                v.wait_ge(s_den, n + (p + 1))
                v.reciprocal(rden[:], den_ps[:]).then_inc(s_rden, 1)
                v.wait_ge(s_rden, n + (p + 2))
                v.wait_ge(s_u, n + (p + 2))
                if p == 0:
                    v.wait_ge(s_proj, uses_before(b, 0))
                v.tensor_tensor(o[:, p], u_sb[:], rden[:], ALU.mult).then_inc(s_o, 1)

            def tail(b):
                v.wait_ge(s_projout, uses_before(b, PAIRS) + 2)
                v.wait_ge(s_bias, b + 1)
                v.tensor_tensor(x_out[:], x_out[:], x_in[:], ALU.add).then_inc(s_x1, 1)

            batches(v, slot, tail)
            v.wait_ge(s_x1, B)
            norm_stats(B + 1)
            norm(B + 1)
            add_norm(B + 1)


def experts(nc, sh, start, xn_d, xnT, xs, ys, shared_up, shared_down, routed_up, routed_down, out, ffn):
    KD, QT, D, B, N, E, F = sh.KD, sh.QT, sh.D, sh.B, sh.N, sh.E, sh.F
    FT = F // P
    NT = B * QT
    TILES = sh.TILES
    LATE = 2
    HEAD = B - LATE
    with ExitStack() as es:
        def sb(name, shape, dt=F32):
            return es.enter_context(nc.sbuf_tensor(name, shape, dt))

        def sem(name):
            return es.enter_context(nc.semaphore(name))

        ident, acc, logits = ffn["ident"], ffn["acc"], ffn["logits"]
        raw = [[sb(f"raw{i}{n}", [P, KD * F]) for n in range(2)] for i in range(2)]
        up = [sb(f"up{i}", [P, 2, KD * F], F32R) for i in range(2)]
        down = [sb(f"down{i}", [P, 2, KD * F], F32R) for i in range(2)]
        xT = [sb(f"xT{i}", [P, 2, KD, N], F32R) for i in range(2)]
        rows = [sb(f"rows{i}", [P, QT, D]) for i in range(2)]
        hid = [sb(f"hid{i}", [P, N]) for i in range(2)]
        hid_split = [sb(f"hid_split{i}", [P, 2, N], F32R) for i in range(4)]
        y_sb = sb("y_sb", [P, QT, D])
        tri = sb("tri", [P, P])
        all_ones = sb("all_ones", [P, P])
        before = sb("before", [P, E, E])
        steps_n = sb("steps_n", [P, E, E])
        tile_no = sb("tile_no", [P, TILES, E - 1])
        probs = sb("r_probs", [P, NT, E])
        mx, tot, rtot = sb("r_mx", [P, NT]), sb("r_tot", [P, NT]), sb("r_rtot", [P, NT])
        rank = sb("r_rank", [P, NT, E])
        sel0, sel1, both = sb("r_sel0", [P, NT, E]), sb("r_sel1", [P, NT, E]), sb("r_both", [P, NT, E])
        gate = [sb(f"gate{i}", [P, NT]) for i in range(2)]
        counts_et = sb("r_counts", [P, E, NT])
        run = sb("r_run", [P, E, NT])
        n_tiles, ends, base, count = sb("r_nt", [P, E]), sb("r_ends", [P, E]), sb("r_base", [P, E]), sb("r_cnt", [P, E])
        ones_e = sb("r_ones", [P, E * NT])
        pos = sb("r_pos", [P, NT, E])
        idx = [sb(f"idx{i}", [P, NT], I32) for i in range(2)]
        tmp = sb("r_tmp", [P, NT, E])
        posf = sb("r_posf", [P, NT])
        tile_e = sb("tile_e", [P, TILES])
        tile_ei = sb("tile_ei", [P, TILES], I32)

        pair_big = raw[1][0][:].rearrange("p (t e f) -> p t e f", e=E, f=E)
        eq_big = raw[1][1][:].rearrange("p (t e f) -> p t e f", e=E, f=E)

        gat = [[sb(f"gat{i}{n}", [P, QT, D]) for n in range(2)] for i in range(2)]

        def ps(name, shape):
            return es.enter_context(nc.psum_tensor(name, shape, F32))

        hp = [ps(f"hp{i}", [P, N]) for i in range(4)]
        yp = ps("yp", [P, QT, D])
        tp = [ps(f"ftp{k}", [P, QT, P]) for k in range(KD)]
        rank_ps = [bank[:].rearrange("p a b -> p (a b)")[:, 0:NT * E] for bank in tp]

        s_cc, s_const = sem("f_cc"), sem("f_const")
        s_accin = sem("f_accin")
        s_r = sem("f_r")
        s_re = sem("f_re")
        s_rm = sem("f_rm")
        s_idx = sem("f_idx")
        stage = rows + gat[0] + gat[1]
        STAGES = len(stage)
        s_stage = [sem(f"f_stage{i}") for i in range(STAGES)]
        s_scat = [sem(f"f_scat{i}") for i in range(STAGES)]
        s_scatall = sem("f_scatall")
        s_raw = [sem(f"f_raw{i}") for i in range(2)]
        s_shT = [sem(f"f_shT{i}") for i in range(2)]
        s_rows = [sem(f"f_rows{i}") for i in range(2)]
        s_whi, s_wlo = sem("f_whi"), sem("f_wlo")
        s_tr = sem("f_tr")
        s_xhi, s_xlo = sem("f_xhi"), sem("f_xlo")
        s_up = sem("f_up")
        s_hhi, s_hlo = sem("f_hhi"), sem("f_hlo")
        s_dn = sem("f_dn")
        s_y = sem("f_y")
        s_yout = sem("f_yout")
        s_gat = [sem(f"f_gat{i}") for i in range(2)]
        s_half = sem("f_half")
        s_comb = sem("f_comb")
        s_out = sem("f_out")
        block = es.enter_context(nc.Block())

        @block.sync
        def _(sp):
            def load_raw(i, up_ap, down_ap):
                if up_ap is not None:
                    sp.dma_start(raw[i][0][:].rearrange("p (k f) -> p k f", k=KD), up_ap.rearrange("(k p) f -> p k f", p=P)).then_inc(s_raw[i], 16)
                if down_ap is not None:
                    sp.dma_start(raw[i][1][:].rearrange("p (c n) -> p c n", n=D), down_ap.rearrange("(c p) n -> p c n", p=P)).then_inc(s_raw[i], 16)

            def load_expert(r, i):
                if isinstance(r, int) and r >= TILES:
                    return load_raw(i, shared_up[0], shared_down[0])
                e = sp.value_load(tile_ei[0:1, bass.ds(r, 1)], min_val=0, max_val=E - 1)
                load_raw(i, routed_up[e], routed_down[e])

            def load_rows(r, i):
                src = xn_d[HEAD + r - TILES] if isinstance(r, int) and r >= TILES else xs[r]
                sp.dma_start(rows[i][:], src.rearrange("(p t) d -> p t d", p=P)).then_inc(s_rows[i], 16)

            def load_shared(b, i):
                sp.dma_start(xT[i][:].rearrange("p a k n -> p (a k n)").bitcast(F32), xnT[b]).then_inc(s_shT[i], 16)

            sp.sem_inc(s_yout, 16)
            load_raw(0, shared_up[0], None)
            load_shared(0, 0)
            sp.wait_ge(s_raw[0], 16)
            load_raw(0, None, shared_down[0])
            load_shared(1, 1)
            for b in range(B):
                sp.dma_start(acc[:, b * QT:(b + 1) * QT], start[b].rearrange("(p t) d -> p t d", p=P)).then_inc(s_accin, 16)

            sp.wait_ge(s_idx, 1)
            sp.wait_ge(s_wlo, FT)
            load_expert(0, 0)
            load_expert(1, 1)
            with sp.Fori(0, HEAD // 2 - 1) as h:
                for i in range(2):
                    b = h * 2 + i
                    sp.wait_ge(s_up, FT * b + FT)
                    load_shared(b + 2, i)
            sp.wait_ge(s_scatall, 1)
            load_rows(0, 0)
            load_rows(1, 1)

            def store(r):
                sp.wait_ge(s_y, HEAD + r + 1)
                sp.dma_start(ys[r].rearrange("(p t) d -> p t d", p=P), y_sb[:]).then_inc(s_yout, 16)

            with sp.Fori(0, TILES // 2 - 1) as k:
                for i in range(2):
                    r = k * 2 + i
                    sp.wait_ge(s_wlo, FT * (r + 2))
                    load_expert(r + 2, i)
                    sp.wait_ge(s_tr, r + 1)
                    load_rows(r + 2, i)
                    store(r)
            for r in range(TILES - 3, TILES):
                sp.wait_ge(s_wlo, FT * (r + 2))
                load_expert(r + 2, r % 2)
                sp.wait_ge(s_tr, r + 1)
                load_rows(r + 2, r % 2)
                store(r)
            sp.wait_ge(s_yout, 16 * (TILES + 1))
            with sp.Fori(0, B // 2) as h:
                for i in range(2):
                    b = h * 2 + i
                    sp.wait_ge(s_comb, b + 1)
                    sp.dma_start(out[b].rearrange("(p t) d -> p t d", p=P), acc[:, bass.ds(b * QT, QT)]).then_inc(s_out, 16)
            sp.wait_ge(s_out, 16 * B)

        @block.gpsimd
        def _(pool):
            pool.memset(tri[:], 1.0)
            pool.memset(all_ones[:], 1.0)
            pool.memset(before[:], 1.0)
            pool.iota(steps_n[:], pattern=[[0, E], [N, E]], base=0, channel_multiplier=0, allow_small_or_imprecise_dtypes=True)
            pool.iota(tile_no[:], pattern=[[1, TILES], [0, E - 1]], base=0, channel_multiplier=0,
                      allow_small_or_imprecise_dtypes=True).then_inc(s_cc, 1)
            pool.wait_ge(s_cc, 1)
            pool.affine_select(out=tri[:], in_=tri[:], compare_op=ALU.is_gt, fill=0.0, base=0,
                               pattern=[[1, P]], channel_multiplier=-1).then_inc(s_cc, 1)
            pool.affine_select(out=before[:], in_=before[:], compare_op=ALU.is_gt, fill=0.0, base=0,
                               pattern=[[1, E], [-1, E]], channel_multiplier=0).then_inc(s_cc, 1)
            pool.wait_ge(s_cc, 3)
            pool.memset(ones_e[:], 1.0).then_inc(s_const, 1)
            for f in range(FT + 2):
                pool.wait_ge(s_hhi, f + 1)
                pool.tensor_tensor(hid_split[f % 4][:, 1], hid[f % 2][:], hid_split[f % 4][:, 0].bitcast(F32),
                                   ALU.subtract).then_inc(s_hlo, 1)
            for b in range(STAGES):
                pool.dma_start(stage[b][:], xn_d[b].rearrange("(p t) d -> p t d", p=P)).then_inc(s_stage[b], 16)
            pool.wait_ge(s_idx, 1)
            for b in range(B):
                i = b % STAGES
                pool.wait_ge(s_stage[i], 16 * (b // STAGES + 1))
                for t in range(QT):
                    for n in range(2):
                        pool.indirect_dma_start(xs.rearrange("r n d -> (r n) d"),
                                                bass.IndirectOffsetOnAxis(ap=idx[n][:, b * QT + t:b * QT + t + 1], axis=0),
                                                stage[i][:, t], None).then_inc(s_scat[i], 16)
                if 1 <= b <= B - STAGES:
                    nxt = b - 1 + STAGES
                    pool.wait_ge(s_scat[b - 1], 16 * 2 * QT)
                    pool.dma_start(stage[b - 1][:], xn_d[nxt].rearrange("(p t) d -> p t d", p=P)).then_inc(s_stage[b - 1], 16)
            for i in range(STAGES):
                pool.wait_ge(s_scat[i], 16 * 2 * QT * (1 + (i < B - STAGES)))
            pool.sem_inc(s_scatall, 1)
            pool.wait_ge(s_yout, 16 * (TILES + 1))
            for b in range(B):
                i = b % 2
                if b >= 2:
                    pool.wait_ge(s_comb, b - 1)
                for t in range(QT):
                    for n in range(2):
                        pool.indirect_dma_start(gat[i][n][:, t], None, ys.rearrange("r n d -> (r n) d"),
                                                bass.IndirectOffsetOnAxis(ap=idx[n][:, b * QT + t:b * QT + t + 1], axis=0)
                                                ).then_inc(s_gat[i], 16)

        def tiles(eng, body):
            body(0, 0, None, "shared", None, 0)
            body(1, 1, None, "shared", None, 1)
            with eng.Fori(1, HEAD // 2 - 1) as h:
                body(h * 2, 0, None, "shared", None, h)
                body(h * 2 + 1, 1, None, "shared", None, h + 1)
            body(HEAD - 2, 0, None, "shared", None, HEAD // 2 - 1)
            body(HEAD - 1, 1, None, "routed", 0, 0)
            with eng.Fori(0, TILES // 2) as k:
                body(HEAD + k * 2, 0, k * 2, "routed", k * 2 + 1, k)
                body(HEAD + k * 2 + 1, 1, k * 2 + 1, "routed", k * 2 + 2, k + 1)
            for r in range(TILES - 1, TILES + 1):
                body(HEAD + r, r % 2, r, "routed", r + 1, r // 2 + r % 2)
            body(HEAD + TILES + 1, 0, TILES + 1, None, None, None)

        def batch_of(T, r):
            if r is None:
                return T
            return HEAD + r - TILES if isinstance(r, int) and r >= TILES else None

        @block.tensor
        def _(pe):
            def rank_rows():
                pe.wait_ge(s_const, 1)
                pe.wait_ge(s_r, R_BOTH)
                for bank, m in zip(rank_ps, (tri, all_ones)):
                    last = pe.matmul(bank, m[:], both[:].rearrange("p t e -> p (t e)"), start=True, stop=True)
                last.then_inc(s_rm, 1)

            def up_product(u, wu, f, read):
                if not isinstance(read, int) or read > 0:
                    pe.wait_ge(s_hhi, read)
                n = 0
                for k in range(KD):
                    for wp, xp in ((0, 0), (0, 1), (1, 0)):
                        last = pe.matmul(hp[f % 4][:], up[wu][:, wp, k * F + f * P:k * F + (f + 1) * P], xT[u][:, xp, k],
                                         start=n == 0, stop=n == 3 * KD - 1)
                        n += 1
                last.then_inc(s_up, 1)

            def down_product(T, wu, f, r):
                pe.wait_ge(s_hlo, FT * T + f + 1)
                if f == 0:
                    if not isinstance(T, int) or T > 0:
                        pe.wait_ge(s_y, T)
                    if r is not None:
                        pe.wait_ge(s_wlo, FT * (r + 2))
                    elif isinstance(T, int) and T == 0:
                        pe.wait_ge(s_wlo, FT)
                hs = hid_split[f % 4]
                for t in range(QT):
                    for n, (hpart, wp) in enumerate(((0, 0), (1, 0), (0, 1))):
                        last = pe.matmul(yp[:, t], hs[:, hpart, t * P:(t + 1) * P], down[wu][:, wp, f * D:(f + 1) * D],
                                         start=f == 0 and n == 0 and t % 2 == 0, stop=f == FT - 1 and n == 2, skip_group_check=True)
                last.then_inc(s_dn, 1)

            def transpose_rows(r, u, k):
                pe.wait_ge(s_rows[u], 16 * (k + 1))
                if not isinstance(r, int) or r > 0:
                    pe.wait_ge(s_xlo, r)
                for kd in range(KD):
                    for q in range(QT):
                        last = pe.transpose(tp[kd][:, q], rows[u][:, q, kd * P:(kd + 1) * P], ident[:])
                last.then_inc(s_tr, 1)

            pe.wait_ge(s_wlo, FT // 2)
            pe.wait_ge(s_shT[0], 16)
            for f in range(2):
                up_product(0, 0, f, 0)

            def body(T, u, r, nxt, n, k):
                wu = 0 if r is None else 1 - u
                for f in range(2, FT):
                    up_product(u, wu, f, FT * T + f - 3)
                    down_product(T, wu, f - 2, r)
                    if f == 6 and isinstance(T, int) and T == 0:
                        rank_rows()
                    if f == 3 and nxt == "routed":
                        transpose_rows(n, 1 - u, k)
                if nxt == "shared":
                    pe.wait_ge(s_shT[1 - u], 16 * k + 16)
                elif nxt == "routed":
                    pe.wait_ge(s_xlo, n + 1)
                    pe.wait_ge(s_wlo, FT * (n + 1) + FT // 2)
                for f in range(2):
                    if nxt is not None:
                        up_product(1 - u, 0 if nxt == "shared" else u, f, FT * (T + 1) + f - 3)
                    down_product(T, wu, FT - 2 + f, r)

            tiles(pe, body)

        @block.scalar
        def _(act):
            act.wait_ge(s_r, R_MAXED)
            act.activation(probs[:], probs[:], ACT.Exp).then_inc(s_re, 1)

            def weight_chunk(u, wu, f):
                n, q = f // 4, f % 4
                act.activation((up, down)[n][wu][:, 0, 512 * q:512 * q + 512], raw[u][n][:, 512 * q:512 * q + 512],
                               ACT.Copy).then_inc(s_whi, 1)

            def hidden(g, f):
                act.wait_ge(s_up, g + 1)
                act.activation(hid[f % 2][:], hp[f % 4][:], ACT.Gelu)
                act.activation(hid_split[f % 4][:, 0], hp[f % 4][:], ACT.Gelu).then_inc(s_hhi, 1)

            act.wait_ge(s_raw[0], 16)
            for f in range(FT // 2):
                weight_chunk(0, 0, f)
            hidden(0, 0)
            act.wait_ge(s_raw[0], 32)
            for f in range(FT // 2, FT):
                weight_chunk(0, 0, f)
            hidden(1, 1)

            def body(T, u, r, nxt, n, k):
                for f in range(2, FT + (0 if nxt is None else 2)):
                    act.wait_ge(s_hlo, FT * T + f - 1)
                    if not isinstance(T, int) or FT * T + f > 3:
                        act.wait_ge(s_dn, FT * T + f - 3)
                    hidden(FT * T + f, f % FT)
                    if nxt == "routed":
                        if f == 2:
                            act.wait_ge(s_dn, FT * T)
                            act.wait_ge(s_raw[1 - u], 32 * k + (64 if u == 1 else 32))
                        weight_chunk(1 - u, u, f - 2)
                if batch_of(T, r) is None:
                    act.wait_ge(s_dn, FT * T + FT)
                    act.wait_ge(s_yout, 16 * r + 16)
                    act.activation(y_sb[:], yp[:], ACT.Copy).then_inc(s_y, 1)

            tiles(act, body)

        @block.vector
        def _(v):
            step = [0]

            def then(ins):
                step[0] += 1
                ins.then_inc(s_r, 1)
                v.wait_ge(s_r, step[0])

            def weight_chunk(u, wu, f, at):
                n, q = f // 4, f % 4
                v.wait_ge(s_whi, at + f + 1)
                dst = (up, down)[n][wu]
                v.tensor_tensor(dst[:, 1, 512 * q:512 * q + 512], raw[u][n][:, 512 * q:512 * q + 512],
                                dst[:, 0, 512 * q:512 * q + 512].bitcast(F32), ALU.subtract).then_inc(s_wlo, 1)

            def hidden(g, f):
                v.wait_ge(s_hhi, g + 1)
                v.tensor_tensor(hid_split[f % 4][:, 1], hid[f % 2][:], hid_split[f % 4][:, 0].bitcast(F32),
                                ALU.subtract).then_inc(s_hlo, 1)

            def over_e(ap):
                return ap.unsqueeze(2).broadcast_to((P, NT, E))

            then(v.tensor_reduce(mx[:], logits[:], AX.X, ALU.max))
            then(v.tensor_tensor(probs[:], logits[:], over_e(mx[:]), ALU.subtract))
            assert step[0] == R_MAXED
            for f in range(FT):
                weight_chunk(0, 0, f, 0)
            v.wait_ge(s_re, 1)
            then(v.tensor_reduce(tot[:], probs[:], AX.X, ALU.add))
            then(v.reciprocal(rtot[:], tot[:]))
            then(v.tensor_tensor(probs[:], probs[:], over_e(rtot[:]), ALU.mult))
            v.wait_ge(s_const, 1)
            mine = probs[:].unsqueeze(3).broadcast_to((P, NT, E, E))
            other = probs[:].unsqueeze(2).broadcast_to((P, NT, E, E))
            v.tensor_tensor(pair_big, other, mine, ALU.is_gt)
            then(v.tensor_tensor(eq_big, other, mine, ALU.is_equal))
            then(v.tensor_tensor(eq_big, eq_big, before[:].unsqueeze(1).broadcast_to((P, NT, E, E)), ALU.mult))
            then(v.tensor_tensor(pair_big, pair_big, eq_big, ALU.add))
            then(v.tensor_reduce(rank[:], pair_big, AX.X, ALU.add))
            v.tensor_scalar(sel0[:], rank[:], 0.0, None, ALU.is_equal)
            v.tensor_scalar(sel1[:], rank[:], 1.0, None, ALU.is_equal)
            then(v.tensor_scalar(both[:], rank[:], 2.0, None, ALU.is_lt))
            assert step[0] == R_BOTH
            for n, s in enumerate((sel0, sel1)):
                then(v.tensor_tensor(tmp[:], s[:], probs[:], ALU.mult))
                then(v.tensor_reduce(gate[n][:], tmp[:], AX.X, ALU.add))
            v.wait_ge(s_rm, 1)
            counts = rank_ps[1].rearrange("p (t e) -> p e t", e=E)
            then(v.tensor_copy(counts_et[:], counts))
            flat = "p e t -> p (e t)"
            then(v.tensor_tensor_scan(run[:].rearrange(flat), ones_e[:], counts_et[:].rearrange(flat), 0.0, ALU.mult, ALU.add))
            v.tensor_copy(count[:, 0:1], run[:, 0, NT - 1:NT])
            then(v.tensor_tensor(count[:, 1:E], run[:, 1:E, NT - 1], run[:, 0:E - 1, NT - 1], ALU.subtract))
            cmp = tmp[:, 0:E]
            then(v.tensor_tensor(cmp, count[:].unsqueeze(2).broadcast_to((P, E, E)), steps_n[:], ALU.is_gt))
            then(v.tensor_reduce(n_tiles[:], cmp, AX.X, ALU.add))
            then(v.tensor_tensor_scan(ends[:], ones_e[:, 0:E], n_tiles[:], 0.0, ALU.mult, ALU.add))
            then(v.tensor_tensor(base[:], ends[:], n_tiles[:], ALU.subtract))
            then(v.tensor_scalar(base[:], base[:], float(N), None, ALU.mult))
            then(v.tensor_tensor(base[:, 1:E], base[:, 1:E], run[:, 0:E - 1, NT - 1], ALU.subtract))
            then(v.tensor_tensor(run[:], run[:], counts_et[:], ALU.subtract))
            then(v.tensor_tensor(run[:], run[:], base[:].unsqueeze(2).broadcast_to((P, E, NT)), ALU.add))
            then(v.tensor_tensor(pos[:], rank_ps[0].rearrange("p (t e) -> p t e", e=E),
                                 run[:].rearrange("p e t -> p t e"), ALU.add))
            assert step[0] == R_READ
            for n, s in enumerate((sel0, sel1)):
                then(v.tensor_tensor(tmp[:], s[:], pos[:], ALU.mult))
                then(v.tensor_reduce(posf[:], tmp[:], AX.X, ALU.add))
                then(v.tensor_copy(idx[n][:], posf[:]))
            te = rank[:].rearrange("p t e -> p (t e)")[:, 0:TILES * (E - 1)].rearrange("p (t e) -> p t e", e=E - 1)
            then(v.tensor_tensor(te, ends[:, 0:E - 1].unsqueeze(1).broadcast_to((P, TILES, E - 1)), tile_no[:], ALU.is_le))
            then(v.tensor_reduce(tile_e[:], te, AX.X, ALU.add))
            v.tensor_copy(tile_ei[:], tile_e[:]).then_inc(s_idx, 1)
            v.wait_ge(s_accin, 16 * B)

            def split_rows(r, u, T, i):
                bank = tp[i % 2][:].rearrange("p a b -> p (a b)")
                if i == 0:
                    v.wait_ge(s_tr, r + 1)
                    v.wait_ge(s_up, FT * T)
                if i < 2:
                    v.tensor_copy(xT[u][:, 0, i], bank).then_inc(s_xhi, 1)
                    return
                v.wait_ge(s_xhi, 2 * r + 2)
                last = v.tensor_tensor(xT[u][:, 1, i - 2], bank, xT[u][:, 0, i - 2].bitcast(F32), ALU.subtract)
                if i == 3:
                    last.then_inc(s_xlo, 1)

            def combine(b):
                i = b % 2
                v.wait_ge(s_gat[i], 16 * 2 * QT * (b // 2 + 1))
                for n in range(2):
                    for t in range(QT):
                        q = b * QT + t
                        last = v.scalar_tensor_tensor(acc[:, q], gat[i][n][:, t], gate[n][:, q:q + 1], acc[:, q], ALU.mult, ALU.add)
                    if n == 0:
                        last.then_inc(s_half, 1)
                        v.wait_ge(s_half, b + 1)
                last.then_inc(s_comb, 1)

            COMBINE = ((TILES, 7), (TILES + 1, 3), (TILES + 1, 6))

            def body(T, u, r, nxt, n, k):
                by_gpsimd = isinstance(T, int) and T == 0
                if by_gpsimd:
                    v.wait_ge(s_hlo, FT + 2)
                for f in () if by_gpsimd else range(2, FT + (0 if nxt is None else 2)):
                    hidden(FT * T + f, f % FT)
                    if nxt == "routed":
                        weight_chunk(1 - u, u, f - 2, FT * (n + 1))
                        for i in {4: (0, 1), 5: (2,), 6: (3,)}.get(f, ()):
                            split_rows(n, 1 - u, T, i)
                    if isinstance(r, int) and (r, f) in COMBINE:
                        combine(COMBINE.index((r, f)))
                b = batch_of(T, r)
                if b is not None:
                    v.wait_ge(s_dn, FT * T + FT)
                    part = acc[:, bass.ds(b * QT, QT)]
                    v.tensor_tensor(part, yp[:], part, ALU.add).then_inc(s_y, 1)

            tiles(v, body)
            v.wait_ge(s_y, B + TILES)
            for b in range(len(COMBINE), B):
                combine(b)


R_MAXED = 2
R_BOTH = 10
R_READ = 26


def build(nc, x, ctx_1024, cos, sin, lat_g, lat_b, ctx_g, ctx_b, Wq, Wkv, Wo, bo,
          shared_up, shared_down, routed_up, routed_down, router_w, out):
    sh = Shapes(x, ctx_1024, cos, Wq, routed_up)
    KD, PAIRS, B, N, D = sh.KD, sh.PAIRS, sh.B, sh.N, sh.D

    def dram(name, shape):
        return nc.dram_tensor(name, shape, F32, kind="Internal").ap()

    wpack = dram("wpack", (PAIRS, P, 3 * 2 * KD * P))
    ctxT = dram("ctx_parts", (B, P, 2 * KD * sh.S))
    latT = dram("lat_parts", (B, P, 2 * KD * N))
    start = dram("result_start", (B, N, D))
    xn_d = dram("normed", (B, N, D))
    xnT = dram("normedT", (B, P, 2 * KD * N))
    xs = dram("sorted_rows", (sh.TILES, N, D))
    ys = dram("sorted_results", (sh.TILES, N, D))
    with ExitStack() as es:
        def sb(name, shape, dt=F32):
            return es.enter_context(nc.sbuf_tensor(name, shape, dt))

        ident = sb("ident", [P, P])
        logits = sb("logits", [P, B * sh.QT, sh.E])
        with ExitStack() as es1:
            def sb1(name, shape, dt=F32):
                return es1.enter_context(nc.sbuf_tensor(name, shape, dt))

            keep = dict(ident=ident, logits=logits, cosT=sb1("cosT", [P, sh.S]), sinT=sb1("sinT", [P, sh.S]),
                        wo=sb1("wo", [P, PAIRS, D]), ones=sb1("ones", [P, sh.HD]), zero=sb1("zero", [P, ZERO]))
            prepare(nc, sh, x, ctx_1024, cos, sin, lat_g, lat_b, ctx_g, ctx_b, Wq, Wkv, Wo, wpack, ctxT, latT, keep)
            attend(nc, sh, x, bo, router_w, wpack, ctxT, latT, start, xn_d, xnT, xs, keep)
        ffn = dict(ident=ident, acc=sb("acc", [P, B * sh.QT, D]), logits=logits)
        experts(nc, sh, start, xn_d, xnT, xs, ys, shared_up, shared_down, routed_up, routed_down, out, ffn)


_INS = ["x", "ctx_1024", "L0_xattn_cos", "L0_xattn_sin", "L0_xattn_ln_lat_g", "L0_xattn_ln_lat_b",
        "L0_xattn_ln_ctx_g", "L0_xattn_ln_ctx_b", "L0_xattn_Wq", "L0_xattn_Wkv", "L0_xattn_Wo", "L0_xattn_bo",
        "L0_ffn_shared_up", "L0_ffn_shared_down", "L0_ffn_routed_up", "L0_ffn_routed_down", "L0_ffn_router_w"]


def kernel(**inputs):
    import numpy as np
    import concourse.bacc as bacc
    from concourse.bass_utils import run_bass_kernel_spmd

    nc = bacc.Bacc("TRN2", target_bir_lowering=False, num_devices=1)
    arrays, args = {}, []
    for name in _INS:
        a = np.ascontiguousarray(inputs[name])
        arrays[name] = a
        args.append(nc.dram_tensor(name, a.shape, mybir.dt.from_np(a.dtype), kind="ExternalInput").ap())
    out = nc.dram_tensor("out", inputs["x"].shape, F32, kind="ExternalOutput").ap()
    build(nc, *args, out)
    return run_bass_kernel_spmd(nc, [arrays], core_ids=[0]).results[0]["out"]
```
